# Optimizing a Trainium2 kernel written in Bass

```python
import numpy as np
import jax
import jax.numpy as jnp

def _softmax(x, axis=-1):
    return jax.nn.softmax(x, axis=axis)

def _gelu(x):
    return jax.nn.gelu(x, approximate=True)

def _silu(x):
    return jax.nn.silu(x)

def _sigmoid(x):
    return jax.nn.sigmoid(x)

def _layernorm(x, axis=-1, eps=1e-05):
    m = jnp.mean(x, axis=axis, keepdims=True)
    v = jnp.var(x, axis=axis, keepdims=True)
    return (x - m) / jnp.sqrt(v + eps)

def _scatter_add(tgt, idx, src, axis=0):
    return tgt.at[idx].add(src)

def _segment_sum(src, seg, n):
    return jax.ops.segment_sum(src, seg, n)
kernel_name = 'mk_conv_attn_hybrid_d4_conv_nhwc768_r4_4a4d87'

def setup_inputs(seed: int=0):
    np.random.seed(seed)
    _w = jnp.asarray

    def _rec_inputs():
        import jax
        import jax.numpy as jnp
        _gk = jax.random.key(seed)
        x = -0.0004039 + 1 * jax.random.normal(jax.random.fold_in(_gk, 1), (4, 16, 16, 192), jnp.float32)
        return x
    x = _rec_inputs()

    def _L0_conv_setup():
        import jax, jax.numpy as jnp
        import numpy as np
        DIM = 192
        NH = 12
        HD = DIM // NH
        WS = 14
        EPS = 1e-05

        def _ln(x, w, b):
            m = jnp.mean(x, -1, keepdims=True)
            v = jnp.var(x, -1, keepdims=True)
            return (x - m) * jax.lax.rsqrt(v + EPS) * w + b

        def _block(x, ln1_w, ln1_b, qkv_w, qkv_b, proj_w, proj_b, rel_pos_h, rel_pos_w, ln2_w, ln2_b, fc1_w, fc1_b, fc2_w, fc2_b):
            B, H, W, C = x.shape
            shortcut = x
            xn = _ln(x, ln1_w, ln1_b)
            pad_h = -H % WS
            pad_w = -W % WS
            xp = jnp.pad(xn, ((0, 0), (0, pad_h), (0, pad_w), (0, 0)))
            Hp, Wp = (H + pad_h, W + pad_w)
            nh, nw = (Hp // WS, Wp // WS)
            xw = xp.reshape(B, nh, WS, nw, WS, C).transpose(0, 1, 3, 2, 4, 5)
            xw = xw.reshape(B * nh * nw, WS, WS, C)
            Bw = B * nh * nw
            N = WS * WS
            qkv = xw.reshape(Bw, N, C) @ qkv_w + qkv_b
            qkv = qkv.reshape(Bw, N, 3, NH, HD).transpose(2, 0, 3, 1, 4)
            q, k, v = (qkv[0], qkv[1], qkv[2])
            scale = HD ** (-0.5)
            attn = jnp.einsum('bhnd,bhmd->bhnm', q * scale, k)
            idx = jnp.arange(WS)[:, None] - jnp.arange(WS)[None, :] + (WS - 1)
            Rh = rel_pos_h[idx]
            Rw = rel_pos_w[idx]
            rq = q.reshape(Bw, NH, WS, WS, HD)
            rel_h = jnp.einsum('bnhwc,hkc->bnhwk', rq, Rh)
            rel_w = jnp.einsum('bnhwc,wkc->bnhwk', rq, Rw)
            attn = (attn.reshape(Bw, NH, WS, WS, WS, WS) + rel_h[..., :, None] + rel_w[..., None, :]).reshape(Bw, NH, N, N)
            attn = jax.nn.softmax(attn, axis=-1)
            out = jnp.einsum('bhnm,bhmd->bhnd', attn, v)
            out = out.transpose(0, 2, 1, 3).reshape(Bw, WS, WS, C)
            out = out @ proj_w + proj_b
            out = out.reshape(B, nh, nw, WS, WS, C).transpose(0, 1, 3, 2, 4, 5)
            out = out.reshape(B, Hp, Wp, C)[:, :H, :W, :]
            x = shortcut + out
            h = _ln(x, ln2_w, ln2_b)
            h = jax.nn.gelu(h @ fc1_w + fc1_b, approximate=False)
            x = x + (h @ fc2_w + fc2_b)
            return x
        key = jax.random.key(seed)
        ks = jax.random.split(key, 8)

        def n(k, shape, s=0.02):
            return jax.random.normal(k, shape, jnp.float32) * s
        return {'x': jax.random.normal(ks[0], (4, 16, 16, DIM), jnp.float32), 'ln1_w': jnp.ones((DIM,), jnp.float32), 'ln1_b': jnp.zeros((DIM,), jnp.float32), 'qkv_w': n(ks[1], (DIM, 3 * DIM)), 'qkv_b': jnp.zeros((3 * DIM,), jnp.float32), 'proj_w': n(ks[2], (DIM, DIM)), 'proj_b': jnp.zeros((DIM,), jnp.float32), 'rel_pos_h': n(ks[3], (2 * WS - 1, HD)), 'rel_pos_w': n(ks[4], (2 * WS - 1, HD)), 'ln2_w': jnp.ones((DIM,), jnp.float32), 'ln2_b': jnp.zeros((DIM,), jnp.float32), 'fc1_w': n(ks[5], (DIM, 4 * DIM)), 'fc1_b': jnp.zeros((4 * DIM,), jnp.float32), 'fc2_w': n(ks[6], (4 * DIM, DIM)), 'fc2_b': jnp.zeros((DIM,), jnp.float32)}
    _L0_conv_all = _L0_conv_setup()
    _L0_conv_in = {k: v for k, v in _L0_conv_all.items() if k in ('ln1_w', 'ln1_b', 'qkv_w', 'qkv_b', 'proj_w', 'proj_b', 'rel_pos_h', 'rel_pos_w', 'ln2_w', 'ln2_b', 'fc1_w', 'fc1_b', 'fc2_w', 'fc2_b')}
    del _L0_conv_all

    def _L1_conv_setup():
        import jax, jax.numpy as jnp
        import numpy as np
        NUM_HEADS = 12

        def get_rel_pos(q_size, k_size, rel_pos):
            max_rel_dist = int(2 * max(q_size, k_size) - 1)
            if rel_pos.shape[0] != max_rel_dist:
                rel_pos = jax.image.resize(rel_pos, (max_rel_dist, rel_pos.shape[1]), method='linear')
            q_coords = jnp.arange(q_size)[:, None] * max(k_size / q_size, 1.0)
            k_coords = jnp.arange(k_size)[None, :] * max(q_size / k_size, 1.0)
            rel = (q_coords - k_coords + (k_size - 1) * max(q_size / k_size, 1.0)).astype(jnp.int32)
            return rel_pos[rel.reshape(-1)].reshape(q_size, k_size, -1)
        key = jax.random.key(seed)
        ks = jax.random.split(key, 7)
        B, H, W, C = (8, 32, 32, 192)
        head_dim = C // NUM_HEADS
        return {'x': jax.random.normal(ks[0], (B, H, W, C), jnp.float32), 'w_qkv': jax.random.normal(ks[1], (C, 3 * C), jnp.float32) * 0.02, 'b_qkv': jnp.zeros((3 * C,), jnp.float32), 'rel_pos_h': jax.random.normal(ks[2], (2 * H - 1, head_dim), jnp.float32) * 0.02, 'rel_pos_w': jax.random.normal(ks[3], (2 * W - 1, head_dim), jnp.float32) * 0.02, 'w_proj': jax.random.normal(ks[4], (C, C), jnp.float32) * 0.02, 'b_proj': jnp.zeros((C,), jnp.float32)}
    _L1_conv_all = _L1_conv_setup()
    _L1_conv_in = {k: v for k, v in _L1_conv_all.items() if k in ('w_qkv', 'b_qkv', 'rel_pos_h', 'rel_pos_w', 'w_proj', 'b_proj')}
    del _L1_conv_all

    def _L2_attn_setup():
        import jax, jax.numpy as jnp
        import numpy as np
        B, T, D, NH = (4, 512, 192, 12)
        DH = D // NH
        NEG = -100000.0
        key = jax.random.key(seed)
        ks = jax.random.split(key, 9)
        s = 1.0 / np.sqrt(D)
        return {'x': jax.random.normal(ks[0], (B, T, D), jnp.float32), 'wq': jax.random.normal(ks[1], (D, D), jnp.float32) * s, 'bq': jax.random.normal(ks[2], (D,), jnp.float32) * 0.02, 'wk': jax.random.normal(ks[3], (D, D), jnp.float32) * s, 'bk': jax.random.normal(ks[4], (D,), jnp.float32) * 0.02, 'wv': jax.random.normal(ks[5], (D, D), jnp.float32) * s, 'bv': jax.random.normal(ks[6], (D,), jnp.float32) * 0.02, 'wo': jax.random.normal(ks[7], (D, D), jnp.float32) * s, 'bo': jax.random.normal(ks[8], (D,), jnp.float32) * 0.02}
    _L2_attn_all = _L2_attn_setup()
    _L2_attn_in = {k: v for k, v in _L2_attn_all.items() if k in ('wq', 'bq', 'wk', 'bk', 'wv', 'bv', 'wo', 'bo')}
    del _L2_attn_all

    def _L2_ffn_setup():
        import jax, jax.numpy as jnp
        import numpy as np
        HID = 192
        NQ = 12
        NKV = 3
        HD = 16
        REP = NQ // NKV
        E = 16
        TOPK = 2
        FF = 384
        EPS = 1e-06
        THETA = 10000.0

        def rms_norm(x, w):
            return x / jnp.sqrt(jnp.mean(x * x, axis=-1, keepdims=True) + EPS) * w

        def rope_tables(seq_len):
            inv = 1.0 / THETA ** (jnp.arange(0, HD, 2, dtype=jnp.float32) / HD)
            f = jnp.arange(seq_len, dtype=jnp.float32)[:, None] * inv[None, :]
            return (jnp.cos(f), jnp.sin(f))

        def apply_rope(t, cos, sin):
            B, S, H, _ = t.shape
            tr = t.reshape(B, S, H, HD // 2, 2)
            c = cos[None, :, None, :]
            s = sin[None, :, None, :]
            r0 = tr[..., 0] * c - tr[..., 1] * s
            r1 = tr[..., 0] * s + tr[..., 1] * c
            return jnp.stack([r0, r1], axis=-1).reshape(B, S, H, HD)

        def attention(x, w_qkv, w_out):
            B, S, _ = x.shape
            qkv = x @ w_qkv
            q, k, v = jnp.split(qkv, [NQ * HD, (NQ + NKV) * HD], axis=-1)
            q = q.reshape(B, S, NQ, HD)
            k = k.reshape(B, S, NKV, HD)
            v = v.reshape(B, S, NKV, HD)
            cos, sin = rope_tables(S)
            q = apply_rope(q, cos, sin)
            k = apply_rope(k, cos, sin)
            k = jnp.repeat(k, REP, axis=2)
            v = jnp.repeat(v, REP, axis=2)
            q = q.transpose(0, 2, 1, 3)
            k = k.transpose(0, 2, 1, 3)
            v = v.transpose(0, 2, 1, 3)
            scores = jnp.einsum('bhqd,bhkd->bhqk', q, k) / jnp.sqrt(jnp.float32(HD))
            causal = jnp.tril(jnp.ones((S, S), dtype=bool))
            scores = jnp.where(causal[None, None], scores, jnp.finfo(scores.dtype).min)
            attn = jax.nn.softmax(scores, axis=-1)
            out = jnp.einsum('bhqk,bhkd->bhqd', attn, v)
            out = out.transpose(0, 2, 1, 3).reshape(B, S, NQ * HD)
            return out @ w_out

        def moe_ffn(x2d, w_router, w_gate_up, w_down):
            logits = x2d @ w_router
            probs = jax.nn.softmax(logits, axis=-1)
            vals, idx = jax.lax.top_k(probs, TOPK)
            vals = vals / jnp.sum(vals, axis=-1, keepdims=True)
            combine = jnp.sum(jax.nn.one_hot(idx, E, dtype=x2d.dtype) * vals[..., None], axis=1)
            out = jnp.zeros_like(x2d)
            for e in range(E):
                gu = x2d @ w_gate_up[e]
                gate, up = jnp.split(gu, 2, axis=-1)
                h = jax.nn.silu(gate) * up
                out = out + combine[:, e:e + 1] * (h @ w_down[e])
            return out
        key = jax.random.key(seed)
        ks = jax.random.split(key, 6)
        B, S = (1, 512)
        return {'x': jax.random.normal(ks[0], (B, S, HID), dtype=jnp.float32), 'norm1_w': jnp.ones((HID,), dtype=jnp.float32), 'w_qkv': jax.random.normal(ks[1], (HID, (NQ + 2 * NKV) * HD), dtype=jnp.float32) * 0.02, 'w_out': jax.random.normal(ks[2], (NQ * HD, HID), dtype=jnp.float32) * 0.02, 'norm2_w': jnp.ones((HID,), dtype=jnp.float32), 'w_router': jax.random.normal(ks[3], (HID, E), dtype=jnp.float32) * 0.02, 'w_gate_up': jax.random.normal(ks[4], (E, HID, 2 * FF), dtype=jnp.float32) * 0.02, 'w_down': jax.random.normal(ks[5], (E, FF, HID), dtype=jnp.float32) * 0.02}
    _L2_ffn_all = _L2_ffn_setup()
    _L2_ffn_in = {k: v for k, v in _L2_ffn_all.items() if k in ('norm1_w', 'w_qkv', 'w_out', 'norm2_w', 'w_router', 'w_gate_up', 'w_down')}
    del _L2_ffn_all

    def _L3_attn_setup():
        import jax, jax.numpy as jnp
        import numpy as np
        NUM_HEADS = 12
        THETA = 10000.0
        EPS = 1e-05

        def _rmsnorm(x, w):
            xf = x.astype(jnp.float32)
            var = jnp.mean(xf * xf, axis=-1, keepdims=True)
            return (xf * jax.lax.rsqrt(var + EPS) * w).astype(x.dtype)

        def _rope(x, cos, sin):
            c = cos[None, :, None, :]
            s = sin[None, :, None, :]
            xe = x[..., 0::2]
            xo = x[..., 1::2]
            oe = xe * c - xo * s
            oo = xe * s + xo * c
            return jnp.stack([oe, oo], axis=-1).reshape(x.shape)
        key = jax.random.key(seed)
        ks = jax.random.split(key, 10)
        B, S, D, F = (2, 512, 192, 768)
        sd = 0.02
        return {'x': jax.random.normal(ks[0], (B, S, D), jnp.float32), 'w_q': jax.random.normal(ks[1], (D, D), jnp.float32) * sd, 'w_k': jax.random.normal(ks[2], (D, D), jnp.float32) * sd, 'w_v': jax.random.normal(ks[3], (D, D), jnp.float32) * sd, 'w_o': jax.random.normal(ks[4], (D, D), jnp.float32) * sd, 'w_ln1': jnp.ones((D,), jnp.float32), 'w_ln2': jnp.ones((D,), jnp.float32), 'w_ffn_w1': jax.random.normal(ks[5], (F, D), jnp.float32) * sd, 'w_ffn_w2': jax.random.normal(ks[6], (D, F), jnp.float32) * sd, 'w_ffn_w3': jax.random.normal(ks[7], (F, D), jnp.float32) * sd}
    _L3_attn_all = _L3_attn_setup()
    _L3_attn_in = {k: v for k, v in _L3_attn_all.items() if k in ('w_q', 'w_k', 'w_v', 'w_o', 'w_ln1', 'w_ln2', 'w_ffn_w1', 'w_ffn_w2', 'w_ffn_w3')}
    del _L3_attn_all

    def _L3_ffn_setup():
        import jax, jax.numpy as jnp
        import numpy as np
        K_ACTIVE = 2
        key = jax.random.key(seed)
        ks = jax.random.split(key, 9)
        B, S, D, F, E, NS = (2, 512, 192, 384, 8, 1)
        sd = 1.0 / np.sqrt(D)
        sf = 1.0 / np.sqrt(F)
        return {'x': jax.random.normal(ks[0], (B, S, D), jnp.float32), 'Wg_s': jax.random.normal(ks[1], (NS, D, F), jnp.float32) * sd, 'Wu_s': jax.random.normal(ks[2], (NS, D, F), jnp.float32) * sd, 'Wd_s': jax.random.normal(ks[3], (NS, F, D), jnp.float32) * sf, 'Wg_r': jax.random.normal(ks[4], (E, D, F), jnp.float32) * sd, 'Wu_r': jax.random.normal(ks[5], (E, D, F), jnp.float32) * sd, 'Wd_r': jax.random.normal(ks[6], (E, F, D), jnp.float32) * sf, 'W_router': jax.random.normal(ks[7], (D, E), jnp.float32) * sd, 'expert_bias': jnp.zeros((E,), jnp.float32)}
    _L3_ffn_all = _L3_ffn_setup()
    _L3_ffn_in = {k: v for k, v in _L3_ffn_all.items() if k in ('Wg_s', 'Wu_s', 'Wd_s', 'Wg_r', 'Wu_r', 'Wd_r', 'W_router', 'expert_bias')}
    del _L3_ffn_all
    return {'x': x, 'L0_conv_ln1_w': _L0_conv_in['ln1_w'], 'L0_conv_ln1_b': _L0_conv_in['ln1_b'], 'L0_conv_qkv_w': _L0_conv_in['qkv_w'], 'L0_conv_qkv_b': _L0_conv_in['qkv_b'], 'L0_conv_proj_w': _L0_conv_in['proj_w'], 'L0_conv_proj_b': _L0_conv_in['proj_b'], 'L0_conv_rel_pos_h': _L0_conv_in['rel_pos_h'], 'L0_conv_rel_pos_w': _L0_conv_in['rel_pos_w'], 'L0_conv_ln2_w': _L0_conv_in['ln2_w'], 'L0_conv_ln2_b': _L0_conv_in['ln2_b'], 'L0_conv_fc1_w': _L0_conv_in['fc1_w'], 'L0_conv_fc1_b': _L0_conv_in['fc1_b'], 'L0_conv_fc2_w': _L0_conv_in['fc2_w'], 'L0_conv_fc2_b': _L0_conv_in['fc2_b'], 'L1_conv_w_qkv': _L1_conv_in['w_qkv'], 'L1_conv_b_qkv': _L1_conv_in['b_qkv'], 'L1_conv_rel_pos_h': _L1_conv_in['rel_pos_h'], 'L1_conv_rel_pos_w': _L1_conv_in['rel_pos_w'], 'L1_conv_w_proj': _L1_conv_in['w_proj'], 'L1_conv_b_proj': _L1_conv_in['b_proj'], 'L2_attn_wq': _L2_attn_in['wq'], 'L2_attn_bq': _L2_attn_in['bq'], 'L2_attn_wk': _L2_attn_in['wk'], 'L2_attn_bk': _L2_attn_in['bk'], 'L2_attn_wv': _L2_attn_in['wv'], 'L2_attn_bv': _L2_attn_in['bv'], 'L2_attn_wo': _L2_attn_in['wo'], 'L2_attn_bo': _L2_attn_in['bo'], 'L2_ffn_norm1_w': _L2_ffn_in['norm1_w'], 'L2_ffn_w_qkv': _L2_ffn_in['w_qkv'], 'L2_ffn_w_out': _L2_ffn_in['w_out'], 'L2_ffn_norm2_w': _L2_ffn_in['norm2_w'], 'L2_ffn_w_router': _L2_ffn_in['w_router'], 'L2_ffn_w_gate_up': _L2_ffn_in['w_gate_up'], 'L2_ffn_w_down': _L2_ffn_in['w_down'], 'L3_attn_w_q': _L3_attn_in['w_q'], 'L3_attn_w_k': _L3_attn_in['w_k'], 'L3_attn_w_v': _L3_attn_in['w_v'], 'L3_attn_w_o': _L3_attn_in['w_o'], 'L3_attn_w_ln1': _L3_attn_in['w_ln1'], 'L3_attn_w_ln2': _L3_attn_in['w_ln2'], 'L3_attn_w_ffn_w1': _L3_attn_in['w_ffn_w1'], 'L3_attn_w_ffn_w2': _L3_attn_in['w_ffn_w2'], 'L3_attn_w_ffn_w3': _L3_attn_in['w_ffn_w3'], 'L3_ffn_Wg_s': _L3_ffn_in['Wg_s'], 'L3_ffn_Wu_s': _L3_ffn_in['Wu_s'], 'L3_ffn_Wd_s': _L3_ffn_in['Wd_s'], 'L3_ffn_Wg_r': _L3_ffn_in['Wg_r'], 'L3_ffn_Wu_r': _L3_ffn_in['Wu_r'], 'L3_ffn_Wd_r': _L3_ffn_in['Wd_r'], 'L3_ffn_W_router': _L3_ffn_in['W_router'], 'L3_ffn_expert_bias': _L3_ffn_in['expert_bias']}

def reference(x, L0_conv_ln1_w, L0_conv_ln1_b, L0_conv_qkv_w, L0_conv_qkv_b, L0_conv_proj_w, L0_conv_proj_b, L0_conv_rel_pos_h, L0_conv_rel_pos_w, L0_conv_ln2_w, L0_conv_ln2_b, L0_conv_fc1_w, L0_conv_fc1_b, L0_conv_fc2_w, L0_conv_fc2_b, L1_conv_w_qkv, L1_conv_b_qkv, L1_conv_rel_pos_h, L1_conv_rel_pos_w, L1_conv_w_proj, L1_conv_b_proj, L2_attn_wq, L2_attn_bq, L2_attn_wk, L2_attn_bk, L2_attn_wv, L2_attn_bv, L2_attn_wo, L2_attn_bo, L2_ffn_norm1_w, L2_ffn_w_qkv, L2_ffn_w_out, L2_ffn_norm2_w, L2_ffn_w_router, L2_ffn_w_gate_up, L2_ffn_w_down, L3_attn_w_q, L3_attn_w_k, L3_attn_w_v, L3_attn_w_o, L3_attn_w_ln1, L3_attn_w_ln2, L3_attn_w_ffn_w1, L3_attn_w_ffn_w2, L3_attn_w_ffn_w3, L3_ffn_Wg_s, L3_ffn_Wu_s, L3_ffn_Wd_s, L3_ffn_Wg_r, L3_ffn_Wu_r, L3_ffn_Wd_r, L3_ffn_W_router, L3_ffn_expert_bias):
    import jax
    import jax.numpy as jnp

    def _L0_conv_ref(x, ln1_w, ln1_b, qkv_w, qkv_b, proj_w, proj_b, rel_pos_h, rel_pos_w, ln2_w, ln2_b, fc1_w, fc1_b, fc2_w, fc2_b):
        import jax, jax.numpy as jnp
        import numpy as np
        DIM = 192
        NH = 12
        HD = DIM // NH
        WS = 14
        EPS = 1e-05

        def _ln(x, w, b):
            m = jnp.mean(x, -1, keepdims=True)
            v = jnp.var(x, -1, keepdims=True)
            return (x - m) * jax.lax.rsqrt(v + EPS) * w + b

        def _block(x, ln1_w, ln1_b, qkv_w, qkv_b, proj_w, proj_b, rel_pos_h, rel_pos_w, ln2_w, ln2_b, fc1_w, fc1_b, fc2_w, fc2_b):
            B, H, W, C = x.shape
            shortcut = x
            xn = _ln(x, ln1_w, ln1_b)
            pad_h = -H % WS
            pad_w = -W % WS
            xp = jnp.pad(xn, ((0, 0), (0, pad_h), (0, pad_w), (0, 0)))
            Hp, Wp = (H + pad_h, W + pad_w)
            nh, nw = (Hp // WS, Wp // WS)
            xw = xp.reshape(B, nh, WS, nw, WS, C).transpose(0, 1, 3, 2, 4, 5)
            xw = xw.reshape(B * nh * nw, WS, WS, C)
            Bw = B * nh * nw
            N = WS * WS
            qkv = xw.reshape(Bw, N, C) @ qkv_w + qkv_b
            qkv = qkv.reshape(Bw, N, 3, NH, HD).transpose(2, 0, 3, 1, 4)
            q, k, v = (qkv[0], qkv[1], qkv[2])
            scale = HD ** (-0.5)
            attn = jnp.einsum('bhnd,bhmd->bhnm', q * scale, k)
            idx = jnp.arange(WS)[:, None] - jnp.arange(WS)[None, :] + (WS - 1)
            Rh = rel_pos_h[idx]
            Rw = rel_pos_w[idx]
            rq = q.reshape(Bw, NH, WS, WS, HD)
            rel_h = jnp.einsum('bnhwc,hkc->bnhwk', rq, Rh)
            rel_w = jnp.einsum('bnhwc,wkc->bnhwk', rq, Rw)
            attn = (attn.reshape(Bw, NH, WS, WS, WS, WS) + rel_h[..., :, None] + rel_w[..., None, :]).reshape(Bw, NH, N, N)
            attn = jax.nn.softmax(attn, axis=-1)
            out = jnp.einsum('bhnm,bhmd->bhnd', attn, v)
            out = out.transpose(0, 2, 1, 3).reshape(Bw, WS, WS, C)
            out = out @ proj_w + proj_b
            out = out.reshape(B, nh, nw, WS, WS, C).transpose(0, 1, 3, 2, 4, 5)
            out = out.reshape(B, Hp, Wp, C)[:, :H, :W, :]
            x = shortcut + out
            h = _ln(x, ln2_w, ln2_b)
            h = jax.nn.gelu(h @ fc1_w + fc1_b, approximate=False)
            x = x + (h @ fc2_w + fc2_b)
            return x
        return _block(x, ln1_w, ln1_b, qkv_w, qkv_b, proj_w, proj_b, rel_pos_h, rel_pos_w, ln2_w, ln2_b, fc1_w, fc1_b, fc2_w, fc2_b)

    def _L1_conv_ref(x, w_qkv, b_qkv, rel_pos_h, rel_pos_w, w_proj, b_proj):
        import jax, jax.numpy as jnp
        import numpy as np
        NUM_HEADS = 12

        def get_rel_pos(q_size, k_size, rel_pos):
            max_rel_dist = int(2 * max(q_size, k_size) - 1)
            if rel_pos.shape[0] != max_rel_dist:
                rel_pos = jax.image.resize(rel_pos, (max_rel_dist, rel_pos.shape[1]), method='linear')
            q_coords = jnp.arange(q_size)[:, None] * max(k_size / q_size, 1.0)
            k_coords = jnp.arange(k_size)[None, :] * max(q_size / k_size, 1.0)
            rel = (q_coords - k_coords + (k_size - 1) * max(q_size / k_size, 1.0)).astype(jnp.int32)
            return rel_pos[rel.reshape(-1)].reshape(q_size, k_size, -1)
        B, H, W, C = x.shape
        heads = NUM_HEADS
        hd = C // heads
        S = H * W
        qkv = x @ w_qkv + b_qkv
        qkv = qkv.reshape(B, S, 3, heads, hd).transpose(2, 0, 3, 1, 4)
        qkv = qkv.reshape(3, B * heads, S, hd)
        q, k, v = (qkv[0], qkv[1], qkv[2])
        attn = q * hd ** (-0.5) @ k.transpose(0, 2, 1)
        rh = get_rel_pos(H, H, rel_pos_h)
        rw = get_rel_pos(W, W, rel_pos_w)
        r_q = q.reshape(B * heads, H, W, hd)
        rel_h = jnp.einsum('bhwc,hkc->bhwk', r_q, rh)
        rel_w = jnp.einsum('bhwc,wkc->bhwk', r_q, rw)
        attn = (attn.reshape(B * heads, H, W, H, W) + rel_h[:, :, :, :, None] + rel_w[:, :, :, None, :]).reshape(B * heads, S, S)
        attn = jax.nn.softmax(attn, axis=-1)
        out = (attn @ v).reshape(B, heads, H, W, hd).transpose(0, 2, 3, 1, 4).reshape(B, H, W, C)
        return out @ w_proj + b_proj

    def _L2_attn_ref(x, wq, bq, wk, bk, wv, bv, wo, bo):
        import jax, jax.numpy as jnp
        import numpy as np
        B, T, D, NH = (4, 512, 192, 12)
        DH = D // NH
        NEG = -100000.0
        Bx, Tx, E = x.shape

        def heads(w, b):
            return (x @ w.T + b).reshape(Bx, Tx, NH, DH).transpose(0, 2, 1, 3)
        Q, K, V = (heads(wq, bq), heads(wk, bk), heads(wv, bv))
        scale = 1.0 / jnp.sqrt(jnp.float32(DH))
        QK = jnp.einsum('bhqd,bhkd->bhqk', Q, K) * scale
        causal = jnp.tril(jnp.ones((Tx, Tx), dtype=bool))
        QK = jnp.where(causal, QK, NEG)
        A = jax.nn.softmax(QK, axis=-1)
        Z = jnp.einsum('bhqk,bhkd->bhqd', A, V)
        Z = Z.transpose(0, 2, 1, 3).reshape(Bx, Tx, E)
        return Z @ wo.T + bo

    def _L2_ffn_ref(x, norm1_w, w_qkv, w_out, norm2_w, w_router, w_gate_up, w_down):
        import jax, jax.numpy as jnp
        import numpy as np
        HID = 192
        NQ = 12
        NKV = 3
        HD = 16
        REP = NQ // NKV
        E = 16
        TOPK = 2
        FF = 384
        EPS = 1e-06
        THETA = 10000.0

        def rms_norm(x, w):
            return x / jnp.sqrt(jnp.mean(x * x, axis=-1, keepdims=True) + EPS) * w

        def rope_tables(seq_len):
            inv = 1.0 / THETA ** (jnp.arange(0, HD, 2, dtype=jnp.float32) / HD)
            f = jnp.arange(seq_len, dtype=jnp.float32)[:, None] * inv[None, :]
            return (jnp.cos(f), jnp.sin(f))

        def apply_rope(t, cos, sin):
            B, S, H, _ = t.shape
            tr = t.reshape(B, S, H, HD // 2, 2)
            c = cos[None, :, None, :]
            s = sin[None, :, None, :]
            r0 = tr[..., 0] * c - tr[..., 1] * s
            r1 = tr[..., 0] * s + tr[..., 1] * c
            return jnp.stack([r0, r1], axis=-1).reshape(B, S, H, HD)

        def attention(x, w_qkv, w_out):
            B, S, _ = x.shape
            qkv = x @ w_qkv
            q, k, v = jnp.split(qkv, [NQ * HD, (NQ + NKV) * HD], axis=-1)
            q = q.reshape(B, S, NQ, HD)
            k = k.reshape(B, S, NKV, HD)
            v = v.reshape(B, S, NKV, HD)
            cos, sin = rope_tables(S)
            q = apply_rope(q, cos, sin)
            k = apply_rope(k, cos, sin)
            k = jnp.repeat(k, REP, axis=2)
            v = jnp.repeat(v, REP, axis=2)
            q = q.transpose(0, 2, 1, 3)
            k = k.transpose(0, 2, 1, 3)
            v = v.transpose(0, 2, 1, 3)
            scores = jnp.einsum('bhqd,bhkd->bhqk', q, k) / jnp.sqrt(jnp.float32(HD))
            causal = jnp.tril(jnp.ones((S, S), dtype=bool))
            scores = jnp.where(causal[None, None], scores, jnp.finfo(scores.dtype).min)
            attn = jax.nn.softmax(scores, axis=-1)
            out = jnp.einsum('bhqk,bhkd->bhqd', attn, v)
            out = out.transpose(0, 2, 1, 3).reshape(B, S, NQ * HD)
            return out @ w_out

        def moe_ffn(x2d, w_router, w_gate_up, w_down):
            logits = x2d @ w_router
            probs = jax.nn.softmax(logits, axis=-1)
            vals, idx = jax.lax.top_k(probs, TOPK)
            vals = vals / jnp.sum(vals, axis=-1, keepdims=True)
            combine = jnp.sum(jax.nn.one_hot(idx, E, dtype=x2d.dtype) * vals[..., None], axis=1)
            out = jnp.zeros_like(x2d)
            for e in range(E):
                gu = x2d @ w_gate_up[e]
                gate, up = jnp.split(gu, 2, axis=-1)
                h = jax.nn.silu(gate) * up
                out = out + combine[:, e:e + 1] * (h @ w_down[e])
            return out
        B, S, _ = x.shape
        h = x + attention(rms_norm(x, norm1_w), w_qkv, w_out)
        moe_in = rms_norm(h, norm2_w).reshape(B * S, HID)
        out = h + moe_ffn(moe_in, w_router, w_gate_up, w_down).reshape(B, S, HID)
        return out

    def _L3_attn_ref(x, w_q, w_k, w_v, w_o, w_ln1, w_ln2, w_ffn_w1, w_ffn_w2, w_ffn_w3):
        import jax, jax.numpy as jnp
        import numpy as np
        NUM_HEADS = 12
        THETA = 10000.0
        EPS = 1e-05

        def _rmsnorm(x, w):
            xf = x.astype(jnp.float32)
            var = jnp.mean(xf * xf, axis=-1, keepdims=True)
            return (xf * jax.lax.rsqrt(var + EPS) * w).astype(x.dtype)

        def _rope(x, cos, sin):
            c = cos[None, :, None, :]
            s = sin[None, :, None, :]
            xe = x[..., 0::2]
            xo = x[..., 1::2]
            oe = xe * c - xo * s
            oo = xe * s + xo * c
            return jnp.stack([oe, oo], axis=-1).reshape(x.shape)
        B, S, D = x.shape
        H = NUM_HEADS
        hd = D // H
        hn = _rmsnorm(x, w_ln1)
        q = (hn @ w_q.T).reshape(B, S, H, hd)
        k = (hn @ w_k.T).reshape(B, S, H, hd)
        v = (hn @ w_v.T).reshape(B, S, H, hd)
        freqs = 1.0 / THETA ** (jnp.arange(0, hd, 2, dtype=jnp.float32) / hd)
        ang = jnp.arange(S, dtype=jnp.float32)[:, None] * freqs[None, :]
        cos, sin = (jnp.cos(ang), jnp.sin(ang))
        q = _rope(q, cos, sin)
        k = _rope(k, cos, sin)
        q = q.transpose(0, 2, 1, 3)
        k = k.transpose(0, 2, 1, 3)
        v = v.transpose(0, 2, 1, 3)
        scale = 1.0 / np.sqrt(hd).astype(np.float32)
        scores = jnp.einsum('bhqd,bhkd->bhqk', q, k) * scale
        causal = jnp.triu(jnp.ones((S, S), dtype=bool), k=1)
        scores = jnp.where(causal, -jnp.inf, scores)
        attn = jax.nn.softmax(scores, axis=-1)
        ctx = jnp.einsum('bhqk,bhkd->bhqd', attn, v)
        ctx = ctx.transpose(0, 2, 1, 3).reshape(B, S, D)
        h = x + ctx @ w_o.T
        g = _rmsnorm(h, w_ln2)
        ffn = jax.nn.silu(g @ w_ffn_w1.T) * (g @ w_ffn_w3.T) @ w_ffn_w2.T
        return h + ffn

    def _L3_ffn_ref(x, Wg_s, Wu_s, Wd_s, Wg_r, Wu_r, Wd_r, W_router, expert_bias):
        import jax, jax.numpy as jnp
        import numpy as np
        K_ACTIVE = 2
        B, S, D = x.shape
        E = Wg_r.shape[0]
        xf = x.reshape(-1, D)
        T = xf.shape[0]
        g_s = jax.nn.silu(jnp.einsum('td,edf->etf', xf, Wg_s))
        u_s = jnp.einsum('td,edf->etf', xf, Wu_s)
        shared_out = jnp.einsum('etf,efd->td', g_s * u_s, Wd_s)
        logits = xf @ W_router + expert_bias
        top_vals, top_idx = jax.lax.top_k(logits, K_ACTIVE)
        rw = jax.nn.softmax(top_vals, axis=-1)
        combine = jnp.zeros((T, E), xf.dtype).at[jnp.arange(T)[:, None], top_idx].set(rw)
        g_r = jax.nn.silu(jnp.einsum('td,edf->etf', xf, Wg_r))
        u_r = jnp.einsum('td,edf->etf', xf, Wu_r)
        out_e = jnp.einsum('etf,efd->etd', g_r * u_r, Wd_r)
        routed_out = jnp.einsum('etd,te->td', out_e, combine)
        return (shared_out + routed_out).reshape(B, S, D)

    def _gn(v, G=32, eps=1e-05):
        B_, H_, W_, C_ = v.shape
        g = v.reshape(B_, H_, W_, G, C_ // G)
        m = jnp.mean(g, axis=(1, 2, 4), keepdims=True)
        s = jnp.var(g, axis=(1, 2, 4), keepdims=True)
        return ((g - m) / jnp.sqrt(s + eps)).reshape(v.shape)

    def _ln_c(v, eps=1e-06):
        m = jnp.mean(v, axis=-1, keepdims=True)
        s = jnp.var(v, axis=-1, keepdims=True)
        return (v - m) / jnp.sqrt(s + eps)

    def _ln_t(v, eps=1e-05):
        m = jnp.mean(v, axis=-1, keepdims=True)
        s = jnp.var(v, axis=-1, keepdims=True)
        return (v - m) / jnp.sqrt(s + eps)

    def _to_tokens(v):
        B_, H_, W_, C_ = v.shape
        return v.reshape(B_, H_ * W_, C_)

    def _from_tokens(t, like):
        return t.reshape(like.shape)
    x = _L0_conv_ref(x, L0_conv_ln1_w, L0_conv_ln1_b, L0_conv_qkv_w, L0_conv_qkv_b, L0_conv_proj_w, L0_conv_proj_b, L0_conv_rel_pos_h, L0_conv_rel_pos_w, L0_conv_ln2_w, L0_conv_ln2_b, L0_conv_fc1_w, L0_conv_fc1_b, L0_conv_fc2_w, L0_conv_fc2_b)
    x = x + _L1_conv_ref(_gn(x), L1_conv_w_qkv, L1_conv_b_qkv, L1_conv_rel_pos_h, L1_conv_rel_pos_w, L1_conv_w_proj, L1_conv_b_proj)
    t = _to_tokens(x)
    t = t + _L2_attn_ref(_ln_t(t), L2_attn_wq, L2_attn_bq, L2_attn_wk, L2_attn_bk, L2_attn_wv, L2_attn_bv, L2_attn_wo, L2_attn_bo)
    t = t + _L2_ffn_ref(_ln_t(t), L2_ffn_norm1_w, L2_ffn_w_qkv, L2_ffn_w_out, L2_ffn_norm2_w, L2_ffn_w_router, L2_ffn_w_gate_up, L2_ffn_w_down)
    t = t + _L3_attn_ref(_ln_t(t), L3_attn_w_q, L3_attn_w_k, L3_attn_w_v, L3_attn_w_o, L3_attn_w_ln1, L3_attn_w_ln2, L3_attn_w_ffn_w1, L3_attn_w_ffn_w2, L3_attn_w_ffn_w3)
    t = t + _L3_ffn_ref(_ln_t(t), L3_ffn_Wg_s, L3_ffn_Wu_s, L3_ffn_Wd_s, L3_ffn_Wg_r, L3_ffn_Wu_r, L3_ffn_Wd_r, L3_ffn_W_router, L3_ffn_expert_bias)
    x = _from_tokens(t, x)
    return x

_drawn_inputs = setup_inputs


def setup_inputs(seed=0):
    import zlib

    import numpy as np

    out = dict(_drawn_inputs(seed))
    spreads = {'L0_conv_ln1_w': (1.0, 0.6),
     'L0_conv_ln1_b': (0.0, 0.489),
     'L0_conv_qkv_b': (0.0, 0.1),
     'L0_conv_proj_b': (0.0, 0.1),
     'L0_conv_ln2_w': (1.0, 0.6),
     'L0_conv_ln2_b': (0.0, 0.438),
     'L0_conv_fc1_b': (0.0, 0.1),
     'L0_conv_fc2_b': (0.0, 0.1),
     'L1_conv_b_qkv': (0.0, 0.1),
     'L1_conv_b_proj': (0.0, 0.1),
     'L2_ffn_norm1_w': (1.0, 0.6),
     'L2_ffn_norm2_w': (1.0, 0.6),
     'L3_attn_w_ln1': (1.0, 0.6),
     'L3_attn_w_ln2': (1.0, 0.6),
     'L3_ffn_expert_bias': (0.0, 0.1)}
    factors = {'L0_conv_qkv_w': 3.292,
     'L0_conv_rel_pos_h': 8.0,
     'L0_conv_rel_pos_w': 8.0,
     'L1_conv_w_qkv': 2.804,
     'L1_conv_rel_pos_h': 8.0,
     'L1_conv_rel_pos_w': 8.0,
     'L2_attn_bq': 8.0,
     'L2_attn_bk': 8.0,
     'L2_ffn_w_qkv': 3.607,
     'L2_ffn_w_out': 3.911,
     'L2_ffn_w_router': 6.53,
     'L2_ffn_w_gate_up': 6.555,
     'L2_ffn_w_down': 7.205,
     'L3_attn_w_q': 8.0,
     'L3_attn_w_k': 8.0,
     'L3_attn_w_v': 4.336,
     'L3_attn_w_o': 4.991,
     'L3_attn_w_ffn_w1': 5.283,
     'L3_attn_w_ffn_w2': 5.078,
     'L3_attn_w_ffn_w3': 5.674}
    for name, (base, spread) in spreads.items():
        noise = np.random.default_rng([zlib.crc32(name.encode()), seed]).standard_normal(out[name].shape)
        drawn = base * np.exp(spread * noise) if base else spread * noise
        out[name] = jnp.asarray(drawn.astype(out[name].dtype))
    for name, factor in factors.items():
        out[name] = (out[name] * factor).astype(out[name].dtype)
    return out
```

```python
from contextlib import ExitStack, contextmanager

import concourse.bass as bass
from concourse import mybir

F32 = mybir.dt.float32
BF16 = mybir.dt.bfloat16
I32 = mybir.dt.int32
U32 = mybir.dt.uint32
ALU = mybir.AluOpType
ACT = mybir.ActivationFunctionType
AX = mybir.AxisListType

IMAGES, SIDE, C = 4, 16, 192
TOKENS = SIDE * SIDE
P = 128
TILES = IMAGES * TOKENS // P
PAIR = 2
PT = PAIR * TOKENS // P
PN = PAIR * TOKENS
HEADS, HD = 12, 16
CH = C // 2
VW = HD + 1
WS = 14
WN = WS * WS
WINDOWS = 4
QSCALE = HD ** -0.5
FF = 768
EF = 384
BANK = 512
RSQRT_SEED = 0x5F3759DF
WINDOW_BOX = [(0, 14, 0, 14), (0, 14, 14, 2), (14, 2, 0, 14), (14, 2, 14, 2)]
WINDOW_AT = [0, 196, 224, 252]


class Chain:

    def __init__(self, eng, sem):
        self.eng, self.sem, self.n = eng, sem, 0

    def free(self, ins):
        self.n += 1
        ins.then_inc(self.sem, 1)

    def wait(self):
        self.eng.wait_ge(self.sem, self.n)

    def __call__(self, ins):
        self.free(ins)
        self.wait()


def unique(names, name):
    names[name] = names.get(name, 0) + 1
    return name if names[name] == 1 else f"{name}_{names[name]}"


@contextmanager
def stage(nc, names):
    sems = []

    def sem(name):
        sems.append(nc.alloc_semaphore(name=unique(names, name)))
        return sems[-1]

    with nc.Block() as block:
        yield block, sem
    nc.clear_and_free_semaphores(sems)
    nc.all_engine_barrier()


class Scratch:

    def __init__(self, sb):
        self.st = sb("norm_stats", [P, PT, 6])
        self.mv = sb("norm_mean_var", [P, PT, 2])
        self.v = sb("norm_v", [P, PT])
        self.a = sb("norm_a", [P, PT])
        self.y = sb("norm_rstd", [P, PT])


def rsqrt(nc, chain, y, v, a, eps):
    chain(nc.vector.tensor_scalar(v, v, eps, None, ALU.add))
    chain(nc.vector.tensor_scalar(a.bitcast(I32), v.bitcast(I32), 1, None, ALU.logical_shift_right))
    chain(nc.vector.tensor_scalar(y.bitcast(I32), a.bitcast(I32), -1, RSQRT_SEED, ALU.mult, ALU.add))
    for _ in range(4):
        chain(nc.vector.scalar_tensor_tensor(a, y, -0.5, y, ALU.mult, ALU.mult))
        chain(nc.vector.tensor_tensor(a, a, v, ALU.mult))
        chain(nc.vector.scalar_tensor_tensor(y, a, 1.5, y, ALU.add, ALU.mult))


def normalise(nc, chain, s, dst, src, eps, centre):
    for t in range(PT):
        chain.free(nc.vector.bn_stats(s.st[:, t, :], src[:, t, :]))
    chain.wait()
    for t in range(PT):
        chain.free(nc.vector.bn_aggr(s.mv[:, t, :], s.st[:, t, :]))
    chain.wait()
    if centre:
        chain(nc.vector.tensor_copy(s.v[:, :], s.mv[:, :, 1]))
    else:
        chain(nc.vector.tensor_tensor(s.a[:, :], s.mv[:, :, 0], s.mv[:, :, 0], ALU.mult))
        chain(nc.vector.tensor_tensor(s.v[:, :], s.a[:, :], s.mv[:, :, 1], ALU.add))
    rsqrt(nc, chain, s.y[:, :], s.v[:, :], s.a[:, :], eps)
    for t in range(PT):
        if centre:
            chain.free(nc.vector.tensor_scalar(dst[:, t, :], src[:, t, :], s.mv[:, t, 0:1], s.y[:, t:t + 1],
                                               ALU.subtract, ALU.mult))
        else:
            chain.free(nc.vector.tensor_scalar(dst[:, t, :], src[:, t, :], s.y[:, t:t + 1], None, ALU.mult))
    chain.wait()


def turn_tiles(nc, banks, src, ident, turned):
    for c in range(2):
        for t in range(PT):
            ins = nc.tensor.transpose(banks[0:CH, c, t * P:(t + 1) * P], src[:, t, c * CH:(c + 1) * CH], ident[:, :])
        ins.then_inc(turned, 1)


def dense(nc, out, lhs, rhs, n_rows=(CH, CH)):
    for k, rows in enumerate(n_rows):
        ins = nc.tensor.matmul(out, lhs(k, rows), rhs(k, rows), start=(k == 0), stop=(k == 1))
    return ins


BIASED = (CH, CH + 1)


def relative_setup(nc, env, w, windows):
    with stage(nc, env.names) as (block, sem):
        loaded, win_made, win_read, steps = sem("loaded"), sem("win_made"), sem("win_read"), sem("steps")
        filled = sem("filled")

        @block.sync
        def _(sp):
            for dst, src in w.loads:
                sp.dma_start(dst, src).then_inc(loaded, 16)
            sp.wait_ge(loaded, 16 * len(w.loads))

        @block.gpsimd
        def _(pool):
            chain = Chain(pool, filled)
            chain(nc.gpsimd.memset(w.V[:, :, :, HD:VW], 1.0))
            chain(nc.gpsimd.memset(w.xT[CH:CH + 1, 1, :], 1.0))
            chain(nc.gpsimd.memset(w.OT[CH:CH + 1, 1, :], 1.0))
            if windows:
                chain(nc.gpsimd.memset(w.xw[0:CH, :, :, :], 0.0))
                chain(nc.gpsimd.memset(w.xw[CH:CH + 1, 1, :, :], 1.0))

        if not windows:
            @block.tensor
            def _(pe):
                pe.wait_ge(loaded, 16 * len(w.loads))
                for n in range(2):
                    ins = nc.tensor.matmul(env.banks[0:CH, n, 0:TOKENS], w.rel[:, n, :], w.shrink[:, :],
                                           start=True, stop=True)
                ins.then_inc(win_made, 1)

        @block.vector
        def _(dve):
            chain = Chain(dve, steps)
            dve.wait_ge(loaded, 16 * len(w.loads))
            if not windows:
                dve.wait_ge(win_made, 1)
                for n in range(2):
                    chain.free(nc.vector.tensor_copy(w.win[:, n, :, :].rearrange("p a b -> p (a b)"),
                                                     env.banks[0:CH, n, 0:TOKENS]))
                chain.wait()
            for s in range(2):
                chain.free(nc.vector.tensor_copy(w.bd[:, 0, :, s, 16:32], w.qslot[:, None, s, :].to_broadcast([CH, SIDE, HD])))
                chain.free(nc.vector.memset(w.bd[:, 1, :, s, 16:32], 0.0))
                for n in range(2):
                    chain.free(nc.vector.tensor_scalar(w.bd[:, n, :, s, 0:16], w.win[:, n, :, :],
                                                       w.odd[:, s:s + 1], None, ALU.mult))
            if windows:
                for g in range(6):
                    for m in range(PAIR):
                        chain.free(nc.vector.tensor_scalar(w.K[:, g, m, :], w.hot[:, :], w.kpad[:, g:g + 1], None,
                                                           ALU.add))
            chain.wait()


def relative_project(nc, env, w, ip, windows):
    R, xn, banks, ident = env.R, env.xn, env.banks, env.ident
    n_vjobs = 8 if windows else PT
    with stage(nc, env.names) as (block, sem):
        steps = sem("steps")
        normed, turned, xT_ready = sem("normed"), sem("turned"), sem("xT_ready")
        stats_ready, group_ready, affine_ready = sem("stats_ready"), sem("group_ready"), sem("affine_ready")
        xw_ready, xw_steps = sem("xw_ready"), sem("xw_steps")
        a_done, a_out, k_done, k_out = sem("a_done"), sem("a_out"), sem("k_done"), sem("k_out")

        @block.vector
        def _(dve):
            chain = Chain(dve, steps)
            chain(nc.vector.tensor_copy(R[:, :, :], env.X[:, bass.ds(ip * PT, PT), :]))
            if windows:
                normalise(nc, chain, env.s, xn, R, 1e-5, True)
            dve.sem_inc(normed, 1)
            if not windows:
                dve.wait_ge(turned, 2)
                for c in range(2):
                    for m in range(PAIR):
                        chain.free(nc.vector.bn_stats(w.gst[:, c * 2 + m, :], banks[0:CH, c, m * TOKENS:(m + 1) * TOKENS]))
                chain.wait()
                for j in range(4):
                    chain.free(nc.vector.bn_aggr(w.gmv[:, j, :], w.gst[:, j, :]))
                chain.wait()
                chain(nc.vector.tensor_tensor(w.ga[:, :], w.gmv[:, :, 0], w.gmv[:, :, 0], ALU.mult))
                chain(nc.vector.tensor_tensor(w.gmv[:, :, 1], w.gmv[:, :, 1], w.ga[:, :], ALU.add))
                dve.sem_inc(stats_ready, 1)
                dve.wait_ge(group_ready, 1)
                chain(nc.vector.tensor_copy(w.gmv[:, :, :].rearrange("p a b -> p (a b)"), banks[0:CH, 2, 0:8]))
                chain(nc.vector.tensor_tensor(w.ga[:, :], w.gmv[:, :, 0], w.gmv[:, :, 0], ALU.mult))
                chain(nc.vector.tensor_tensor(w.gv[:, :], w.gmv[:, :, 1], w.ga[:, :], ALU.subtract))
                rsqrt(nc, chain, w.gscale[:, :], w.gv[:, :], w.ga[:, :], 1e-5)
                chain(nc.vector.scalar_tensor_tensor(w.gbias[:, :], w.gmv[:, :, 0], -1.0, w.gscale[:, :], ALU.mult, ALU.mult))
                dve.sem_inc(affine_ready, 1)
            for g in range(6):
                dve.wait_ge(k_done, g + 1)
                src = banks[:, 4 + g % 4, :]
                if windows:
                    for n, (h0, nh, w0, nw) in enumerate(WINDOW_BOX):
                        real = src.rearrange("p (m a b) -> p m a b", m=PAIR, b=SIDE)[:, :, h0:h0 + nh, w0:w0 + nw]
                        dst = w.K[:, g, :, n * WN:(n + 1) * WN].rearrange("p m (a b) -> p m a b", b=WS)[:, :, 0:nh, 0:nw]
                        hot = w.hot[:, n * WN:(n + 1) * WN].rearrange("p (a b) -> p a b", b=WS)[:, None, 0:nh, 0:nw]
                        ins = nc.vector.tensor_tensor(dst, real, hot.to_broadcast([P, PAIR, nh, nw]), ALU.add)
                else:
                    for m in range(PAIR):
                        ins = nc.vector.tensor_tensor(w.K[:, g, m, :], src[:, m * TOKENS:(m + 1) * TOKENS],
                                                      w.hot[:, :], ALU.add)
                ins.then_inc(k_out, 1)
            dve.wait_ge(k_out, 6)

        @block.scalar
        def _(act):
            for c in range(2):
                act.wait_ge(turned, c + 1)
                if windows:
                    nc.scalar.activation(w.xT[0:CH, c, :], banks[0:CH, c, :], ACT.Identity,
                                         bias=w.nb[:, c:c + 1], scale=w.nw[:, c:c + 1]).then_inc(xT_ready, 1)
                else:
                    act.wait_ge(affine_ready, 1)
                    for m in range(PAIR):
                        j = c * 2 + m
                        ins = nc.scalar.activation(w.xT[0:CH, c, m * TOKENS:(m + 1) * TOKENS],
                                                   banks[0:CH, c, m * TOKENS:(m + 1) * TOKENS], ACT.Identity,
                                                   bias=w.gbias[:, j:j + 1], scale=w.gscale[:, j:j + 1])
                    ins.then_inc(xT_ready, 1)
            for a in range(2 + n_vjobs + 6):
                act.wait_ge(a_done, a + 1)
                bank = banks[:, a % 4, :]
                if a < 2:
                    ins = nc.scalar.activation(w.qT[:, a, :], bank[0:CH, :], ACT.Copy)
                elif a < 2 + n_vjobs:
                    j = a - 2
                    if windows:
                        ins = nc.scalar.activation(w.V[0:98, 2 * j:2 * j + 2, :, 0:HD],
                                                   bank[0:98, 0:2 * C].rearrange("p (n h d) -> p n h d", n=2, d=HD), ACT.Copy)
                    else:
                        ins = nc.scalar.activation(w.V[:, j, :, 0:HD], bank[:, 0:C].rearrange("p (h d) -> p h d", d=HD),
                                                   ACT.Copy)
                elif windows:
                    for n, (h0, nh, w0, nw) in enumerate(WINDOW_BOX):
                        src = bank.rearrange("p (m a b) -> p m a b", m=PAIR, b=SIDE)[:, :, h0:h0 + nh, w0:w0 + nw]
                        dst = w.Q[:, a - 2 - n_vjobs, :].rearrange("p (m t) -> p m t", m=PAIR)
                        dst = dst[:, :, WINDOW_AT[n]:WINDOW_AT[n] + nh * nw].rearrange("p m (a b) -> p m a b", b=nw)
                        ins = nc.scalar.activation(dst, src, ACT.Copy)
                else:
                    ins = nc.scalar.activation(w.Q[:, a - 2 - n_vjobs, :], bank, ACT.Copy)
                ins.then_inc(a_out, 1)
            act.wait_ge(a_out, 2 + n_vjobs + 6)

        if windows:
            @block.gpsimd
            def _(pool):
                chain = Chain(pool, xw_steps)
                pool.wait_ge(xT_ready, 2)
                for c in range(2):
                    for n, (h0, nh, w0, nw) in enumerate(WINDOW_BOX):
                        for m in range(PAIR):
                            src = w.xT[0:CH, c, m * TOKENS:(m + 1) * TOKENS].rearrange("p (a b) -> p a b", b=SIDE)
                            dst = w.xw[0:CH, c, m, n * WN:(n + 1) * WN].rearrange("p (a b) -> p a b", b=WS)
                            chain(nc.gpsimd.tensor_copy(dst[:, 0:nh, 0:nw], src[:, h0:h0 + nh, w0:w0 + nw]))
                pool.sem_inc(xw_ready, 1)

        @block.tensor
        def _(pe):
            pe.wait_ge(normed, 1)
            turn_tiles(nc, banks, xn if windows else R, ident, turned)
            if not windows:
                pe.wait_ge(stats_ready, 1)
                nc.tensor.matmul(banks[0:CH, 2, 0:8], w.gavg[:, :], w.gmv[:, :, :].rearrange("p a b -> p (a b)"),
                                 start=True, stop=True).then_inc(group_ready, 1)
            pe.wait_ge(xT_ready, 2)

            def queries(a):
                dense(nc, banks[0:CH, a % 4, :], lambda k, r: w.wq[0:r, k, a * CH:(a + 1) * CH],
                      lambda k, r: w.xT[0:r, k, :], BIASED).then_inc(a_done, 1)

            def keys(g):
                if g >= 4:
                    pe.wait_ge(k_out, g - 3)
                dense(nc, banks[:, 4 + g % 4, :], lambda k, r: w.wk[0:r, k, g * P:(g + 1) * P],
                      lambda k, r: w.xT[0:r, k, :], BIASED).then_inc(k_done, 1)

            def values(j):
                a = 2 + j
                if a >= 4:
                    pe.wait_ge(a_out, a - 3)
                if not windows:
                    ins = dense(nc, banks[:, a % 4, 0:C], lambda k, r: w.xT[0:r, k, j * P:(j + 1) * P],
                                lambda k, r: w.wv[0:r, k, :], BIASED)
                else:
                    for n in range(2):
                        m, at = divmod((2 * j + n) * 98, WINDOWS * WN)
                        ins = dense(nc, banks[0:98, a % 4, n * C:(n + 1) * C], lambda k, r: w.xw[0:r, k, m, at:at + 98],
                                    lambda k, r: w.wv[0:r, k, :], BIASED)
                ins.then_inc(a_done, 1)

            def relative(g):
                a = 2 + n_vjobs + g
                pe.wait_ge(a_out, a - 3)
                row, c = 32 * (g % 3), g // 3
                q = w.qT[row:row + 32, c, :].rearrange("p (m a b) -> p m a b", m=PAIR, b=SIDE)
                o = banks[:, a % 4, :].rearrange("p (m a b) -> p m a b", m=PAIR, b=SIDE)
                for r in range(SIDE):
                    for s in range(2):
                        nc.tensor.matmul(o[64 * s:64 * s + 32, :, r, :], w.bd[row:row + 32, 0, r, s, :], q[:, :, r, :],
                                         start=True, stop=True)
                        ins = nc.tensor.matmul(o[64 * s + 32:64 * s + 64, :, :, r], w.bd[row:row + 32, 1, r, s, :],
                                               q[:, :, :, r], start=True, stop=True)
                ins.then_inc(a_done, 1)

            queries(0)
            queries(1)
            for g in range(6):
                keys(g)
            if windows:
                pe.wait_ge(xw_ready, 1)
            for j in range(n_vjobs):
                values(j)
            for g in range(6):
                relative(g)


class Layout:

    def __init__(self, kind, w):
        self.kind, self.w = kind, w
        self.tiles = 3 if kind == "windows" else 2
        self.slots = 3 if kind == "causal" else 2
        self.slot_rows = 32 if kind == "causal" else 64

    def rows(self, t):
        return P if self.kind != "windows" else (98, 98, 68)[t]

    def width(self, t):
        return {"windows": WN, "full": TOKENS, "causal": (t + 1) * P}[self.kind]

    def chunk(self):
        return 98 if self.kind == "windows" else P

    def chunks(self, t):
        return self.width(t) // self.chunk()

    def parts(self, t):
        if self.kind != "windows":
            return [(0, P, 0)]
        return [(0, 98, 0)] if t < 2 else [(32 * (n - 1), WINDOW_BOX[n][1] * WINDOW_BOX[n][3], n) for n in (1, 2, 3)]

    def heads(self, hp):
        h = hp % self.slots + 2 * self.slots * (hp // self.slots)
        return h, h + self.slots

    def rows_of(self, h):
        r0 = self.slot_rows * (h % self.slots)
        return slice(r0, r0 + (HD if self.kind == "causal" else self.slot_rows)), h // self.slots

    def tokens(self, ap, m, t, window):
        if self.kind != "windows":
            return ap[:, m * TOKENS + t * P:m * TOKENS + (t + 1) * P]
        h0, nh, w0, nw = WINDOW_BOX[window]
        if window == 0:
            h0, nh = 7 * t, 7
        a = ap[:, m * TOKENS:(m + 1) * TOKENS].rearrange("p (a b) -> p a b", b=SIDE)
        return a[:, h0:h0 + nh, w0:w0 + nw]

    def q(self, m, t, h, window):
        rows, g = self.rows_of(h)
        q = self.w.Q[rows, g, :]
        if self.kind != "windows":
            return self.tokens(q, m, t, window)
        at = m * TOKENS + (98 * t if window == 0 else WINDOW_AT[window])
        return q[:, at:at + (98 if window == 0 else WINDOW_BOX[window][1] * WINDOW_BOX[window][3])]

    def k(self, m, t, h, window):
        rows, g = self.rows_of(h)
        if self.kind == "causal":
            return self.w.K[rows, g, m * TOKENS:m * TOKENS + self.width(t)]
        if self.kind == "full":
            return self.w.K[rows, g, m, :]
        return self.w.K[rows, g, m, window * WN:(window + 1) * WN]

    def v(self, m, h, c, window):
        if self.kind == "windows":
            return self.w.V[0:98, m * 8 + window * 2 + c, h, :]
        return self.w.V[:, m * 2 + c, h * self.w.kv_heads // HEADS, :]


def attend(nc, env, w, kind):
    R, banks, ident = env.R, env.banks, env.ident
    lay = Layout(kind, w)
    HP = HEADS // 2
    units = [(m, t, hp) for m in range(PAIR) for t in range(lay.tiles) for hp in range(HP)]
    U = len(units)
    ck = lay.chunk()
    with stage(nc, env.names) as (block, sem):
        scores_ready, max_ready, exp_ready = sem("scores_ready"), sem("max_ready"), sem("exp_ready")
        turned, copied, pv_done = sem("turned"), sem("copied"), sem("pv_done")
        normed, o_turned, OT_ready = sem("normed"), sem("o_turned"), sem("OT_ready")
        O_out, om_turned = sem("O_out"), sem("om_turned")
        projected, added, steps = sem("projected"), sem("added"), sem("steps")

        def ends_tile(u):
            return u // HP if 0 <= u < U and u % HP == HP - 1 else None

        def ends_image(u):
            return u // (HP * lay.tiles) if 0 <= u < U and (u + 1) % (HP * lay.tiles) == 0 else None

        def S(u):
            return banks[:, u % 3, :].rearrange("p (h k) -> p h k", h=2)

        def PTb(u):
            return banks[:, 3 + u % 2, :].rearrange("p (s q) -> p s q", q=P)

        def O(tile):
            return banks[:, 5 + tile % 2, 0:3 * P].rearrange("p (g q) -> p g q", q=P)

        OM = banks[:, 7, 0:3 * P].rearrange("p (h d) -> p h d", d=32)

        @block.tensor
        def _(pe):
            for s in range(U + 9):
                if s < U:
                    m, t, hp = units[s]
                    if s >= 3:
                        pe.wait_ge(exp_ready, s - 2)
                    for hh, h in enumerate(lay.heads(hp)):
                        for r0, rn, win in lay.parts(t):
                            ins = nc.tensor.matmul(S(s)[r0:r0 + rn, hh, 0:lay.width(t)], lay.q(m, t, h, win),
                                                   lay.k(m, t, h, win), start=True, stop=(kind != "causal"),
                                                   skip_group_check=(kind == "causal"))
                        if kind == "causal":
                            ins = nc.tensor.matmul(S(s)[:, hh, t * P:(t + 1) * P], env.ident16[:, :], env.mask16[:, :],
                                                   start=False, stop=True, skip_group_check=True)
                    ins.then_inc(scores_ready, 1)
                u = s - 2
                if 0 <= u < U:
                    m, t, hp = units[u]
                    rows = lay.rows(t)
                    pe.wait_ge(exp_ready, u + 1)
                    if u >= 2:
                        pe.wait_ge(copied, u - 1)
                    for hh in range(2):
                        for c in range(lay.chunks(t)):
                            ins = nc.tensor.transpose(PTb(u)[0:ck, hh * lay.chunks(t) + c, 0:rows],
                                                      w.Pr[0:rows, u % 3, hh, c * ck:(c + 1) * ck], ident[0:rows, 0:rows])
                    ins.then_inc(turned, 1)
                u = s - 3
                if 0 <= u < U:
                    m, t, hp = units[u]
                    tile = u // HP
                    pe.wait_ge(copied, u + 1)
                    if hp == 0 and tile >= 2:
                        pe.wait_ge(O_out, tile - 1)
                    for hh, h in enumerate(lay.heads(hp)):
                        for r0, rn, win in lay.parts(t):
                            for c in range(lay.chunks(t)):
                                ins = nc.tensor.matmul(O(tile)[32 * (h % 4):32 * (h % 4) + VW, h // 4, r0:r0 + rn],
                                                       lay.v(m, h, c, win),
                                                       w.PT[0:ck, u % 2, hh * lay.chunks(t) + c, r0:r0 + rn],
                                                       start=(c == 0), stop=(c == lay.chunks(t) - 1))
                    ins.then_inc(pv_done, 1)
                tile = ends_tile(s - 5)
                if tile is not None:
                    m, t, _ = units[s - 5]
                    rows = lay.rows(t)
                    pe.wait_ge(O_out, tile + 1)
                    if tile >= 1:
                        pe.wait_ge(OT_ready, tile)
                    if m >= 1:
                        pe.wait_ge(added, m)
                    for g in range(3):
                        ins = nc.tensor.transpose(banks[0:rows, 7, g * P:(g + 1) * P], w.Os[:, tile % 2, g, 0:rows],
                                                  ident[:, :])
                    ins.then_inc(om_turned, 1)
                tile = ends_tile(s - 7)
                if tile is not None:
                    m, t, _ = units[s - 7]
                    rows = lay.rows(t)
                    pe.wait_ge(normed, tile + 1)
                    for c in range(2):
                        ins = nc.tensor.transpose(banks[0:CH, 7, c * P:c * P + rows],
                                                  w.On[0:rows, tile % 2, c * CH:(c + 1) * CH], ident[0:rows, 0:rows])
                    ins.then_inc(o_turned, 1)
                m = ends_image(s - 8)
                if m is not None:
                    pe.wait_ge(OT_ready, lay.tiles * (m + 1))
                    for t in range(2):
                        cols = slice(m * TOKENS + t * P, m * TOKENS + (t + 1) * P)
                        ins = dense(nc, banks[:, 7, t * C:(t + 1) * C], lambda k, r: w.OT[0:r, k, cols],
                                    lambda k, r: w.wo[0:r, k, :], w.out_rows)
                    ins.then_inc(projected, 1)

        @block.scalar
        def _(act):
            for s in range(U + 9):
                if s < U:
                    _, t, _ = units[s]
                    rows = lay.rows(t)
                    act.wait_ge(max_ready, s + 1)
                    if s >= 3:
                        act.wait_ge(turned, s - 2)
                    for hh in range(2):
                        ins = nc.scalar.activation(w.Pr[0:rows, s % 3, hh, 0:lay.width(t)],
                                                   S(s)[0:rows, hh, 0:lay.width(t)], ACT.Exp,
                                                   bias=w.nmax[0:rows, s % 4, hh:hh + 1])
                    ins.then_inc(exp_ready, 1)
                tile = ends_tile(s - 4)
                if tile is not None:
                    _, t, _ = units[s - 4]
                    rows = lay.rows(t)
                    act.wait_ge(pv_done, s - 4 + 1)
                    if tile >= 2:
                        act.wait_ge(om_turned, tile - 1)
                    nc.scalar.activation(w.Os[:, tile % 2, :, 0:rows], O(tile)[:, :, 0:rows], ACT.Copy).then_inc(O_out, 1)
                tile = ends_tile(s - 7)
                if tile is not None:
                    m, t, _ = units[s - 7]
                    act.wait_ge(o_turned, tile + 1)
                    for r0, rn, win in lay.parts(t):
                        for c in range(2):
                            src = banks[0:CH, 7, c * P + r0:c * P + r0 + rn]
                            dst = lay.tokens(w.OT[0:CH, c, :], m, t, win)
                            if kind == "windows":
                                src = src.rearrange("p (a b) -> p a b", b=WINDOW_BOX[win][3])
                            ins = nc.scalar.activation(dst, src, ACT.Copy)
                    ins.then_inc(OT_ready, 1)

        @block.vector
        def _(dve):
            chain = Chain(dve, steps)
            for s in range(U + 9):
                if s < U:
                    _, t, _ = units[s]
                    rows = lay.rows(t)
                    dve.wait_ge(scores_ready, s + 1)
                    if s >= 4:
                        dve.wait_ge(exp_ready, s - 3)
                    nc.vector.tensor_reduce(w.nmax[0:rows, s % 4, :], S(s)[0:rows, :, 0:lay.width(t)], AX.X, ALU.max,
                                            negate=True).then_inc(max_ready, 1)
                u = s - 2
                if 0 <= u < U:
                    _, t, _ = units[u]
                    rows, n = lay.rows(t), 2 * lay.chunks(t)
                    dve.wait_ge(turned, u + 1)
                    if u >= 2:
                        dve.wait_ge(pv_done, u - 1)
                    nc.vector.tensor_copy(w.PT[0:ck, u % 2, 0:n, 0:rows], PTb(u)[0:ck, 0:n, 0:rows]).then_inc(copied, 1)
                tile = ends_tile(s - 6)
                if tile is not None:
                    _, t, _ = units[s - 6]
                    rows = lay.rows(t)
                    dve.wait_ge(om_turned, tile + 1)
                    if tile >= 2:
                        dve.wait_ge(o_turned, tile - 1)
                    chain(nc.vector.reciprocal(w.rsum[0:rows, tile % 2, :], OM[0:rows, :, HD]))
                    nc.vector.tensor_tensor(w.On[0:rows, tile % 2, :].rearrange("p (h d) -> p h d", d=HD),
                                            OM[0:rows, :, 0:HD],
                                            w.rsum[0:rows, tile % 2, :, None].to_broadcast([rows, HEADS, HD]),
                                            ALU.mult).then_inc(normed, 1)
                m = ends_image(s - 9)
                if m is not None:
                    dve.wait_ge(projected, m + 1)
                    r = R[:, 2 * m:2 * m + 2, :]
                    nc.vector.tensor_tensor(r, r, banks[:, 7, 0:2 * C].rearrange("p (t c) -> p t c", c=C),
                                            ALU.add).then_inc(added, 1)
            dve.wait_ge(added, PAIR)


def store_residual(nc, chain, env, ip, add):
    x = env.X[:, bass.ds(ip * PT, PT), :]
    if add:
        chain(nc.vector.tensor_tensor(x, x, env.R[:, :, :], ALU.add))
    else:
        chain(nc.vector.tensor_copy(x, env.R[:, :, :]))


def causal_project(nc, env, w, ip, base_ln, inner_rms, rope):
    R, xn, banks, ident = env.R, env.xn, env.banks, env.ident
    NKV = w.kv_heads
    NQK = HEADS + NKV
    with stage(nc, env.names) as (block, sem):
        steps = sem("steps")
        normed, turned, xT_ready = sem("normed"), sem("turned"), sem("xT_ready")
        qk_done, v_done, v_out = sem("qk_done"), sem("v_done"), sem("v_out")
        spread, qk_turned, qk_out = sem("spread"), sem("qk_turned"), sem("qk_out")

        @block.vector
        def _(dve):
            chain = Chain(dve, steps)
            chain(nc.vector.tensor_copy(R[:, :, :], env.X[:, bass.ds(ip * PT, PT), :]))
            normalise(nc, chain, env.s, xn, R, 1e-5, True)
            if base_ln:
                chain(nc.vector.tensor_copy(R[:, :, :], xn[:, :, :]))
            if inner_rms is not None:
                normalise(nc, chain, env.s, xn, R, inner_rms, False)
            dve.sem_inc(normed, 1)
            for t in range(PT):
                dve.wait_ge(qk_done, t + 1)
                ps = banks[:, t, 0:NQK * HD].rearrange("p (h d) -> p h d", d=HD)
                if t >= 2:
                    dve.wait_ge(qk_turned, t - 1)
                qs, ks = w.spread[:, t % 2, 0], w.spread[:, t % 2, 1]
                if rope:
                    cos = w.cos[:, t % 2, None, :].to_broadcast([P, NQK, HD])
                    sin = w.sin[:, t % 2, None, :].to_broadcast([P, NQK, HD])
                    chain.free(nc.vector.tensor_tensor(w.ra[:, :, :], ps, cos, ALU.mult))
                    chain.free(nc.vector.tensor_tensor(w.rb[:, :, 0::2], ps[:, :, 1::2], sin[:, :, 0::2], ALU.mult))
                    chain.free(nc.vector.tensor_tensor(w.rb[:, :, 1::2], ps[:, :, 0::2], sin[:, :, 1::2], ALU.mult))
                    chain.wait()
                    chain.free(nc.vector.tensor_tensor(qs[:, :, 0:HD], w.ra[:, 0:HEADS, :], w.rb[:, 0:HEADS, :], ALU.add))
                    if NKV == HEADS:
                        chain.free(nc.vector.tensor_tensor(ks[:, :, 0:HD], w.ra[:, HEADS:, :], w.rb[:, HEADS:, :], ALU.add))
                    else:
                        rep = HEADS // NKV
                        for j in range(rep):
                            chain.free(nc.vector.tensor_tensor(ks[:, j::rep, 0:HD], w.ra[:, HEADS:, :], w.rb[:, HEADS:, :],
                                                               ALU.add))
                else:
                    chain.free(nc.vector.tensor_copy(qs[:, :, 0:HD], ps[:, 0:HEADS, :]))
                    chain.free(nc.vector.tensor_copy(ks[:, :, 0:HD], ps[:, HEADS:, :]))
                chain.wait()
                dve.sem_inc(spread, 1)

        @block.scalar
        def _(act):
            for c in range(2):
                act.wait_ge(turned, c + 1)
                nc.scalar.activation(w.xT[0:CH, c, :], banks[0:CH, c, :], ACT.Copy if w.nw is None else ACT.Identity,
                                     scale=1.0 if w.nw is None else w.nw[:, c:c + 1]).then_inc(xT_ready, 1)
            for t in range(PT):
                act.wait_ge(v_done, t + 1)
                nc.scalar.activation(w.V[:, t, :, 0:HD],
                                     banks[:, 4 + t, 0:NKV * HD].rearrange("p (h d) -> p h d", d=HD), ACT.Copy).then_inc(v_out, 1)
            for t in range(PT):
                act.wait_ge(qk_turned, t + 1)
                nc.scalar.activation(w.Q[:, :, t * P:(t + 1) * P], banks[0:CH, t, :].rearrange("p (g q) -> p g q", g=4),
                                     ACT.Copy, scale=QSCALE)
                nc.scalar.activation(w.K[:, :, t * P:(t + 1) * P], banks[0:CH, 4 + t, :].rearrange("p (g q) -> p g q", g=4),
                                     ACT.Copy).then_inc(qk_out, 1)
            act.wait_ge(qk_out, PT)

        @block.tensor
        def _(pe):
            pe.wait_ge(normed, 1)
            turn_tiles(nc, banks, xn, ident, turned)
            pe.wait_ge(xT_ready, 2)
            for t in range(PT):
                x = lambda k, r: w.xT[0:r, k, t * P:(t + 1) * P]
                dense(nc, banks[:, t, 0:NQK * HD], x, lambda k, r: w.wqkv[0:r, k, 0:NQK * HD],
                      w.in_rows).then_inc(qk_done, 1)
                dense(nc, banks[:, 4 + t, 0:NKV * HD], x, lambda k, r: w.wqkv[0:r, k, NQK * HD:],
                      w.in_rows).then_inc(v_done, 1)
            for t in range(PT):
                pe.wait_ge(spread, t + 1)
                pe.wait_ge(v_out, t + 1)
                for g in range(4):
                    for n in range(2):
                        ins = nc.tensor.transpose(banks[0:CH, 4 * n + t, g * P:(g + 1) * P],
                                                  w.spread[:, t % 2, n, 3 * g:3 * g + 3, :].rearrange("p h d -> p (h d)"),
                                                  ident[:, :])
                ins.then_inc(qk_turned, 1)


def causal_setup(nc, env, w):
    with stage(nc, env.names) as (block, sem):
        loaded, filled = sem("loaded"), sem("filled")

        @block.sync
        def _(sp):
            for dst, src in w.loads:
                sp.dma_start(dst, src).then_inc(loaded, 16)
            sp.wait_ge(loaded, 16 * len(w.loads))

        @block.gpsimd
        def _(pool):
            chain = Chain(pool, filled)
            chain(nc.gpsimd.memset(w.V[:, :, :, HD:VW], 1.0))
            chain(nc.gpsimd.memset(w.xT[CH:CH + 1, 1, :], 1.0))
            chain(nc.gpsimd.memset(w.OT[CH:CH + 1, 1, :], 1.0))
            chain(nc.gpsimd.memset(w.spread[:, :, :, :, HD:], 0.0))


def feed_forward(nc, env, w, ip, gated):
    R, xn, banks, ident = env.R, env.xn, env.banks, env.ident
    NF = FF // P
    with stage(nc, env.names) as (block, sem):
        steps = sem("steps")
        normed, turned, xT_ready = sem("normed"), sem("turned"), sem("xT_ready")
        up_done, act_done, h_ready, out_done = sem("up_done"), sem("act_done"), sem("h_ready"), sem("out_done")

        @block.vector
        def _(dve):
            chain = Chain(dve, steps)
            normalise(nc, chain, env.s, xn, R, 1e-5, not gated)
            dve.sem_inc(normed, 1)
            if gated:
                for f in range(NF):
                    dve.wait_ge(act_done, f + 1)
                    nc.vector.tensor_tensor(w.hT[:, f, :], w.sg[:, f % 2, :], banks[:, 2 + f % 2, :],
                                            ALU.mult).then_inc(h_ready, 1)
            for t in range(PT):
                dve.wait_ge(out_done, t + 1)
                chain.free(nc.vector.tensor_tensor(R[:, t, :], R[:, t, :], banks[:, 4 + t, 0:C], ALU.add))
            chain.wait()
            store_residual(nc, chain, env, ip, gated)

        @block.scalar
        def _(act):
            for c in range(2):
                act.wait_ge(turned, c + 1)
                nc.scalar.activation(w.xT[0:CH, c, :], banks[0:CH, c, :], ACT.Identity, scale=w.fnw[:, c:c + 1],
                                     bias=0.0 if gated else w.fnb[:, c:c + 1]).then_inc(xT_ready, 1)
            for f in range(NF):
                act.wait_ge(up_done, f + 1)
                if gated:
                    if f >= 2:
                        act.wait_ge(h_ready, f - 1)
                    nc.scalar.activation(w.sg[:, f % 2, :], banks[:, f % 2, :], ACT.Silu).then_inc(act_done, 1)
                else:
                    nc.scalar.activation(w.hT[:, f, :], banks[:, f % 4, :], ACT.Gelu).then_inc(h_ready, 1)

        @block.tensor
        def _(pe):
            pe.wait_ge(normed, 1)
            turn_tiles(nc, banks, xn, ident, turned)
            pe.wait_ge(xT_ready, 2)
            for f in range(NF):
                slots = 2 if gated else 4
                if f >= slots:
                    pe.wait_ge(h_ready, f - slots + 1)
                x = lambda k, r: w.xT[0:r, k, :]
                if gated:
                    dense(nc, banks[:, f % 2, :], lambda k, r: w.w1[0:r, k, f * P:(f + 1) * P], x)
                    ins = dense(nc, banks[:, 2 + f % 2, :], lambda k, r: w.w3[0:r, k, f * P:(f + 1) * P], x)
                else:
                    ins = dense(nc, banks[:, f % 4, :], lambda k, r: w.w1[0:r, k, f * P:(f + 1) * P], x, BIASED)
                ins.then_inc(up_done, 1)
            pe.wait_ge(h_ready, NF)
            for t in range(PT):
                for f in range(NF):
                    ins = nc.tensor.matmul(banks[:, 4 + t, 0:C], w.hT[:, f, t * P:(t + 1) * P], w.w2[:, f, :],
                                           start=(f == 0), stop=(gated and f == NF - 1))
                if not gated:
                    ins = nc.tensor.matmul(banks[:, 4 + t, 0:C], env.ones[0:1, :], w.b2[0:1, :], start=False, stop=True)
                ins.then_inc(out_done, 1)


def route(nc, env, w, ip, first):
    R, xn, banks, ident, E = env.R, env.xn, env.banks, env.ident, w.experts
    with stage(nc, env.names) as (block, sem):
        steps = sem("steps")
        normed, turned, xT_ready = sem("normed"), sem("turned"), sem("xT_ready")
        logits_done, margin_ready, exp_done = sem("logits_done"), sem("margin_ready"), sem("exp_done")

        @block.vector
        def _(dve):
            chain = Chain(dve, steps)
            if first:
                store_residual(nc, chain, env, ip, True)
                normalise(nc, chain, env.s, xn, R, 1e-6, False)
            else:
                chain(nc.vector.tensor_copy(R[:, :, :], env.X[:, bass.ds(ip * PT, PT), :]))
                normalise(nc, chain, env.s, xn, R, 1e-5, True)
            dve.sem_inc(normed, 1)
            dve.wait_ge(logits_done, 1)
            chain(nc.vector.tensor_copy(w.logits[:, :, :], banks[:, 2, 0:PT * E].rearrange("p (t e) -> p t e", e=E)))
            for t in range(PT):
                chain.free(nc.vector.max(w.top[:, t, :], w.logits[:, t, :]))
            chain.wait()
            for t in range(PT):
                chain.free(nc.vector.max_index(w.topi[:, t, :], w.top[:, t, :], w.logits[:, t, :]))
            chain.wait()
            chain.free(nc.vector.tensor_copy(w.topf[:, :, :], w.topi[:, :, :]))
            chain.free(nc.vector.tensor_tensor(w.margin[:, :], w.top[:, :, 1], w.top[:, :, 0], ALU.subtract))
            chain.wait()
            dve.sem_inc(margin_ready, 1)
            dve.wait_ge(exp_done, 1)
            chain(nc.vector.tensor_scalar(w.g1[:, :], w.margin[:, :], 1.0, None, ALU.add))
            chain(nc.vector.reciprocal(w.g0[:, :], w.g1[:, :]))
            chain(nc.vector.tensor_tensor(w.g1[:, :], w.margin[:, :], w.g0[:, :], ALU.mult))
            for t in range(PT):
                chain.free(nc.vector.tensor_scalar(w.pick[:, t, :], env.iota[:, 0:E], w.topf[:, t, 1:2], w.g1[:, t:t + 1],
                                                   ALU.is_equal, ALU.mult))
                chain.free(nc.vector.tensor_scalar(w.pick0[:, t, :], env.iota[:, 0:E], w.topf[:, t, 0:1], w.g0[:, t:t + 1],
                                                   ALU.is_equal, ALU.mult))
            chain.wait()
            chain(nc.vector.tensor_tensor(w.comb[:, bass.ds(ip * PT, PT), 0:E], w.pick[:, :, :], w.pick0[:, :, :], ALU.add))

        @block.scalar
        def _(act):
            for c in range(2):
                act.wait_ge(turned, c + 1)
                nc.scalar.activation(w.xT[0:CH, c, :], banks[0:CH, c, :],
                                     ACT.Identity if first else ACT.Copy,
                                     scale=w.nw2[:, c:c + 1] if first else 1.0).then_inc(xT_ready, 1)
            act.wait_ge(xT_ready, 2)
            for c in range(2):
                nc.scalar.activation(w.mT[0:CH, c, bass.ds(ip * PN, PN)], w.xT[0:CH, c, :], ACT.Copy).then_inc(xT_ready, 1)
            act.wait_ge(margin_ready, 1)
            nc.scalar.activation(w.margin[:, :], w.margin[:, :], ACT.Exp).then_inc(exp_done, 1)
            act.wait_ge(xT_ready, 4)

        @block.tensor
        def _(pe):
            pe.wait_ge(normed, 1)
            turn_tiles(nc, banks, xn, ident, turned)
            pe.wait_ge(xT_ready, 2)
            for t in range(PT):
                ins = dense(nc, banks[:, 2, t * E:(t + 1) * E], lambda k, r: w.xT[0:r, k, t * P:(t + 1) * P],
                            lambda k, r: w.wr[0:r, k, :], w.r_rows)
            ins.then_inc(logits_done, 1)


def experts(nc, env, w):
    banks, E = env.banks, w.comb.shape[2]
    NF = EF // P
    HALF = IMAGES * TOKENS // BANK
    BLOCKS = 2 * HALF
    UNITS = BLOCKS * NF
    DOWNS = BLOCKS * 2
    pairs = E // 2
    with stage(nc, env.names) as (block, sem):
        w_loaded = [sem("w_loaded_a"), sem("w_loaded_b")]
        w_free = [sem("w_free_a"), sem("w_free_b")]
        gu_done, silu_done, h_done, sg_free = sem("gu_done"), sem("silu_done"), sem("h_done"), sem("sg_free")
        block_done, down_done, summed = sem("block_done"), sem("down_done"), sem("summed")

        @block.sync
        def _(sp):
            def load(i, b):
                sp.wait_ge(w_free[b], i + 1)
                e = i * 2 + b
                e = slice(e, e + 1) if isinstance(e, int) else bass.ds(e, 1)
                sp.dma_start(w.gu[:, b, :, :], w.gu_dram[e, :, :, :].rearrange("o p k n -> (o p) k n")).then_inc(w_loaded[b], 16)
                sp.dma_start(w.dn[:, b, :, :], w.dn_dram[e, :, :, :].rearrange("o p f n -> (o p) f n")).then_inc(w_loaded[b], 16)

            with sp.Fori(0, pairs) as i:
                for b in range(2):
                    load(i, b)
            if E % 2:
                load(pairs, 0)
            sp.wait_ge(w_loaded[0], 32 * (pairs + E % 2))
            sp.wait_ge(w_loaded[1], 32 * pairs)

        @block.tensor
        def _(pe):
            pe.sem_inc(w_free[0], 1)
            pe.sem_inc(w_free[1], 1)

            def up(i, blk):
                b, n = divmod(blk, HALF)
                if n == 0:
                    pe.wait_ge(w_loaded[b], i * 32 + 32)
                for f in range(NF):
                    u = blk * NF + f
                    pe.wait_ge(h_done, i * UNITS + u + 1)
                    for half in range(2):
                        ins = dense(nc, banks[:, 2 * half + u % 2, :],
                                    lambda k, r: w.gu[0:r, b, k, half * EF + f * P:half * EF + (f + 1) * P],
                                    lambda k, r: w.mT[0:r, k, n * BANK:(n + 1) * BANK])
                    ins.then_inc(gu_done, 1)

            def down(i, blk):
                b, n = divmod(blk, HALF)
                pe.wait_ge(h_done, i * UNITS + (blk + 1) * NF + 2)
                for j in range(2):
                    d = blk * 2 + j
                    pe.wait_ge(summed, i * DOWNS + d + 1)
                    for tt in range(2):
                        t = 2 * j + tt
                        for f in range(NF):
                            ins = nc.tensor.matmul(banks[:, 4 + d % 4, tt * C:(tt + 1) * C],
                                                   w.ehT[:, blk % 2, f, t * P:(t + 1) * P], w.dn[:, b, f, :],
                                                   start=(f == 0), stop=(f == NF - 1))
                    ins.then_inc(down_done, 1)
                if n == HALF - 1:
                    pe.wait_ge(down_done, i * DOWNS + (blk + 1) * 2)
                    pe.sem_inc(w_free[b], 1)

            with pe.Fori(0, pairs) as i:
                for blk in range(BLOCKS + 1):
                    if blk < BLOCKS:
                        up(i, blk)
                    if blk >= 1:
                        down(i, blk - 1)
            if E % 2:
                for blk in range(HALF + 1):
                    if blk < HALF:
                        up(pairs, blk)
                    if blk >= 1:
                        down(pairs, blk - 1)

        @block.scalar
        def _(act):
            def gate(i, u):
                act.wait_ge(gu_done, i * UNITS + u + 1)
                act.wait_ge(h_done, i * UNITS + u + 1)
                nc.scalar.activation(w.esg[:, u % 2, :], banks[:, u % 2, :], ACT.Silu).then_inc(silu_done, 1)

            with act.Fori(0, pairs) as i:
                for u in range(UNITS):
                    gate(i, u)
            if E % 2:
                for u in range(HALF * NF):
                    gate(pairs, u)

        @block.vector
        def _(dve):
            dve.sem_inc(h_done, 2)
            dve.sem_inc(summed, 4)

            def hidden(i, blk):
                for f in range(NF):
                    u = blk * NF + f
                    dve.wait_ge(silu_done, i * UNITS + u + 1)
                    nc.vector.tensor_tensor(w.ehT[:, blk % 2, f, :], w.esg[:, u % 2, :], banks[:, 2 + u % 2, :],
                                            ALU.mult).then_inc(h_done, 1)

            def add(i, blk):
                b, n = divmod(blk, HALF)
                expert = slice(i * 2 + b, i * 2 + b + 1) if isinstance(i, int) else bass.ds(i * 2 + b, 1)
                for j in range(2):
                    d = blk * 2 + j
                    dve.wait_ge(down_done, i * DOWNS + d + 1)
                    for tt in range(2):
                        t = n * 4 + 2 * j + tt
                        ins = nc.vector.scalar_tensor_tensor(
                            env.X[:, t, :], banks[:, 4 + d % 4, tt * C:(tt + 1) * C],
                            w.comb[:, t, expert], env.X[:, t, :], ALU.mult, ALU.add)
                    ins.then_inc(summed, 1)
                dve.wait_ge(summed, i * DOWNS + (blk + 1) * 2 + 4)

            with dve.Fori(0, pairs) as i:
                for blk in range(BLOCKS + 1):
                    if blk < BLOCKS:
                        hidden(i, blk)
                    if blk >= 1:
                        add(i, blk - 1)
            if E % 2:
                for blk in range(HALF + 1):
                    if blk < HALF:
                        hidden(pairs, blk)
                    if blk >= 1:
                        add(pairs, blk - 1)


class Env:
    pass


def build(nc, d, out):
    ctx = ExitStack()
    env = Env()
    env.names = {}

    def allocator(stack):
        def sb(name, shape, dt=F32):
            return stack.enter_context(nc.sbuf_tensor(unique(env.names, name), shape, dt))
        return sb

    with ctx:
        sb = allocator(ctx)
        env.banks = ctx.enter_context(nc.psum_tensor("banks", [P, 8, BANK], F32))
        env.X, env.R, env.xn = sb("X", [P, TILES, C]), sb("R", [P, PT, C]), sb("xn", [P, PT, C])
        env.ident, env.mask = sb("ident", [P, P]), sb("mask", [P, P])
        env.ident16, env.mask16 = sb("ident16", [P, P], BF16), sb("mask16", [P, P], BF16)
        env.ones, env.iota = sb("ones", [1, P]), sb("iota", [P, 16])
        env.s = Scratch(sb)

        with stage(nc, env.names) as (block, sem):
            loaded, cast, cleared = sem("loaded"), sem("cast"), sem("cleared")

            @block.sync
            def _(sp):
                for dst, src in ((env.X[:], d["x"]), (env.ident[:], d["ident"]), (env.mask[:], d["mask"]),
                                 (env.iota[:], d["iota"])):
                    sp.dma_start(dst, src).then_inc(loaded, 16)
                sp.wait_ge(loaded, 64)

            @block.vector
            def _(dve):
                nc.vector.memset(env.banks[:, :, :].rearrange("p a b -> p (a b)"), 0.0).then_inc(cleared, 1)
                nc.vector.memset(env.ones[:, :], 1.0).then_inc(cleared, 1)
                dve.wait_ge(loaded, 64)
                nc.vector.tensor_copy(env.ident16[:, :], env.ident[:, :]).then_inc(cast, 1)
                nc.vector.tensor_copy(env.mask16[:, :], env.mask[:, :]).then_inc(cast, 1)
                dve.wait_ge(cast, 2)
                dve.wait_ge(cleared, 2)

        def attention_buffers(w, sb):
            w.Pr, w.PT = sb("Pr", [P, 3, 2, TOKENS]), sb("PT", [P, 2, 4, P])
            w.nmax, w.rsum = sb("nmax", [P, 4, 2]), sb("rsum", [P, 2, HEADS])
            w.Os = sb("Os", [P, 2, 3, P])
            w.On, w.OT, w.xT = sb("On", [P, 2, C]), sb("OT", [CH + 1, 2, PN]), sb("xT", [CH + 1, 2, PN])

        def loader(w, sb):
            w.loads = []

            def load(name, shape, key):
                t = sb(name, shape)
                w.loads.append((t[:], d[key]))
                return t
            return load

        for layer, windows in (("L0", True), ("L1", False)):
            with ExitStack() as stack:
                sb, w = allocator(stack), Env()
                attention_buffers(w, sb)
                load = loader(w, sb)
                w.wq, w.wk = load("wq", [CH + 1, 2, C], layer + "_wq"), load("wk", [CH + 1, 2, 6 * P], layer + "_wk")
                w.wv, w.wo = load("wv", [CH + 1, 2, C], layer + "_wv"), load("wo", [CH + 1, 2, C], layer + "_wo")
                w.hot = load("hot", [P, WINDOWS * WN if windows else TOKENS], layer + "_hot")
                w.qslot, w.odd = load("qslot", [CH, 2, HD], "qslot"), load("odd", [CH, 2], "odd")
                w.bd, w.qT = sb("bd", [CH, 2, SIDE, 2, 32]), sb("qT", [CH, 2, PN])
                w.Q = sb("Q", [P, 6, PN])
                w.in_rows = w.out_rows = BIASED
                w.kv_heads = HEADS
                if windows:
                    w.win = load("win", [CH, 2, SIDE, 16], layer + "_win")
                    w.kpad = load("kpad", [P, 6], layer + "_kpad")
                    w.nw, w.nb = load("nw", [CH, 2], "L0_ln1_w"), load("nb", [CH, 2], "L0_ln1_b")
                    w.fnw, w.fnb = load("fnw", [CH, 2], "L0_ln2_w"), load("fnb", [CH, 2], "L0_ln2_b")
                    w.w1, w.w2 = load("w1", [CH + 1, 2, FF], "L0_w1"), load("w2", [P, FF // P, C], "L0_w2")
                    w.b2 = load("b2", [1, C], "L0_b2")
                    w.K, w.V = sb("K", [P, 6, PAIR, WINDOWS * WN]), sb("V", [98, 8 * PAIR, HEADS, VW])
                    w.xw, w.hT = sb("xw", [CH + 1, 2, PAIR, WINDOWS * WN]), sb("hT", [P, FF // P, PN])
                else:
                    w.win = sb("win", [CH, 2, SIDE, 16])
                    w.rel, w.shrink = load("rel", [63, 2, CH], "L1_rel"), load("shrink", [63, TOKENS], "shrink")
                    w.gavg = load("gavg", [CH, CH], "gavg")
                    w.K, w.V = sb("K", [P, 6, PAIR, TOKENS]), sb("V", [P, PT, HEADS, VW])
                    w.gst, w.gmv = sb("gst", [CH, 4, 6]), sb("gmv", [CH, 4, 2])
                    w.ga, w.gv, w.gscale, w.gbias = (sb(n, [CH, 4]) for n in ("ga", "gv", "gscale", "gbias"))
                relative_setup(nc, env, w, windows)
                with nc.Fori(0, IMAGES // PAIR) as ip:
                    relative_project(nc, env, w, ip, windows)
                    attend(nc, env, w, "windows" if windows else "full")
                    if windows:
                        feed_forward(nc, env, w, ip, False)
                    else:
                        with stage(nc, env.names) as (block, sem):
                            steps = sem("steps")

                            @block.vector
                            def _(dve):
                                store_residual(nc, Chain(dve, steps), env, ip, False)

        for layer in ("L2a", "L2f", "L3a"):
            with ExitStack() as stack:
                sb, w = allocator(stack), Env()
                attention_buffers(w, sb)
                load = loader(w, sb)
                w.kv_heads = 3 if layer == "L2f" else HEADS
                nqkv = (HEADS + 2 * w.kv_heads) * HD
                w.wqkv, w.wo = load("wqkv", [CH + 1, 2, nqkv], layer + "_wqkv"), load("wo", [CH + 1, 2, C], layer + "_wo")
                w.in_rows = w.out_rows = BIASED if layer == "L2a" else (CH, CH)
                w.Q, w.K = sb("Q", [CH, 4, PN]), sb("K", [CH, 4, PN])
                w.V, w.spread = sb("V", [P, PT, w.kv_heads, VW]), sb("spread", [P, 2, 2, HEADS, 32])
                w.nw = None
                if layer != "L2a":
                    w.nw = load("nw", [CH, 2], layer + "_norm1")
                    w.cos, w.sin = load("cos", [P, 2, HD], "cos"), load("sin", [P, 2, HD], "sin")
                    w.ra, w.rb = (sb(n, [P, HEADS + w.kv_heads, HD]) for n in ("ra", "rb"))
                if layer == "L3a":
                    w.fnw = load("fnw", [CH, 2], "L3a_norm2")
                    w.w1, w.w3 = load("w1", [CH + 1, 2, FF], "L3a_w1"), load("w3", [CH + 1, 2, FF], "L3a_w3")
                    w.w2 = load("w2", [P, FF // P, C], "L3a_w2")
                    w.hT, w.sg = sb("hT", [P, FF // P, PN]), sb("sg", [P, 2, PN])
                if layer == "L2f":
                    expert_buffers(w, sb, load, d, layer, 16)
                causal_setup(nc, env, w)
                with nc.Fori(0, IMAGES // PAIR) as ip:
                    causal_project(nc, env, w, ip, layer != "L2a", {"L2a": None, "L2f": 1e-6, "L3a": 1e-5}[layer],
                                   layer != "L2a")
                    attend(nc, env, w, "causal")
                    if layer == "L2a":
                        with stage(nc, env.names) as (block, sem):
                            steps = sem("steps")

                            @block.vector
                            def _(dve):
                                store_residual(nc, Chain(dve, steps), env, ip, False)
                    elif layer == "L2f":
                        route(nc, env, w, ip, True)
                    else:
                        feed_forward(nc, env, w, ip, True)
                if layer == "L2f":
                    experts(nc, env, w)

        with ExitStack() as stack:
            sb, w = allocator(stack), Env()
            load = loader(w, sb)
            w.xT = sb("xT", [CH + 1, 2, PN])
            expert_buffers(w, sb, load, d, "L3f", 8)
            with stage(nc, env.names) as (block, sem):
                loaded, filled = sem("loaded"), sem("filled")

                @block.sync
                def _(sp):
                    for dst, src in w.loads:
                        sp.dma_start(dst, src).then_inc(loaded, 16)
                    sp.wait_ge(loaded, 16 * len(w.loads))

                @block.gpsimd
                def _(pool):
                    chain = Chain(pool, filled)
                    chain(nc.gpsimd.memset(w.xT[CH:CH + 1, 1, :], 1.0))
                    chain(nc.gpsimd.memset(w.comb[:, :, w.experts:], 1.0))
            with nc.Fori(0, IMAGES // PAIR) as ip:
                route(nc, env, w, ip, False)
            experts(nc, env, w)

        with stage(nc, env.names) as (block, sem):
            written = sem("written")

            @block.sync
            def _(sp):
                sp.dma_start(out, env.X[:]).then_inc(written, 16)
                sp.wait_ge(written, 16)


def expert_buffers(w, sb, load, d, layer, n):
    w.experts = n
    w.wr = load("wr", [CH + 1, 2, n], layer + "_wr")
    w.r_rows = (CH, CH) if layer == "L2f" else BIASED
    if layer == "L2f":
        w.nw2 = load("nw2", [CH, 2], layer + "_norm2")
    w.logits, w.pick, w.pick0 = (sb(x, [P, PT, n]) for x in ("logits", "pick", "pick0"))
    w.comb = sb("comb", [P, TILES, d[layer + "_gu"].shape[0]])
    w.top, w.topf, w.topi = sb("top", [P, PT, 8]), sb("topf", [P, PT, 8]), sb("topi", [P, PT, 8], U32)
    w.margin, w.g0, w.g1 = (sb(x, [P, PT]) for x in ("margin", "g0", "g1"))
    w.mT = sb("mT", [CH, 2, IMAGES * TOKENS])
    w.gu, w.dn = sb("gu", [CH, 2, 2, 2 * EF]), sb("dn", [P, 2, EF // P, C])
    w.gu_dram, w.dn_dram = d[layer + "_gu"], d[layer + "_dn"]
    w.esg, w.ehT = sb("esg", [P, 2, BANK]), sb("ehT", [P, 2, EF // P, BANK])


def _chunked(np, w, b=None):
    a = np.zeros((CH + 1, 2, w.shape[1]), np.float32)
    a[0:CH] = w.reshape(2, CH, -1).transpose(1, 0, 2)
    if b is not None:
        a[CH, 1] = b
    return a


def _columns(v):
    return v.reshape(2, CH).T


def _padded_keys(np, a):
    out = np.zeros(a.shape[:-1] + (6, 2, 4, HD), np.float32)
    out[..., 1, :] = a.reshape(a.shape[:-1] + (6, 2, HD))
    return out.reshape(a.shape[:-1] + (6 * P,))


def _one_hot_rows(np, positions):
    hot = np.zeros((2, 64, len(positions)), np.float32)
    for j, (r, c) in enumerate(positions):
        hot[:, r, j] = 1
        hot[:, 32 + c, j] = 1
    return hot.reshape(P, -1)


def _shrink(np, n_in, n_out):
    inv = np.float32(n_in) / np.float32(n_out)
    at = (np.arange(n_out, dtype=np.float32) + np.float32(0.5)) * inv - np.float32(0.5)
    x = np.abs(at[None, :] - np.arange(n_in, dtype=np.float32)[:, None]) / max(inv, np.float32(1))
    w = np.maximum(0, 1 - x)
    return (w / w.sum(0, keepdims=True)).astype(np.float32)


def _constants(np):
    c = {}
    c["ident"] = np.eye(P, dtype=np.float32)
    c["mask"] = np.triu(np.full((P, P), -1e30, np.float32), 1)
    c["iota"] = np.tile(np.arange(16, dtype=np.float32), (P, 1))
    qslot = np.zeros((6, HD, 2, HD), np.float32)
    for h in range(6):
        qslot[h, :, h % 2, :] = QSCALE * np.eye(HD)
    c["qslot"] = qslot.reshape(CH, 2, HD)
    odd = np.zeros((6, HD, 2), np.float32)
    for h in range(6):
        odd[h, :, h % 2] = 1
    c["odd"] = odd.reshape(CH, 2)
    c["gavg"] = np.kron(np.eye(16), np.full((6, 6), 1 / 6)).astype(np.float32)
    window = [(r, k) for r in range(WS) for k in range(WS)]
    c["L0_hot"] = _one_hot_rows(np, window * WINDOWS)
    c["L1_hot"] = _one_hot_rows(np, [(r, k) for r in range(SIDE) for k in range(SIDE)])
    at = np.arange(SIDE)[:, None] - np.arange(SIDE)[None, :] + SIDE - 1
    c["shrink"] = _shrink(np, 63, 2 * SIDE - 1)[:, at.reshape(-1)]
    inv = (1.0 / 10000.0 ** (np.arange(0, HD, 2, dtype=np.float32) / HD)).astype(np.float32)
    ang = np.arange(TOKENS, dtype=np.float32)[:, None] * inv[None, :]
    cos, sin = np.cos(ang), np.sin(ang)
    cos = np.stack([cos, cos], -1).reshape(2, P, HD).transpose(1, 0, 2)
    sin = np.stack([-sin, sin], -1).reshape(2, P, HD).transpose(1, 0, 2)
    c["cos"], c["sin"] = cos.astype(np.float32), sin.astype(np.float32)
    return c


def _lay_out(np, i):
    a = _constants(np)
    a["x"] = i["x"].reshape(-1, C)
    for layer, p, names in (("L0", "L0_conv_", ("qkv_w", "qkv_b", "proj_w", "proj_b")),
                            ("L1", "L1_conv_", ("w_qkv", "b_qkv", "w_proj", "b_proj"))):
        w, b, wo, bo = (i[p + n] for n in names)
        a[layer + "_wq"] = _chunked(np, w[:, 0:C], b[0:C])
        a[layer + "_wk"] = _chunked(np, _padded_keys(np, w[:, C:2 * C]), _padded_keys(np, b[C:2 * C]))
        a[layer + "_wv"] = _chunked(np, w[:, 2 * C:], b[2 * C:])
        a[layer + "_wo"] = _chunked(np, wo, bo)
    a["L0_kpad"] = _padded_keys(np, i["L0_conv_qkv_b"][C:2 * C]).reshape(6, P).T
    row = np.arange(SIDE) % WS
    at = row[:, None] - np.arange(WS)[None, :] + WS - 1
    win = np.zeros((6, HD, 2, SIDE, 16), np.float32)
    for n, rel in enumerate((i["L0_conv_rel_pos_h"], i["L0_conv_rel_pos_w"])):
        win[:, :, n, :, 0:WS] = rel[at].transpose(2, 0, 1)[None]
    a["L0_win"] = win.reshape(CH, 2, SIDE, 16)
    a["L1_rel"] = np.stack([np.tile(i["L1_conv_rel_pos_" + n], (1, 6)) for n in "hw"], 1)
    for n in ("ln1_w", "ln1_b", "ln2_w", "ln2_b"):
        a["L0_" + n] = _columns(i["L0_conv_" + n])
    a["L0_w1"] = _chunked(np, i["L0_conv_fc1_w"], i["L0_conv_fc1_b"])
    a["L0_w2"] = i["L0_conv_fc2_w"].reshape(FF // P, P, C).transpose(1, 0, 2)
    a["L0_b2"] = i["L0_conv_fc2_b"].reshape(1, C)
    a["L2a_wqkv"] = _chunked(np, np.concatenate([i["L2_attn_w" + n].T for n in "qkv"], 1),
                             np.concatenate([i["L2_attn_b" + n] for n in "qkv"]))
    a["L2a_wo"] = _chunked(np, i["L2_attn_wo"].T, i["L2_attn_bo"])
    a["L2f_wqkv"] = _chunked(np, i["L2_ffn_w_qkv"])
    a["L2f_wo"] = _chunked(np, i["L2_ffn_w_out"])
    a["L2f_norm1"], a["L2f_norm2"] = _columns(i["L2_ffn_norm1_w"]), _columns(i["L2_ffn_norm2_w"])
    a["L2f_wr"] = _chunked(np, i["L2_ffn_w_router"])
    a["L2f_gu"] = i["L2_ffn_w_gate_up"].reshape(16, 2, CH, 2 * EF).transpose(0, 2, 1, 3)
    a["L2f_dn"] = i["L2_ffn_w_down"].reshape(16, EF // P, P, C).transpose(0, 2, 1, 3)
    a["L3a_wqkv"] = _chunked(np, np.concatenate([i["L3_attn_w_" + n].T for n in "qkv"], 1))
    a["L3a_wo"] = _chunked(np, i["L3_attn_w_o"].T)
    a["L3a_norm1"], a["L3a_norm2"] = _columns(i["L3_attn_w_ln1"]), _columns(i["L3_attn_w_ln2"])
    a["L3a_w1"], a["L3a_w3"] = _chunked(np, i["L3_attn_w_ffn_w1"].T), _chunked(np, i["L3_attn_w_ffn_w3"].T)
    a["L3a_w2"] = i["L3_attn_w_ffn_w2"].T.reshape(FF // P, P, C).transpose(1, 0, 2)
    a["L3f_wr"] = _chunked(np, i["L3_ffn_W_router"], i["L3_ffn_expert_bias"])
    gate = np.concatenate([i["L3_ffn_Wg_r"], i["L3_ffn_Wg_s"]], 0)
    up = np.concatenate([i["L3_ffn_Wu_r"], i["L3_ffn_Wu_s"]], 0)
    down = np.concatenate([i["L3_ffn_Wd_r"], i["L3_ffn_Wd_s"]], 0)
    a["L3f_gu"] = np.concatenate([gate, up], 2).reshape(9, 2, CH, 2 * EF).transpose(0, 2, 1, 3)
    a["L3f_dn"] = down.reshape(9, EF // P, P, C).transpose(0, 2, 1, 3)
    return {k: np.ascontiguousarray(v) for k, v in a.items()}


def kernel(**inputs):
    import numpy as np
    import concourse.bacc as bacc
    from concourse.bass_utils import run_bass_kernel_spmd as run

    nc = bacc.Bacc("TRN2", target_bir_lowering=False, num_devices=1)
    arrays = _lay_out(np, {k: np.asarray(v) for k, v in inputs.items()})
    dram = {k: nc.dram_tensor("in_" + k, v.shape, F32, kind="ExternalInput").ap() for k, v in arrays.items()}
    dram["x"] = dram["x"].rearrange("(t p) c -> p t c", p=P)
    out = nc.dram_tensor("out", (IMAGES * TOKENS, C), F32, kind="ExternalOutput").ap()
    build(nc, dram, out.rearrange("(t p) c -> p t c", p=P))
    r = run(nc, [{"in_" + k: v for k, v in arrays.items()}], core_ids=[0])
    return r.results[0]["out"].reshape(IMAGES, SIDE, SIDE, C)
```

```python
from contextlib import ExitStack, contextmanager

import concourse.bass as bass
from concourse import mybir

F32 = mybir.dt.float32
BF16 = mybir.dt.bfloat16
I32 = mybir.dt.int32
U32 = mybir.dt.uint32
ALU = mybir.AluOpType
ACT = mybir.ActivationFunctionType
AX = mybir.AxisListType

IMAGES, SIDE, C = 4, 16, 192
TOKENS = SIDE * SIDE
P = 128
TILES = IMAGES * TOKENS // P
PAIR = 2
PT = PAIR * TOKENS // P
PN = PAIR * TOKENS
HEADS, HD = 12, 16
CH = C // 2
VW = HD + 1
WS = 14
WN = WS * WS
WINDOWS = 4
QSCALE = HD ** -0.5
FF = 768
EF = 384
BANK = 512
RSQRT_SEED = 0x5F3759DF
PICKS = 2 * TILES
SORTED_TILES = {E: PICKS + E - 1 for E in (16, 8)}
SLOT_TILES = SORTED_TILES[16]
assert SLOT_TILES == SORTED_TILES[8] + TILES
SHARED_FIRST = TILES // 2
WINDOW_BOX = [(0, 14, 0, 14), (0, 14, 14, 2), (14, 2, 0, 14), (14, 2, 14, 2)]
WINDOW_AT = [0, 196, 224, 252]


class Chain:

    def __init__(self, eng, sem):
        self.eng, self.sem, self.n = eng, sem, 0

    def free(self, ins):
        self.n += 1
        ins.then_inc(self.sem, 1)

    def wait(self):
        self.eng.wait_ge(self.sem, self.n)

    def __call__(self, ins):
        self.free(ins)
        self.wait()


def unique(names, name):
    names[name] = names.get(name, 0) + 1
    return name if names[name] == 1 else f"{name}_{names[name]}"


@contextmanager
def stage(nc, names):
    sems = []

    def sem(name):
        sems.append(nc.alloc_semaphore(name=unique(names, name)))
        return sems[-1]

    with nc.Block() as block:
        yield block, sem
    nc.clear_and_free_semaphores(sems)
    nc.all_engine_barrier()


class Scratch:

    def __init__(self, sb):
        self.st = sb("norm_stats", [P, PT, 6])
        self.mv = sb("norm_mean_var", [P, PT, 2])
        self.v = sb("norm_v", [P, PT])
        self.a = sb("norm_a", [P, PT])
        self.w = sb("norm_w", [P, PT])
        self.y, self.y2 = sb("norm_rstd", [P, PT]), sb("norm_rstd_both", [P, PT])


def rsqrt(nc, chain, y, src, v, a, eps):
    chain(nc.vector.tensor_scalar(v, src, eps, None, ALU.add))
    chain(nc.vector.tensor_scalar(a.bitcast(I32), v.bitcast(I32), 1, None, ALU.logical_shift_right))
    chain(nc.vector.tensor_scalar(y.bitcast(I32), a.bitcast(I32), -1, RSQRT_SEED, ALU.mult, ALU.add))
    for _ in range(3):
        chain(nc.vector.scalar_tensor_tensor(a, y, -0.5, y, ALU.mult, ALU.mult))
        chain(nc.vector.tensor_tensor(a, a, v, ALU.mult))
        chain(nc.vector.scalar_tensor_tensor(y, a, 1.5, y, ALU.add, ALU.mult))


def normalise(nc, chain, s, dst, src, eps, centre, inner=None):
    for t in range(PT):
        chain.free(nc.vector.bn_stats(s.st[:, t, :], src[:, t, :]))
    chain.wait()
    for t in range(PT):
        chain.free(nc.vector.bn_aggr(s.mv[:, t, :], s.st[:, t, :]))
    chain.wait()
    y = s.y
    if centre:
        rsqrt(nc, chain, s.y[:, :], s.mv[:, :, 1], s.v[:, :], s.a[:, :], eps)
        if inner is not None:
            chain(nc.vector.tensor_tensor(s.a[:, :], s.y[:, :], s.y[:, :], ALU.mult))
            chain(nc.vector.tensor_tensor(s.w[:, :], s.mv[:, :, 1], s.a[:, :], ALU.mult))
            rsqrt(nc, chain, s.y2[:, :], s.w[:, :], s.v[:, :], s.a[:, :], inner)
            chain(nc.vector.tensor_tensor(s.y2[:, :], s.y2[:, :], s.y[:, :], ALU.mult))
            y = s.y2
    else:
        chain(nc.vector.tensor_tensor(s.a[:, :], s.mv[:, :, 0], s.mv[:, :, 0], ALU.mult))
        chain(nc.vector.tensor_tensor(s.w[:, :], s.a[:, :], s.mv[:, :, 1], ALU.add))
        rsqrt(nc, chain, s.y[:, :], s.w[:, :], s.v[:, :], s.a[:, :], eps)
    for t in range(PT):
        if centre:
            chain.free(nc.vector.tensor_scalar(dst[:, t, :], src[:, t, :], s.mv[:, t, 0:1], y[:, t:t + 1],
                                               ALU.subtract, ALU.mult))
        else:
            chain.free(nc.vector.tensor_scalar(dst[:, t, :], src[:, t, :], y[:, t:t + 1], None, ALU.mult))
    chain.wait()


def turn_tiles(nc, banks, src, ident, turned):
    for c in range(2):
        for t in range(PT):
            ins = nc.tensor.transpose(banks[0:CH, c, t * P:(t + 1) * P], src[:, t, c * CH:(c + 1) * CH], ident[:, :])
        ins.then_inc(turned, 1)


def dense(nc, out, lhs, rhs, n_rows=(CH, CH)):
    for k, rows in enumerate(n_rows):
        ins = nc.tensor.matmul(out, lhs(k, rows), rhs(k, rows), start=(k == 0), stop=(k == 1))
    return ins


BIASED = (CH, CH + 1)


def start_loads(sp, w, loaded):
    for dst, src in w.loads:
        sp.dma_start(dst, src).then_inc(loaded, 16)
    for dst, src in w.ffn_loads:
        sp.dma_start(dst, src).then_inc(w.ffn_loaded, 16)
    for dst, src in w.late_loads:
        sp.dma_start(dst, src).then_inc(w.late_loaded, 16)


def relative_setup(nc, env, w, windows):
    with stage(nc, env.names) as (block, sem):
        loaded, win_made, win_read, steps = sem("loaded"), sem("win_made"), sem("win_read"), sem("steps")
        filled = sem("filled")

        @block.sync
        def _(sp):
            start_loads(sp, w, loaded)
            if not windows:
                sp.dma_start(env.slots_in.rearrange("(t p) c -> p t c", p=P),
                             env.zeros[:, None, :].to_broadcast([P, SLOT_TILES, C])).then_inc(env.slots_zeroed, 16)
            sp.wait_ge(loaded, 16 * len(w.loads))

        @block.gpsimd
        def _(pool):
            chain = Chain(pool, filled)
            chain(nc.gpsimd.memset(w.V[:, :, :, HD:VW], 1.0))
            chain(nc.gpsimd.memset(w.xT[CH:CH + 1, 1, :], 1.0))
            chain(nc.gpsimd.memset(w.OT[CH:CH + 1, 1, :], 1.0))
            chain(nc.gpsimd.memset(w.Q[64:P, 0::2, :], 0.0))
            chain(nc.gpsimd.memset(w.Q[0:64, 1::2, :], 0.0))
            if windows:
                chain(nc.gpsimd.memset(w.xw[0:CH, :, :, :], 0.0))
                chain(nc.gpsimd.memset(w.xw[CH:CH + 1, 1, :, :], 1.0))

        if not windows:
            @block.tensor
            def _(pe):
                pe.wait_ge(loaded, 16 * len(w.loads))
                for n in range(2):
                    ins = nc.tensor.matmul(env.banks[0:CH, n, 0:TOKENS], w.rel[:, n, :], w.shrink[:, :],
                                           start=True, stop=True)
                ins.then_inc(win_made, 1)

        @block.vector
        def _(dve):
            chain = Chain(dve, steps)
            dve.wait_ge(loaded, 16 * len(w.loads))
            if not windows:
                dve.wait_ge(win_made, 1)
                for n in range(2):
                    chain.free(nc.vector.tensor_copy(w.win[:, n, :, :].rearrange("p a b -> p (a b)"),
                                                     env.banks[0:CH, n, 0:TOKENS]))
                chain.wait()
            for s in range(2):
                chain.free(nc.vector.tensor_copy(w.bd[:, 0, :, s, 16:32], w.qslot[:, None, s, :].to_broadcast([CH, SIDE, HD])))
                chain.free(nc.vector.memset(w.bd[:, 1, :, s, 16:32], 0.0))
                for n in range(2):
                    chain.free(nc.vector.tensor_scalar(w.bd[:, n, :, s, 0:16], w.win[:, n, :, :],
                                                       w.odd[:, s:s + 1], None, ALU.mult))
            if windows:
                for g in range(6):
                    for m in range(PAIR):
                        chain.free(nc.vector.tensor_scalar(w.K[:, g, m, :], w.hot[:, :], w.kpad[:, g:g + 1], None,
                                                           ALU.add))
            chain.wait()


def relative_project(nc, env, w, ip, windows):
    R, xn, banks, ident = env.R, env.xn, env.banks, env.ident
    n_vjobs = 8 if windows else PT
    with stage(nc, env.names) as (block, sem):
        steps = sem("steps")
        normed, turned, xT_ready = sem("normed"), sem("turned"), sem("xT_ready")
        stats_ready, group_ready, affine_ready = sem("stats_ready"), sem("group_ready"), sem("affine_ready")
        xw_ready, xw_steps = sem("xw_ready"), sem("xw_steps")
        a_done, a_out, k_done, k_out = sem("a_done"), sem("a_out"), sem("k_done"), sem("k_out")
        odd_out, copied = sem("odd_out"), sem("copied")

        def queries_out(copy, g, half):
            rows = slice(64 * half, 64 * half + 64)
            bank, q = banks[rows, (2 + n_vjobs + g) % 4, :], w.Q[rows, 2 * g + half, :]
            if not windows:
                return copy(q, bank)
            for n, (h0, nh, w0, nw) in enumerate(WINDOW_BOX):
                src = bank.rearrange("p (m a b) -> p m a b", m=PAIR, b=SIDE)[:, :, h0:h0 + nh, w0:w0 + nw]
                dst = q.rearrange("p (m t) -> p m t", m=PAIR)[:, :, WINDOW_AT[n]:WINDOW_AT[n] + nh * nw]
                ins = copy(dst.rearrange("p m (a b) -> p m a b", b=nw), src)
            return ins

        @block.vector
        def _(dve):
            chain = Chain(dve, steps)
            if windows:
                normalise(nc, chain, env.s, xn, env.X[:, bass.ds(ip * PT, PT), :], 1e-5, True)
            else:
                dve.wait_ge(copied, 1)
            dve.sem_inc(normed, 1)
            if not windows:
                dve.wait_ge(turned, 2)
                for c in range(2):
                    for m in range(PAIR):
                        chain.free(nc.vector.bn_stats(w.gst[:, c * 2 + m, :], banks[0:CH, c, m * TOKENS:(m + 1) * TOKENS]))
                chain.wait()
                for j in range(4):
                    chain.free(nc.vector.bn_aggr(w.gmv[:, j, :], w.gst[:, j, :]))
                chain.wait()
                chain(nc.vector.tensor_tensor(w.ga[:, :], w.gmv[:, :, 0], w.gmv[:, :, 0], ALU.mult))
                chain(nc.vector.tensor_tensor(w.gmv[:, :, 1], w.gmv[:, :, 1], w.ga[:, :], ALU.add))
                dve.sem_inc(stats_ready, 1)
                dve.wait_ge(group_ready, 1)
                chain(nc.vector.tensor_copy(w.gmv[:, :, :].rearrange("p a b -> p (a b)"), banks[0:CH, 2, 0:8]))
                chain(nc.vector.tensor_tensor(w.ga[:, :], w.gmv[:, :, 0], w.gmv[:, :, 0], ALU.mult))
                chain(nc.vector.tensor_tensor(w.gv[:, :], w.gmv[:, :, 1], w.ga[:, :], ALU.subtract))
                rsqrt(nc, chain, w.gscale[:, :], w.gv[:, :], w.gv[:, :], w.ga[:, :], 1e-5)
                chain(nc.vector.scalar_tensor_tensor(w.gbias[:, :], w.gmv[:, :, 0], -1.0, w.gscale[:, :], ALU.mult, ALU.mult))
                dve.sem_inc(affine_ready, 1)
            for g in range(6):
                dve.wait_ge(k_done, g + 1)
                src = banks[:, 4 + g % 4, :]
                if windows:
                    for n, (h0, nh, w0, nw) in enumerate(WINDOW_BOX):
                        real = src.rearrange("p (m a b) -> p m a b", m=PAIR, b=SIDE)[:, :, h0:h0 + nh, w0:w0 + nw]
                        dst = w.K[:, g, :, n * WN:(n + 1) * WN].rearrange("p m (a b) -> p m a b", b=WS)[:, :, 0:nh, 0:nw]
                        hot = w.hot[:, n * WN:(n + 1) * WN].rearrange("p (a b) -> p a b", b=WS)[:, None, 0:nh, 0:nw]
                        ins = nc.vector.tensor_tensor(dst, real, hot.to_broadcast([P, PAIR, nh, nw]), ALU.add)
                else:
                    for m in range(PAIR):
                        ins = nc.vector.tensor_tensor(w.K[:, g, m, :], src[:, m * TOKENS:(m + 1) * TOKENS],
                                                      w.hot[:, :], ALU.add)
                ins.then_inc(k_out, 1)
            for g in range(6):
                dve.wait_ge(a_done, 2 + n_vjobs + g + 1)
                queries_out(nc.vector.tensor_copy, g, 1).then_inc(odd_out, 1)
            dve.wait_ge(odd_out, 6)
            dve.wait_ge(k_out, 6)

        @block.scalar
        def _(act):
            for c in range(2):
                act.wait_ge(turned, c + 1)
                if windows:
                    nc.scalar.activation(w.xT[0:CH, c, :], banks[0:CH, c, :], ACT.Identity,
                                         bias=w.nb[:, c:c + 1], scale=w.nw[:, c:c + 1]).then_inc(xT_ready, 1)
                else:
                    act.wait_ge(affine_ready, 1)
                    for m in range(PAIR):
                        j = c * 2 + m
                        ins = nc.scalar.activation(w.xT[0:CH, c, m * TOKENS:(m + 1) * TOKENS],
                                                   banks[0:CH, c, m * TOKENS:(m + 1) * TOKENS], ACT.Identity,
                                                   bias=w.gbias[:, j:j + 1], scale=w.gscale[:, j:j + 1])
                    ins.then_inc(xT_ready, 1)
            for a in range(2 + n_vjobs + 6):
                act.wait_ge(a_done, a + 1)
                bank = banks[:, a % 4, :]
                if a < 2:
                    ins = nc.scalar.activation(w.qT[:, a, :], bank[0:CH, :], ACT.Copy)
                elif a < 2 + n_vjobs:
                    j = a - 2
                    if windows:
                        ins = nc.scalar.activation(w.V[0:98, 2 * j:2 * j + 2, :, 0:HD],
                                                   bank[0:98, 0:2 * C].rearrange("p (n h d) -> p n h d", n=2, d=HD), ACT.Copy)
                    else:
                        ins = nc.scalar.activation(w.V[:, j, :, 0:HD], bank[:, 0:C].rearrange("p (h d) -> p h d", d=HD),
                                                   ACT.Copy)
                else:
                    ins = queries_out(nc.scalar.copy, a - 2 - n_vjobs, 0)
                ins.then_inc(a_out, 1)
            act.wait_ge(a_out, 2 + n_vjobs + 6)

        @block.gpsimd
        def _(pool):
            nc.gpsimd.tensor_copy(R[:, :, :], env.X[:, bass.ds(ip * PT, PT), :]).then_inc(copied, 1)
            pool.wait_ge(copied, 1)
            if windows:
                chain = Chain(pool, xw_steps)
                pool.wait_ge(xT_ready, 2)
                for c in range(2):
                    for n, (h0, nh, w0, nw) in enumerate(WINDOW_BOX):
                        for m in range(PAIR):
                            src = w.xT[0:CH, c, m * TOKENS:(m + 1) * TOKENS].rearrange("p (a b) -> p a b", b=SIDE)
                            dst = w.xw[0:CH, c, m, n * WN:(n + 1) * WN].rearrange("p (a b) -> p a b", b=WS)
                            chain(nc.gpsimd.tensor_copy(dst[:, 0:nh, 0:nw], src[:, h0:h0 + nh, w0:w0 + nw]))
                pool.sem_inc(xw_ready, 1)

        @block.tensor
        def _(pe):
            pe.wait_ge(normed, 1)
            turn_tiles(nc, banks, xn if windows else R, ident, turned)
            if not windows:
                pe.wait_ge(stats_ready, 1)
                nc.tensor.matmul(banks[0:CH, 2, 0:8], w.gavg[:, :], w.gmv[:, :, :].rearrange("p a b -> p (a b)"),
                                 start=True, stop=True).then_inc(group_ready, 1)
            pe.wait_ge(xT_ready, 2)

            def queries(a):
                dense(nc, banks[0:CH, a % 4, :], lambda k, r: w.wq[0:r, k, a * CH:(a + 1) * CH],
                      lambda k, r: w.xT[0:r, k, :], BIASED).then_inc(a_done, 1)

            def keys(g):
                if g >= 4:
                    pe.wait_ge(k_out, g - 3)
                dense(nc, banks[:, 4 + g % 4, :], lambda k, r: w.wk[0:r, k, g * P:(g + 1) * P],
                      lambda k, r: w.xT[0:r, k, :], BIASED).then_inc(k_done, 1)

            def values(j):
                a = 2 + j
                if a >= 4:
                    pe.wait_ge(a_out, a - 3)
                if not windows:
                    ins = dense(nc, banks[:, a % 4, 0:C], lambda k, r: w.xT[0:r, k, j * P:(j + 1) * P],
                                lambda k, r: w.wv[0:r, k, :], BIASED)
                else:
                    for n in range(2):
                        m, at = divmod((2 * j + n) * 98, WINDOWS * WN)
                        ins = dense(nc, banks[0:98, a % 4, n * C:(n + 1) * C], lambda k, r: w.xw[0:r, k, m, at:at + 98],
                                    lambda k, r: w.wv[0:r, k, :], BIASED)
                ins.then_inc(a_done, 1)

            def relative(g):
                a = 2 + n_vjobs + g
                pe.wait_ge(a_out, a - 3)
                if g >= 4:
                    pe.wait_ge(odd_out, g - 3)
                row, c = 32 * (g % 3), g // 3
                q = w.qT[row:row + 32, c, :].rearrange("p (m a b) -> p m a b", m=PAIR, b=SIDE)
                o = banks[:, a % 4, :].rearrange("p (m a b) -> p m a b", m=PAIR, b=SIDE)
                for r in range(SIDE):
                    for s in range(2):
                        nc.tensor.matmul(o[64 * s:64 * s + 32, :, r, :], w.bd[row:row + 32, 0, r, s, :], q[:, :, r, :],
                                         start=True, stop=True)
                        ins = nc.tensor.matmul(o[64 * s + 32:64 * s + 64, :, :, r], w.bd[row:row + 32, 1, r, s, :],
                                               q[:, :, :, r], start=True, stop=True)
                ins.then_inc(a_done, 1)

            queries(0)
            queries(1)
            for g in range(6):
                keys(g)
            if windows:
                pe.wait_ge(xw_ready, 1)
            for j in range(n_vjobs):
                values(j)
            for g in range(6):
                relative(g)


class Layout:

    def __init__(self, kind, w):
        self.kind, self.w = kind, w
        self.tiles = 3 if kind == "windows" else 2
        self.rows_in = CH if kind == "causal" else P
        self.group = 6 if kind == "causal" else 2

    def rows(self, t):
        return P if self.kind != "windows" else (98, 98, 68)[t]

    def width(self, t):
        return {"windows": WN, "full": TOKENS, "causal": (t + 1) * P}[self.kind]

    def chunk(self):
        return 98 if self.kind == "windows" else P

    def chunks(self, t):
        return self.width(t) // self.chunk()

    def parts(self, t):
        if self.kind != "windows":
            return [(0, P, 0)]
        return [(0, 98, 0)] if t < 2 else [(32 * (n - 1), WINDOW_BOX[n][1] * WINDOW_BOX[n][3], n) for n in (1, 2, 3)]

    def tokens(self, ap, m, t, window):
        if self.kind != "windows":
            return ap[:, m * TOKENS + t * P:m * TOKENS + (t + 1) * P]
        h0, nh, w0, nw = WINDOW_BOX[window]
        if window == 0:
            h0, nh = 7 * t, 7
        a = ap[:, m * TOKENS:(m + 1) * TOKENS].rearrange("p (a b) -> p a b", b=SIDE)
        return a[:, h0:h0 + nh, w0:w0 + nw]

    def q(self, m, t, h, window):
        q = self.w.Q[0:self.rows_in, h, :]
        if self.kind != "windows":
            return self.tokens(q, m, t, window)
        at = m * TOKENS + (98 * t if window == 0 else WINDOW_AT[window])
        return q[:, at:at + (98 if window == 0 else WINDOW_BOX[window][1] * WINDOW_BOX[window][3])]

    def k(self, m, t, h, window):
        g = h // self.group
        if self.kind == "causal":
            return self.w.K[:, g, m * TOKENS:m * TOKENS + self.width(t)]
        if self.kind == "full":
            return self.w.K[:, g, m, :]
        return self.w.K[:, g, m, window * WN:(window + 1) * WN]

    def v(self, m, h, c, window):
        if self.kind == "windows":
            return self.w.V[0:98, m * 8 + window * 2 + c, h, :]
        return self.w.V[:, m * 2 + c, h * self.w.kv_heads // HEADS, :]


def attend(nc, env, w, kind):
    R, banks, ident = env.R, env.banks, env.ident
    lay = Layout(kind, w)
    HP = HEADS // 2
    units = [(m, t, hp) for m in range(PAIR) for t in range(lay.tiles) for hp in range(HP)]
    U = len(units)
    ck = lay.chunk()
    with stage(nc, env.names) as (block, sem):
        scores_ready, max_ready, exp_ready = sem("scores_ready"), sem("max_ready"), sem("exp_ready")
        turned, copied, pv_done = sem("turned"), sem("copied"), sem("pv_done")
        normed, o_turned, OT_ready = sem("normed"), sem("o_turned"), sem("OT_ready")
        O_out, om_turned = sem("O_out"), sem("om_turned")
        projected, added, steps = sem("projected"), sem("added"), sem("steps")

        def ends_tile(u):
            return u // HP if 0 <= u < U and u % HP == HP - 1 else None

        def ends_image(u):
            return u // (HP * lay.tiles) if 0 <= u < U and (u + 1) % (HP * lay.tiles) == 0 else None

        def S(u):
            return banks[:, u % 3, :].rearrange("p (h k) -> p h k", h=2)

        def PTb(u):
            return banks[:, 3 + u % 2, :].rearrange("p (s q) -> p s q", q=P)

        def O(tile):
            return banks[:, 5 + tile % 2, 0:3 * P].rearrange("p (g q) -> p g q", q=P)

        OM = banks[:, 7, 0:3 * P].rearrange("p (h d) -> p h d", d=32)

        @block.tensor
        def _(pe):
            for s in range(U + 9):
                if s < U:
                    m, t, hp = units[s]
                    if s >= 3:
                        pe.wait_ge(exp_ready, s - 2)
                    for hh in range(2):
                        h = 2 * hp + hh
                        for r0, rn, win in lay.parts(t):
                            ins = nc.tensor.matmul(S(s)[r0:r0 + rn, hh, 0:lay.width(t)], lay.q(m, t, h, win),
                                                   lay.k(m, t, h, win), start=(hh == 0 or kind != "causal"),
                                                   stop=(kind != "causal"),
                                                   skip_group_check=(kind == "causal"))
                    if kind != "causal":
                        ins.then_inc(scores_ready, 1)
                u = s - 3
                if 0 <= u < U and u % 2 == 1:
                    m, t, hp = units[u]
                    tile = u // HP
                    pe.wait_ge(copied, u + 1)
                    if hp == 1 and tile >= 2:
                        pe.wait_ge(O_out, tile - 1)
                    for r0, rn, win in lay.parts(t):
                        for c in range(lay.chunks(t)):
                            for j in range(4):
                                h = 2 * hp - 2 + j
                                ins = nc.tensor.matmul(O(tile)[32 * j:32 * j + VW, h // 4, r0:r0 + rn],
                                                       lay.v(m, h, c, win),
                                                       w.PT[0:ck, (u - 1 + j // 2) % 4, j % 2 * lay.chunks(t) + c, r0:r0 + rn],
                                                       start=(c == 0), stop=(c == lay.chunks(t) - 1))
                    ins.then_inc(pv_done, 1)
                if s < U and kind == "causal":
                    t = units[s][1]
                    nc.tensor.matmul(S(s)[:, :, t * P:(t + 1) * P], env.ident16[:, :], env.mask16[:, :, :],
                                     start=False, stop=True, skip_group_check=True).then_inc(scores_ready, 1)
                u = s - 2
                if 0 <= u < U:
                    m, t, hp = units[u]
                    rows = lay.rows(t)
                    pe.wait_ge(exp_ready, u + 1)
                    if u >= 2:
                        pe.wait_ge(copied, u - 1)
                    for hh in range(2):
                        for c in range(lay.chunks(t)):
                            ins = nc.tensor.transpose(PTb(u)[0:ck, hh * lay.chunks(t) + c, 0:rows],
                                                      w.Pr[0:rows, u % 3, hh, c * ck:(c + 1) * ck], ident[0:rows, 0:rows])
                    ins.then_inc(turned, 1)
                tile = ends_tile(s - 5)
                if tile is not None:
                    m, t, _ = units[s - 5]
                    rows = lay.rows(t)
                    pe.wait_ge(O_out, tile + 1)
                    if tile >= 1:
                        pe.wait_ge(OT_ready, tile)
                    if m >= 1:
                        pe.wait_ge(added, m)
                    for g in range(3):
                        ins = nc.tensor.transpose(banks[0:rows, 7, g * P:(g + 1) * P], w.Os[:, tile % 2, g, 0:rows],
                                                  ident[:, :])
                    ins.then_inc(om_turned, 1)
                tile = ends_tile(s - 7)
                if tile is not None:
                    m, t, _ = units[s - 7]
                    rows = lay.rows(t)
                    pe.wait_ge(normed, tile + 1)
                    for c in range(2):
                        ins = nc.tensor.transpose(banks[0:CH, 7, c * P:c * P + rows],
                                                  w.On[0:rows, tile % 2, c * CH:(c + 1) * CH], ident[0:rows, 0:rows])
                    ins.then_inc(o_turned, 1)
                m = ends_image(s - 8)
                if m is not None:
                    pe.wait_ge(OT_ready, lay.tiles * (m + 1))
                    for t in range(2):
                        cols = slice(m * TOKENS + t * P, m * TOKENS + (t + 1) * P)
                        ins = dense(nc, banks[:, 7, t * C:(t + 1) * C], lambda k, r: w.OT[0:r, k, cols],
                                    lambda k, r: w.wo[0:r, k, :], w.out_rows)
                    ins.then_inc(projected, 1)

        @block.scalar
        def _(act):
            for s in range(U + 9):
                if s < U:
                    _, t, _ = units[s]
                    rows = lay.rows(t)
                    act.wait_ge(max_ready, s + 1)
                    if s >= 3:
                        act.wait_ge(turned, s - 2)
                    for hh in range(2):
                        ins = nc.scalar.activation(w.Pr[0:rows, s % 3, hh, 0:lay.width(t)],
                                                   S(s)[0:rows, hh, 0:lay.width(t)], ACT.Exp,
                                                   bias=w.nmax[0:rows, s % 4, hh:hh + 1])
                    ins.then_inc(exp_ready, 1)
                tile = ends_tile(s - 4)
                if tile is not None:
                    _, t, _ = units[s - 4]
                    rows = lay.rows(t)
                    act.wait_ge(pv_done, (s - 4 + 1) // 2)
                    if tile >= 2:
                        act.wait_ge(om_turned, tile - 1)
                    nc.scalar.activation(w.Os[:, tile % 2, :, 0:rows], O(tile)[:, :, 0:rows], ACT.Copy).then_inc(O_out, 1)
                tile = ends_tile(s - 7)
                if tile is not None:
                    m, t, _ = units[s - 7]
                    act.wait_ge(o_turned, tile + 1)
                    for r0, rn, win in lay.parts(t):
                        for c in range(2):
                            src = banks[0:CH, 7, c * P + r0:c * P + r0 + rn]
                            dst = lay.tokens(w.OT[0:CH, c, :], m, t, win)
                            if kind == "windows":
                                src = src.rearrange("p (a b) -> p a b", b=WINDOW_BOX[win][3])
                            ins = nc.scalar.activation(dst, src, ACT.Copy)
                    ins.then_inc(OT_ready, 1)

        @block.vector
        def _(dve):
            chain = Chain(dve, steps)
            for s in range(U + 9):
                if s < U:
                    _, t, _ = units[s]
                    rows = lay.rows(t)
                    dve.wait_ge(scores_ready, s + 1)
                    if s >= 4:
                        dve.wait_ge(exp_ready, s - 3)
                    nc.vector.tensor_reduce(w.nmax[0:rows, s % 4, :], S(s)[0:rows, :, 0:lay.width(t)], AX.X, ALU.max,
                                            negate=True).then_inc(max_ready, 1)
                u = s - 2
                if 0 <= u < U:
                    _, t, _ = units[u]
                    rows, n = lay.rows(t), 2 * lay.chunks(t)
                    dve.wait_ge(turned, u + 1)
                    if u >= 4:
                        dve.wait_ge(pv_done, u // 2 - 1)
                    nc.vector.tensor_copy(w.PT[0:ck, u % 4, 0:n, 0:rows], PTb(u)[0:ck, 0:n, 0:rows]).then_inc(copied, 1)
                tile = ends_tile(s - 6)
                if tile is not None:
                    _, t, _ = units[s - 6]
                    rows = lay.rows(t)
                    dve.wait_ge(om_turned, tile + 1)
                    if tile >= 2:
                        dve.wait_ge(o_turned, tile - 1)
                    chain(nc.vector.reciprocal(w.rsum[0:rows, tile % 2, :], OM[0:rows, :, HD]))
                    nc.vector.tensor_tensor(w.On[0:rows, tile % 2, :].rearrange("p (h d) -> p h d", d=HD),
                                            OM[0:rows, :, 0:HD],
                                            w.rsum[0:rows, tile % 2, :, None].to_broadcast([rows, HEADS, HD]),
                                            ALU.mult).then_inc(normed, 1)
                m = ends_image(s - 9)
                if m is not None:
                    dve.wait_ge(projected, m + 1)
                    r = R[:, 2 * m:2 * m + 2, :]
                    nc.vector.tensor_tensor(r, r, banks[:, 7, 0:2 * C].rearrange("p (t c) -> p t c", c=C),
                                            ALU.add).then_inc(added, 1)
            dve.wait_ge(added, PAIR)


def store_residual(nc, chain, env, ip, add):
    x = env.X[:, bass.ds(ip * PT, PT), :]
    if add:
        chain(nc.vector.tensor_tensor(x, x, env.R[:, :, :], ALU.add))
    else:
        chain(nc.vector.tensor_copy(x, env.R[:, :, :]))


def causal_project(nc, env, w, ip, base_ln, inner_rms, rope):
    R, xn, banks, ident = env.R, env.xn, env.banks, env.ident
    NKV = w.kv_heads
    products = [(n, c, sw) for n in range(2) for c in range(2) for sw in range(2 if rope else 1)]
    per = 2 if rope else 1
    act_heads = [(c, j) for c in range(2) for j in range(6) if (j >= 2 if rope else c == 0)]
    dve_heads = [(c, j) for c in range(2) for j in range(6) if (c, j) not in act_heads]
    with stage(nc, env.names) as (block, sem):
        steps = sem("steps")
        normed, turned, xT_ready = sem("normed"), sem("turned"), sem("xT_ready")
        product_done, v_done, v_out = sem("product_done"), sem("v_done"), sem("v_out")
        copied = sem("copied")
        rotated, Q_out, bank_read = sem("rotated"), sem("Q_out"), sem("bank_read")

        def bank(i):
            return banks[0:CH, 2 + i % 6, :]

        @block.vector
        def _(dve):
            chain = Chain(dve, steps)
            x = env.X[:, bass.ds(ip * PT, PT), :]
            normalise(nc, chain, env.s, xn, x, 1e-5, True, inner_rms)
            dve.sem_inc(normed, 1)

            def heads_out(c, src):
                for _, j in [head for head in dve_heads if head[0] == c]:
                    chain.free(nc.vector.tensor_scalar(w.Q[:, 6 * c + j, :], src, w.own[:, j:j + 1], None, ALU.mult))

            if base_ln:
                for t in range(PT):
                    chain.free(nc.vector.tensor_scalar(R[:, t, :], x[:, t, :], env.s.mv[:, t, 0:1], env.s.y[:, t:t + 1],
                                                       ALU.subtract, ALU.mult))
            if rope:
                halves = lambda ap: ap.rearrange("p (m q) -> p m q", m=PAIR)
                for i in range(0, len(products), 2):
                    n, c, _ = products[i]
                    dve.wait_ge(product_done, i + 2)
                    cos = w.cos[:, None, :].to_broadcast([CH, PAIR, TOKENS])
                    sin = w.sin[:, None, :].to_broadcast([CH, PAIR, TOKENS])
                    dst = w.qT[:, c, :] if n == 0 else w.K[:, c, :]
                    chain.free(nc.vector.tensor_tensor(halves(dst), halves(bank(i)), cos, ALU.mult))
                    chain.free(nc.vector.tensor_tensor(halves(w.rb[:, :]), halves(bank(i + 1)), sin, ALU.mult))
                    chain.wait()
                    dve.sem_inc(bank_read, 2)
                    chain(nc.vector.tensor_tensor(dst, dst, w.rb[:, :], ALU.add))
                    dve.sem_inc(rotated, 1)
                    if n == 0:
                        heads_out(c, w.qT[:, c, :])
            else:
                for c in range(2):
                    dve.wait_ge(product_done, c + 1)
                    heads_out(c, bank(c))
            chain.wait()

        if not base_ln:
            @block.gpsimd
            def _(pool):
                nc.gpsimd.tensor_copy(R[:, :, :], env.X[:, bass.ds(ip * PT, PT), :]).then_inc(copied, 1)
                pool.wait_ge(copied, 1)

        @block.scalar
        def _(act):
            for c in range(2):
                act.wait_ge(turned, c + 1)
                nc.scalar.activation(w.xT[0:CH, c, :], banks[0:CH, c, :], ACT.Copy if w.nw is None else ACT.Identity,
                                     scale=1.0 if w.nw is None else w.nw[:, c:c + 1]).then_inc(xT_ready, 1)
            for c, j in act_heads:
                act.wait_ge(rotated if rope else product_done, c + 1)
                src = w.qT[:, c, :] if rope else bank(c)
                nc.scalar.activation(w.Q[:, 6 * c + j, :], src, ACT.Identity,
                                     scale=w.own[:, j:j + 1]).then_inc(Q_out, 1)
            if not rope:
                for c in range(2):
                    act.wait_ge(product_done, 2 + c + 1)
                    nc.scalar.activation(w.K[:, c, :], bank(2 + c), ACT.Copy).then_inc(Q_out, 1)
            for b in range(2):
                act.wait_ge(v_done, b + 1)
                nc.scalar.activation(w.V[:, 2 * b:2 * b + 2, :, 0:HD].rearrange("p t h d -> p (t h) d"),
                                     banks[:, b, 0:2 * NKV * HD].rearrange("p (t h d) -> p (t h) d", t=2, d=HD),
                                     ACT.Copy).then_inc(v_out, 1)
            act.wait_ge(v_out, 2)
            act.wait_ge(Q_out, 8)

        @block.tensor
        def _(pe):
            pe.wait_ge(normed, 1)
            turn_tiles(nc, banks, xn, ident, turned)
            pe.wait_ge(xT_ready, 2)

            def values():
                for t in range(PT):
                    ins = dense(nc, banks[:, t // 2, t % 2 * NKV * HD:(t % 2 + 1) * NKV * HD],
                                lambda k, r: w.xT[0:r, k, t * P:(t + 1) * P], lambda k, r: w.wv[0:r, k, :], w.in_rows)
                    if t % 2 == 1:
                        ins.then_inc(v_done, 1)

            for i, (n, c, sw) in enumerate(products):
                if i == 2 * per:
                    values()
                if i >= 6:
                    pe.wait_ge(bank_read, i - 5)
                at = ((n * per + sw) * 2 + c) * CH
                dense(nc, bank(i), lambda k, r: w.wqk[0:r, k, at:at + CH], lambda k, r: w.xT[0:r, k, :],
                      w.in_rows).then_inc(product_done, 1)


def causal_setup(nc, env, w):
    with stage(nc, env.names) as (block, sem):
        loaded, filled = sem("loaded"), sem("filled")

        @block.sync
        def _(sp):
            start_loads(sp, w, loaded)
            sp.wait_ge(loaded, 16 * len(w.loads))

        @block.gpsimd
        def _(pool):
            chain = Chain(pool, filled)
            chain(nc.gpsimd.memset(w.V[:, :, :, HD:VW], 1.0))
            chain(nc.gpsimd.memset(w.xT[CH:CH + 1, 1, :], 1.0))
            chain(nc.gpsimd.memset(w.OT[CH:CH + 1, 1, :], 1.0))


def feed_forward(nc, env, w, ip, gated):
    R, xn, banks, ident = env.R, env.xn, env.banks, env.ident
    NF = FF // P
    with stage(nc, env.names) as (block, sem):
        steps = sem("steps")
        normed, turned, xT_ready = sem("normed"), sem("turned"), sem("xT_ready")
        up_done, act_done, h_ready, out_done = sem("up_done"), sem("act_done"), sem("h_ready"), sem("out_done")

        @block.vector
        def _(dve):
            chain = Chain(dve, steps)
            normalise(nc, chain, env.s, xn, R, 1e-5, not gated)
            dve.sem_inc(normed, 1)
            if gated:
                for f in range(NF):
                    dve.wait_ge(act_done, f + 1)
                    nc.vector.tensor_tensor(w.hT[:, f, :], w.sg[:, f % 2, :], banks[:, 2 + f % 2, :],
                                            ALU.mult).then_inc(h_ready, 1)
            for t in range(PT):
                dve.wait_ge(out_done, t + 1)
                chain.free(nc.vector.tensor_tensor(R[:, t, :], R[:, t, :], banks[:, 4 + t, 0:C], ALU.add))
            chain.wait()
            store_residual(nc, chain, env, ip, gated)

        @block.scalar
        def _(act):
            act.wait_ge(w.ffn_loaded, 16 * len(w.ffn_loads))
            for c in range(2):
                act.wait_ge(turned, c + 1)
                nc.scalar.activation(w.xT[0:CH, c, :], banks[0:CH, c, :], ACT.Identity, scale=w.fnw[:, c:c + 1],
                                     bias=0.0 if gated else w.fnb[:, c:c + 1]).then_inc(xT_ready, 1)
            for f in range(NF):
                act.wait_ge(up_done, f + 1)
                if gated:
                    if f >= 2:
                        act.wait_ge(h_ready, f - 1)
                    nc.scalar.activation(w.sg[:, f % 2, :], banks[:, f % 2, :], ACT.Silu).then_inc(act_done, 1)
                else:
                    nc.scalar.activation(w.hT[:, f, :], banks[:, f % 4, :], ACT.Gelu).then_inc(h_ready, 1)

        @block.tensor
        def _(pe):
            pe.wait_ge(normed, 1)
            turn_tiles(nc, banks, xn, ident, turned)
            pe.wait_ge(w.ffn_loaded, 16 * len(w.ffn_loads))
            pe.wait_ge(xT_ready, 2)
            for f in range(NF):
                slots = 2 if gated else 4
                if f >= slots:
                    pe.wait_ge(h_ready, f - slots + 1)
                x = lambda k, r: w.xT[0:r, k, :]
                if gated:
                    dense(nc, banks[:, f % 2, :], lambda k, r: w.w1[0:r, k, f * P:(f + 1) * P], x)
                    ins = dense(nc, banks[:, 2 + f % 2, :], lambda k, r: w.w3[0:r, k, f * P:(f + 1) * P], x)
                else:
                    ins = dense(nc, banks[:, f % 4, :], lambda k, r: w.w1[0:r, k, f * P:(f + 1) * P], x, BIASED)
                ins.then_inc(up_done, 1)
            pe.wait_ge(h_ready, NF)
            for t in range(PT):
                for f in range(NF):
                    ins = nc.tensor.matmul(banks[:, 4 + t, 0:C], w.hT[:, f, t * P:(t + 1) * P], w.w2[:, f, :],
                                           start=(f == 0), stop=(gated and f == NF - 1))
                if not gated:
                    ins = nc.tensor.matmul(banks[:, 4 + t, 0:C], env.ones[0:1, :], w.b2[0:1, :], start=False, stop=True)
                ins.then_inc(out_done, 1)


def route(nc, env, w, ip, first):
    R, xn, banks, ident, E = env.R, env.xn, env.banks, env.ident, w.experts
    with stage(nc, env.names) as (block, sem):
        steps = sem("steps")
        normed, turned, xT_ready, kept = sem("normed"), sem("turned"), sem("xT_ready"), sem("kept")
        logits_done, margin_ready, exp_done = sem("logits_done"), sem("margin_ready"), sem("exp_done")

        @block.vector
        def _(dve):
            chain = Chain(dve, steps)
            if first:
                store_residual(nc, chain, env, ip, True)
                normalise(nc, chain, env.s, xn, R, 1e-6, False)
            else:
                chain(nc.vector.tensor_copy(R[:, :, :], env.X[:, bass.ds(ip * PT, PT), :]))
                normalise(nc, chain, env.s, xn, R, 1e-5, True)
            dve.sem_inc(normed, 1)
            dve.wait_ge(logits_done, 1)
            chain(nc.vector.tensor_copy(w.logits[:, :, :], banks[:, 2, 0:PT * E].rearrange("p (t e) -> p t e", e=E)))
            for t in range(PT):
                chain.free(nc.vector.max(w.top[:, t, :], w.logits[:, t, :]))
            chain.wait()
            for t in range(PT):
                chain.free(nc.vector.max_index(w.topi[:, t, :], w.top[:, t, :], w.logits[:, t, :]))
            chain.free(nc.vector.tensor_tensor(w.margin[:, :], w.top[:, :, 1], w.top[:, :, 0], ALU.subtract))
            chain.wait()
            dve.sem_inc(margin_ready, 1)
            chain.free(nc.vector.tensor_copy(w.expert[:, bass.ds(ip * PT, PT), :], w.topi[:, :, 0:2]))
            dve.wait_ge(exp_done, 1)
            chain(nc.vector.tensor_scalar(w.g1[:, :], w.margin[:, :], 1.0, None, ALU.add))
            chain(nc.vector.reciprocal(w.g0[:, :], w.g1[:, :]))
            chain.free(nc.vector.tensor_copy(w.weight[:, bass.ds(ip * PT, PT), 0], w.g0[:, :]))
            chain(nc.vector.tensor_tensor(w.weight[:, bass.ds(ip * PT, PT), 1], w.margin[:, :], w.g0[:, :], ALU.mult))

        @block.gpsimd
        def _(pool):
            pool.wait_ge(normed, 1)
            nc.gpsimd.tensor_copy(w.M[:, bass.ds(ip * PT, PT), :], xn[:, :, :]).then_inc(kept, 1)
            pool.wait_ge(kept, 1)

        @block.scalar
        def _(act):
            for c in range(2):
                act.wait_ge(turned, c + 1)
                nc.scalar.activation(w.xT[0:CH, c, :], banks[0:CH, c, :],
                                     ACT.Identity if first else ACT.Copy,
                                     scale=w.nw2[:, c:c + 1] if first else 1.0).then_inc(xT_ready, 1)
            act.wait_ge(margin_ready, 1)
            nc.scalar.activation(w.margin[:, :], w.margin[:, :], ACT.Exp).then_inc(exp_done, 1)

        @block.tensor
        def _(pe):
            pe.wait_ge(normed, 1)
            turn_tiles(nc, banks, xn, ident, turned)
            pe.wait_ge(xT_ready, 2)
            for t in range(PT):
                ins = dense(nc, banks[:, 2, t * E:(t + 1) * E], lambda k, r: w.xT[0:r, k, t * P:(t + 1) * P],
                            lambda k, r: w.wr[0:r, k, :], w.r_rows)
            ins.then_inc(logits_done, 1)


def running_sum(nc, chain, bufs, n, at):
    src, dst = bufs
    s = 1
    while s < n:
        chain.free(nc.vector.tensor_tensor(at(dst, s, n), at(src, s, n), at(src, 0, n - s), ALU.add))
        chain.free(nc.vector.tensor_copy(at(dst, 0, s), at(src, 0, s)))
        chain.wait()
        src, dst, s = dst, src, 2 * s
    return src


def sort_tokens(nc, env, w):
    banks, E = env.banks, w.experts
    with stage(nc, env.names) as (block, sem):
        steps, picked, counted = sem("steps"), sem("picked"), sem("counted")
        slots_ready, scattered, shared_in = sem("slots_ready"), sem("scattered"), sem("shared_in")

        @block.vector
        def _(dve):
            chain = Chain(dve, steps)
            expert = w.expert[:, :, :].rearrange("p t k -> p (t k)")
            chain(nc.vector.tensor_tensor(w.hit[:, :, :], env.iota[:, None, 0:E].to_broadcast([P, PICKS, E]),
                                          expert[:, :, None].to_broadcast([P, PICKS, E]), ALU.is_equal))
            chain(nc.vector.tensor_copy(w.hit16[:, :, :], w.hit[:, :, :]))
            dve.sem_inc(picked, 1)
            dve.wait_ge(counted, 1)
            before = banks[:, 0, 0:PICKS * E].rearrange("p (a e) -> p a e", e=E)
            column = banks[:, 1, 0:PICKS * E].rearrange("p (a e) -> p a e", e=E)
            chain(nc.vector.tensor_copy(w.sum_a[:, :, :], column))
            total = running_sum(nc, chain, (w.sum_a, w.sum_b), PICKS, lambda b, lo, hi: b[:, lo:hi, :])
            chain(nc.vector.tensor_scalar(w.count[:, :], total[:, PICKS - 1, :], float(P - 1), None, ALU.add))
            chain(nc.vector.tensor_scalar(w.count[:, :], w.count[:, :], P.bit_length() - 1, None, ALU.logical_shift_right))
            chain(nc.vector.tensor_copy(w.ends[0][:, :], w.count[:, :]))
            end = running_sum(nc, chain, w.ends, E, lambda b, lo, hi: b[:, lo:hi])
            chain(nc.vector.tensor_tensor(w.passed[:, :, :], env.iota[0:1, 0:SORTED_TILES[E], None].to_broadcast([1, SORTED_TILES[E], E]),
                                          end[0:1, None, :].to_broadcast([1, SORTED_TILES[E], E]), ALU.is_ge))
            chain(nc.vector.tensor_reduce(w.owner[:, :], w.passed[:, :, :], AX.X, ALU.add))
            at = SHARED_FIRST if w.shared else 0
            chain(nc.vector.tensor_scalar(w.tile_expert[:, at:at + SORTED_TILES[E]], w.owner[:, :], float(E - 1), None, ALU.min))
            chain(nc.vector.tensor_tensor(w.slots[:, :, :], total[:, :, :], column, ALU.subtract))
            chain(nc.vector.tensor_tensor(w.slots[:, :, :], w.slots[:, :, :], before, ALU.add))
            chain(nc.vector.tensor_copy(w.first[:, :], w.count[:, :]))
            chain(nc.vector.tensor_tensor(w.first[:, :], end[:, :], w.first[:, :], ALU.subtract))
            if w.shared:
                chain(nc.vector.tensor_scalar(w.first[:, :], w.first[:, :], float(SHARED_FIRST), None, ALU.add))
            chain(nc.vector.scalar_tensor_tensor(w.slots[:, :, :], w.first[:, None, :].to_broadcast([P, PICKS, E]), float(P),
                                                 w.slots[:, :, :], ALU.mult, ALU.add))
            chain(nc.vector.tensor_tensor(w.slots[:, :, :], w.slots[:, :, :], w.hit[:, :, :], ALU.mult))
            chain(nc.vector.tensor_reduce(w.slot[:, :], w.slots[:, :, :], AX.X, ALU.add))
            chain(nc.vector.tensor_copy(w.slot_index[:, :], w.slot[:, :]))
            dve.sem_inc(slots_ready, 1)

        @block.tensor
        def _(pe):
            pe.wait_ge(picked, 1)
            hit = w.hit16[:, :, :].rearrange("p a e -> p (a e)")
            nc.tensor.matmul(banks[:, 0, 0:PICKS * E], env.above16[:, :], hit, start=True, stop=True)
            nc.tensor.matmul(banks[:, 1, 0:PICKS * E], env.ones16[:, :], hit, start=True, stop=True).then_inc(counted, 1)

        if not w.shared:
            @block.gpsimd
            def _(pool):
                pool.wait_ge(env.slots_zeroed, 16)
                pool.wait_ge(slots_ready, 1)
                scatter(nc, env, w, scattered)
                pool.wait_ge(scattered, 16 * PICKS)

        @block.sync
        def _(sp):
            for dst, src in w.last_loads:
                sp.dma_start(dst, src).then_inc(w.experts_loaded, 16)
            if w.shared:
                sp.wait_ge(env.slots_zeroed, 16)
                for (lo, hi), t in zip(shared_tiles(E), (0, SHARED_FIRST)):
                    dst = env.slots_in[lo * P:hi * P, :].rearrange("(t p) c -> p t c", p=P)
                    sp.dma_start(dst, w.M[:, t:t + hi - lo, :]).then_inc(shared_in, 16)
                sp.wait_ge(shared_in, 32)


def shared_tiles(E):
    return (0, SHARED_FIRST), (SHARED_FIRST + SORTED_TILES[E], SLOT_TILES)


def scatter(nc, env, w, scattered):
    for a in range(PICKS):
        nc.gpsimd.indirect_dma_start(
            env.slots_in[:, :], bass.IndirectOffsetOnAxis(ap=w.slot_index[:, a:a + 1], axis=0),
            w.M[:, a // 2, :], None).then_inc(scattered, 16)


def pipeline(eng, n, jobs):
    last = max(lag for _, lag in jobs)
    head = last + 2 + (n - last) % 2

    def step(s, j=None):
        for job, lag in jobs:
            if j is not None or 0 <= s - lag < n:
                i, half = s - lag, (s - lag) // 2
                job(i if j is None else j * 2 + i, i % 2, half if j is None else j + half)

    for s in range(head):
        step(s)
    with eng.Fori(0, (n - head) // 2) as j:
        for r in range(2):
            step(head + r, j)
    for s in range(n, n + last):
        step(s)


def experts(nc, env, w):
    banks, ident, E = env.banks, env.ident, w.experts
    NF = EF // P
    with stage(nc, env.names) as (block, sem):
        x_loaded = [sem("x_loaded_even"), sem("x_loaded_odd")]
        y_stored = [sem("y_stored_even"), sem("y_stored_odd")]
        x_turned, xT_out, gu_done, silu_done = sem("x_turned"), sem("xT_out"), sem("gu_done"), sem("silu_done")
        h_done, h_turned, hT_out, down_done, y_out = (sem("h_done"), sem("h_turned"), sem("hT_out"), sem("down_done"),
                                                      sem("y_out"))
        gathered = [sem(f"gathered_{q}") for q in range(TILES // 2)]
        shared_out, summed, scattered = sem("shared_out"), sem("summed"), sem("scattered")

        @block.sync
        def _(sp):
            def rows(dram, i):
                r = slice(i * P, (i + 1) * P) if isinstance(i, int) else bass.ds(i * P, P)
                return dram[r, :]

            def load(i, par, half):
                if w.shared and isinstance(i, int) and i == SHARED_FIRST:
                    sp.wait_ge(scattered, 16 * PICKS)
                sp.wait_ge(x_turned, i + 1)
                sp.dma_start(w.xin[:, par, :], rows(env.slots_in, i)).then_inc(x_loaded[par], 16)

            def store(i, par, half):
                sp.wait_ge(y_out, i + 2)
                sp.dma_start(rows(env.slots_out, i), w.y[:, par, :]).then_inc(y_stored[par], 16)

            pipeline(sp, SLOT_TILES, ((load, 0), (store, 5)))
            sp.wait_ge(y_stored[0], 16 * ((SLOT_TILES + 1) // 2))
            sp.wait_ge(y_stored[1], 16 * (SLOT_TILES // 2))
            if w.shared:
                for (lo, hi), t in zip(shared_tiles(E), (0, SHARED_FIRST)):
                    src = env.slots_out[lo * P:hi * P, :].rearrange("(t p) c -> p t c", p=P)
                    sp.dma_start(w.shared_y[:, t:t + hi - lo, :], src).then_inc(shared_out, 16)

        @block.tensor
        def _(pe):
            def expert_of(i):
                at = slice(i, i + 1) if isinstance(i, int) else bass.ds(i, 1)
                return pe.value_load(w.tile_expert[0:1, at], min_val=0, max_val=w.stored - 1)

            def turn(i, par, half):
                pe.wait_ge(x_loaded[par], half * 16 + 16)
                pe.wait_ge(xT_out, i + 1)
                for c in range(2):
                    ins = nc.tensor.transpose(banks[0:CH, par, c * P:(c + 1) * P], w.xin[:, par, c * CH:(c + 1) * CH],
                                              ident[:, :])
                ins.then_inc(x_turned, 1)

            def up(i, par, half):
                e = expert_of(i)
                pe.wait_ge(xT_out, i + 3)
                pe.wait_ge(h_done, i + 1)
                for k in range(2):
                    for n in range(2):
                        ins = nc.tensor.matmul(banks[:, 2 + 2 * par + n, 0:EF], w.sxT[:, par, k, :],
                                               w.gu[:, bass.ds(e, 1), k, n * EF:(n + 1) * EF].rearrange("p o f -> p (o f)"),
                                               start=(k == 0), stop=(k == 1))
                ins.then_inc(gu_done, 1)

            def turn_hidden(i, par, half):
                pe.wait_ge(h_done, i + 3)
                pe.wait_ge(hT_out, i + 1)
                for f in range(NF):
                    ins = nc.tensor.transpose(banks[:, 6, f * P:(f + 1) * P], w.h[:, par, f * P:(f + 1) * P], ident[:, :])
                ins.then_inc(h_turned, 1)

            def down(i, par, half):
                e = expert_of(i)
                pe.wait_ge(hT_out, i + 2)
                pe.wait_ge(y_out, i + 1)
                for f in range(NF):
                    ins = nc.tensor.matmul(banks[:, 7, 0:C], w.ehT[:, par, f, :],
                                           w.dn[:, bass.ds(e, 1), f, :].rearrange("p o c -> p (o c)"),
                                           start=(f == 0), stop=(f == NF - 1))
                ins.then_inc(down_done, 1)

            pe.sem_inc(x_turned, 2)
            pe.sem_inc(gu_done, 2)
            pe.sem_inc(h_turned, 2)
            pe.sem_inc(down_done, 2)
            pe.wait_ge(w.experts_loaded, 16 * (len(w.expert_loads) + len(w.last_loads)))
            pipeline(pe, SLOT_TILES, ((turn, 0), (up, 1), (turn_hidden, 2), (down, 3)))

        @block.scalar
        def _(act):
            def x_evacuate(i, par, half):
                act.wait_ge(x_turned, i + 3)
                act.wait_ge(gu_done, i + 1)
                for c in range(2):
                    ins = nc.scalar.activation(w.sxT[:, par, c, :], banks[0:CH, par, c * P:(c + 1) * P],
                                               ACT.Identity if w.nw2 is not None else ACT.Copy,
                                               scale=1.0 if w.nw2 is None else w.nw2[:, c:c + 1])
                ins.then_inc(xT_out, 1)

            def gate(i, par, half):
                act.wait_ge(gu_done, i + 3)
                act.wait_ge(h_done, i + 1)
                nc.scalar.activation(w.sg[:, par, :], banks[:, 2 + 2 * par, 0:EF], ACT.Silu).then_inc(silu_done, 1)

            def y_evacuate(i, par, half):
                act.wait_ge(down_done, i + 3)
                if not (isinstance(half, int) and half == 0):
                    act.wait_ge(y_stored[par], half * 16)
                nc.scalar.activation(w.y[:, par, :], banks[:, 7, 0:C], ACT.Copy).then_inc(y_out, 1)

            act.sem_inc(xT_out, 2)
            act.sem_inc(y_out, 1)
            pipeline(act, SLOT_TILES, ((x_evacuate, 0), (gate, 1), (y_evacuate, 3)))

        @block.vector
        def _(dve):
            def hidden(i, par, half):
                dve.wait_ge(silu_done, i + 1)
                dve.wait_ge(h_turned, i + 1)
                nc.vector.tensor_tensor(w.h[:, par, :], w.sg[:, par, :], banks[:, 3 + 2 * par, 0:EF],
                                        ALU.mult).then_inc(h_done, 1)

            def h_evacuate(i, par, half):
                dve.wait_ge(h_turned, i + 3)
                dve.wait_ge(down_done, i + 1)
                nc.vector.tensor_copy(w.ehT[:, par, :, :].rearrange("p f t -> p (f t)"),
                                      banks[:, 6, 0:NF * P]).then_inc(hT_out, 1)

            dve.sem_inc(h_done, 2)
            dve.sem_inc(hT_out, 1)
            pipeline(dve, SLOT_TILES, ((hidden, 1), (h_evacuate, 2)))

            chain = Chain(dve, summed)
            for q in range(TILES // 2):
                dve.wait_ge(gathered[q], 64)
                for k in range(2):
                    for t in (2 * q, 2 * q + 1):
                        chain.free(nc.vector.scalar_tensor_tensor(
                            env.X[:, t, :], w.picked_y[:, 2 * t + k, :], w.weight[:, t, k:k + 1], env.X[:, t, :],
                            ALU.mult, ALU.add))
                    chain.wait()
            if w.shared:
                dve.wait_ge(shared_out, 32)
                chain(nc.vector.tensor_tensor(env.X[:, :, :], env.X[:, :, :], w.shared_y[:, :, :], ALU.add))

        @block.gpsimd
        def _(pool):
            if w.shared:
                scatter(nc, env, w, scattered)
            done = SHARED_FIRST + SORTED_TILES[E] if w.shared else SLOT_TILES
            pool.wait_ge(y_stored[0], 16 * ((done + 1) // 2))
            pool.wait_ge(y_stored[1], 16 * (done // 2))
            for a in range(PICKS):
                nc.gpsimd.indirect_dma_start(
                    w.picked_y[:, a, :], None, env.slots_out[:, :],
                    bass.IndirectOffsetOnAxis(ap=w.slot_index[:, a:a + 1], axis=0)).then_inc(gathered[a // 4], 16)


class Env:
    pass


def build(nc, d, out):
    ctx = ExitStack()
    env = Env()
    env.names = {}

    def allocator(stack):
        def sb(name, shape, dt=F32):
            return stack.enter_context(nc.sbuf_tensor(unique(env.names, name), shape, dt))
        return sb

    with ctx:
        sb = allocator(ctx)
        env.banks = ctx.enter_context(nc.psum_tensor("banks", [P, 8, BANK], F32))
        env.X, env.R, env.xn = sb("X", [P, TILES, C]), sb("R", [P, PT, C]), sb("xn", [P, PT, C])
        env.ident, env.mask = sb("ident", [P, P]), sb("mask", [P, P])
        env.ident16, env.mask16 = sb("ident16", [P, P], BF16), sb("mask16", [P, 2, P], BF16)
        env.ones, env.iota = sb("ones", [1, P]), sb("iota", [P, SLOT_TILES + 1])
        env.above16, env.ones16 = sb("above16", [P, P], BF16), sb("ones16", [P, P], BF16)
        env.zeros = sb("zeros", [P, C])
        env.slots_in = nc.dram_tensor("slots_in", (SLOT_TILES * P, C), F32, kind="Internal").ap()
        env.slots_out = nc.dram_tensor("slots_out", (SLOT_TILES * P, C), F32, kind="Internal").ap()
        env.slots_zeroed = nc.alloc_semaphore(name="slots_zeroed")
        env.s = Scratch(sb)

        with stage(nc, env.names) as (block, sem):
            loaded, cast, cleared = sem("loaded"), sem("cast"), sem("cleared")

            @block.sync
            def _(sp):
                for dst, src in ((env.X[:], d["x"]), (env.ident[:], d["ident"]), (env.mask[:], d["mask"]),
                                 (env.iota[:], d["iota"])):
                    sp.dma_start(dst, src).then_inc(loaded, 16)
                sp.wait_ge(loaded, 64)

            @block.vector
            def _(dve):
                nc.vector.memset(env.banks[:, :, :].rearrange("p a b -> p (a b)"), 0.0).then_inc(cleared, 1)
                nc.vector.memset(env.ones[:, :], 1.0).then_inc(cleared, 1)
                nc.vector.memset(env.zeros[:, :], 0.0).then_inc(cleared, 1)
                nc.vector.memset(env.ones16[:, :], 1.0).then_inc(cleared, 1)
                dve.wait_ge(loaded, 64)
                nc.vector.tensor_copy(env.ident16[:, :], env.ident[:, :]).then_inc(cast, 1)
                nc.vector.tensor_copy(env.mask16[:, :, :], env.mask[:, None, :].to_broadcast([P, 2, P])).then_inc(cast, 1)
                nc.vector.tensor_scalar(env.above16[:, :], env.mask[:, :], 0.0, None, ALU.is_lt).then_inc(cast, 1)
                dve.wait_ge(cast, 3)
                dve.wait_ge(cleared, 4)

        def attention_buffers(w, sb):
            w.Pr, w.PT = sb("Pr", [P, 3, 2, TOKENS]), sb("PT", [P, 4, 4, P])
            w.nmax, w.rsum = sb("nmax", [P, 4, 2]), sb("rsum", [P, 2, HEADS])
            w.Os = sb("Os", [P, 2, 3, P])
            w.On, w.OT, w.xT = sb("On", [P, 2, C]), sb("OT", [CH + 1, 2, PN]), sb("xT", [CH + 1, 2, PN])

        def loader(w, sb, layer):
            w.loads, w.ffn_loads, w.late_loads = [], [], []
            w.ffn_loaded = nc.alloc_semaphore(name=layer + "_ffn_loaded")

            def load(name, shape, key, ffn=False):
                t = sb(name, shape)
                (w.ffn_loads if ffn else w.loads).append((t[:], d[key]))
                return t
            return load

        for layer, windows in (("L0", True), ("L1", False)):
            with ExitStack() as stack:
                sb, w = allocator(stack), Env()
                attention_buffers(w, sb)
                load = loader(w, sb, layer)
                w.wq, w.wk = load("wq", [CH + 1, 2, C], layer + "_wq"), load("wk", [CH + 1, 2, 6 * P], layer + "_wk")
                w.wv, w.wo = load("wv", [CH + 1, 2, C], layer + "_wv"), load("wo", [CH + 1, 2, C], layer + "_wo")
                w.hot = load("hot", [P, WINDOWS * WN if windows else TOKENS], layer + "_hot")
                w.qslot, w.odd = load("qslot", [CH, 2, HD], "qslot"), load("odd", [CH, 2], "odd")
                w.bd, w.qT = sb("bd", [CH, 2, SIDE, 2, 32]), sb("qT", [CH, 2, PN])
                w.Q = sb("Q", [P, HEADS, PN])
                w.in_rows = w.out_rows = BIASED
                w.kv_heads = HEADS
                if windows:
                    w.win = load("win", [CH, 2, SIDE, 16], layer + "_win")
                    w.kpad = load("kpad", [P, 6], layer + "_kpad")
                    w.nw, w.nb = load("nw", [CH, 2], "L0_ln1_w"), load("nb", [CH, 2], "L0_ln1_b")
                    w.fnw, w.fnb = load("fnw", [CH, 2], "L0_ln2_w", True), load("fnb", [CH, 2], "L0_ln2_b", True)
                    w.w1 = load("w1", [CH + 1, 2, FF], "L0_w1", True)
                    w.w2, w.b2 = load("w2", [P, FF // P, C], "L0_w2", True), load("b2", [1, C], "L0_b2", True)
                    w.K, w.V = sb("K", [P, 6, PAIR, WINDOWS * WN]), sb("V", [98, 8 * PAIR, HEADS, VW])
                    w.xw, w.hT = sb("xw", [CH + 1, 2, PAIR, WINDOWS * WN]), sb("hT", [P, FF // P, PN])
                else:
                    w.win = sb("win", [CH, 2, SIDE, 16])
                    w.rel, w.shrink = load("rel", [63, 2, CH], "L1_rel"), load("shrink", [63, TOKENS], "shrink")
                    w.gavg = load("gavg", [CH, CH], "gavg")
                    w.K, w.V = sb("K", [P, 6, PAIR, TOKENS]), sb("V", [P, PT, HEADS, VW])
                    w.gst, w.gmv = sb("gst", [CH, 4, 6]), sb("gmv", [CH, 4, 2])
                    w.ga, w.gv, w.gscale, w.gbias = (sb(n, [CH, 4]) for n in ("ga", "gv", "gscale", "gbias"))
                relative_setup(nc, env, w, windows)
                with nc.Fori(0, IMAGES // PAIR) as ip:
                    relative_project(nc, env, w, ip, windows)
                    attend(nc, env, w, "windows" if windows else "full")
                    if windows:
                        feed_forward(nc, env, w, ip, False)
                    else:
                        with stage(nc, env.names) as (block, sem):
                            steps = sem("steps")

                            @block.vector
                            def _(dve):
                                store_residual(nc, Chain(dve, steps), env, ip, False)

        for layer in ("L2a", "L2f", "L3a"):
            experts_stack = ExitStack()
            x = expert_buffers(allocator(experts_stack), nc, d, layer) if layer != "L2a" else None
            with ExitStack() as stack:
                sb, w = allocator(stack), Env()
                attention_buffers(w, sb)
                load = loader(w, sb, layer)
                w.kv_heads = 3 if layer == "L2f" else HEADS
                w.wqk = load("wqk", [CH + 1, 2, 2 * C if layer == "L2a" else 4 * C], layer + "_wqk")
                w.wv = load("wv", [CH + 1, 2, w.kv_heads * HD], layer + "_wv")
                w.wo, w.own = load("wo", [CH + 1, 2, C], layer + "_wo"), load("own", [CH, 6], "own")
                w.in_rows = w.out_rows = BIASED if layer == "L2a" else (CH, CH)
                if layer == "L2f":
                    w.Q = x.gu[:, x.experts - 4:, :, :].rearrange("p e k f -> p (e k f)").rearrange("p (h n) -> p h n", h=HEADS)
                else:
                    w.Q = sb("Q", [CH, HEADS, PN])
                w.K = sb("K", [CH, 2, PN])
                w.V = sb("V", [P, PT, w.kv_heads, VW])
                w.nw = None
                if layer != "L2a":
                    w.nw = load("nw", [CH, 2], layer + "_norm1")
                    w.cos, w.sin = load("cos", [CH, TOKENS], "cos"), load("sin", [CH, TOKENS], "sin")
                    w.qT, w.rb = sb("qT", [CH, 2, PN]), sb("rb", [CH, PN])
                if layer == "L3a":
                    w.fnw = load("fnw", [CH, 2], "L3a_norm2", True)
                    w.w1, w.w3 = load("w1", [CH + 1, 2, FF], "L3a_w1", True), load("w3", [CH + 1, 2, FF], "L3a_w3", True)
                    w.w2 = load("w2", [P, FF // P, C], "L3a_w2", True)
                    w.hT, w.sg = sb("hT", [P, FF // P, PN]), sb("sg", [P, 2, PN])
                if layer != "L2a":
                    w.loads += x.loads
                    w.late_loads, w.late_loaded = x.expert_loads, x.experts_loaded
                if layer == "L2f":
                    x.xT = w.xT
                causal_setup(nc, env, w)
                with nc.Fori(0, IMAGES // PAIR) as ip:
                    causal_project(nc, env, w, ip, layer != "L2a", {"L2a": None, "L2f": 1e-6, "L3a": 1e-5}[layer],
                                   layer != "L2a")
                    attend(nc, env, w, "causal")
                    if layer == "L2a":
                        with stage(nc, env.names) as (block, sem):
                            steps = sem("steps")

                            @block.vector
                            def _(dve):
                                store_residual(nc, Chain(dve, steps), env, ip, False)
                    elif layer == "L2f":
                        route(nc, env, x, ip, True)
                    else:
                        feed_forward(nc, env, w, ip, True)
            if layer == "L3a":
                with ExitStack() as stack:
                    x.xT = allocator(stack)("xT", [CH + 1, 2, PN])
                    with stage(nc, env.names) as (block, sem):
                        filled = sem("filled")

                        @block.gpsimd
                        def _(pool):
                            chain = Chain(pool, filled)
                            chain(nc.gpsimd.memset(x.xT[CH:CH + 1, 1, :], 1.0))
                            for lo, hi in shared_tiles(x.experts):
                                chain(nc.gpsimd.memset(x.tile_expert[:, lo:hi], x.experts))
                    with nc.Fori(0, IMAGES // PAIR) as ip:
                        route(nc, env, x, ip, False)
            if layer != "L2a":
                with ExitStack() as stack:
                    sort_buffers(x, allocator(stack))
                    sort_tokens(nc, env, x)
                with ExitStack() as stack:
                    slot_buffers(x, allocator(stack))
                    experts(nc, env, x)
                nc.clear_and_free_semaphores([x.experts_loaded])
                nc.all_engine_barrier()
            experts_stack.close()

        with stage(nc, env.names) as (block, sem):
            written = sem("written")

            @block.sync
            def _(sp):
                sp.dma_start(out, env.X[:]).then_inc(written, 16)
                sp.wait_ge(written, 16)


def expert_buffers(sb, nc, d, layer):
    x = Env()
    x.experts, name = (16, "L2f") if layer == "L2f" else (8, "L3f")
    n = x.experts
    x.shared = name == "L3f"
    x.stored = n + x.shared
    x.r_rows = BIASED if x.shared else (CH, CH)
    x.wr = sb("wr", [CH + 1, 2, n])
    x.loads = [(x.wr[:], d[name + "_wr"])]
    x.nw2 = None
    if not x.shared:
        x.nw2 = sb("nw2", [CH, 2])
        x.loads.append((x.nw2[:], d["L2f_norm2"]))
    x.gu, x.dn = sb("gu", [CH, x.stored, 2, 2 * EF]), sb("dn", [P, x.stored, EF // P, C])
    x.expert_loads, x.last_loads = [], []
    for e in range(0, x.stored, 4):
        loads = x.last_loads if n == 16 and e == n - 4 else x.expert_loads
        e = slice(e, min(e + 4, x.stored))
        loads.append((x.gu[:, e], d[name + "_gu"][:, e]))
        x.expert_loads.append((x.dn[:, e], d[name + "_dn"][:, e]))
    x.experts_loaded = nc.alloc_semaphore(name=name + "_experts_loaded")
    x.M = sb("M", [P, TILES, C])
    x.expert, x.weight = sb("expert", [P, TILES, 2]), sb("weight", [P, TILES, 2])
    x.logits, x.margin, x.g0, x.g1 = sb("logits", [P, PT, n]), sb("margin", [P, PT]), sb("g0", [P, PT]), sb("g1", [P, PT])
    x.top, x.topi = sb("top", [P, PT, 8]), sb("topi", [P, PT, 8], U32)
    x.slot_index, x.tile_expert = sb("slot_index", [P, PICKS], U32), sb("tile_expert", [1, SLOT_TILES], I32)
    return x


def sort_buffers(x, sb):
    n = x.experts
    x.hit, x.hit16 = sb("hit", [P, PICKS, n]), sb("hit16", [P, PICKS, n], BF16)
    x.sum_a, x.sum_b, x.slots = (sb(name, [P, PICKS, n]) for name in ("sum_a", "sum_b", "slots"))
    x.count, x.ends = sb("count", [P, n], I32), (sb("end_a", [P, n]), sb("end_b", [P, n]))
    x.first, x.slot = sb("first", [P, n]), sb("slot", [P, PICKS])
    x.passed, x.owner = sb("passed", [1, SORTED_TILES[n], n]), sb("owner", [1, SORTED_TILES[n]])


def slot_buffers(x, sb):
    x.xin, x.sxT = sb("xin", [P, 2, C]), sb("sxT", [CH, 2, 2, P])
    x.sg, x.h, x.ehT = sb("sg", [P, 2, EF]), sb("h", [P, 2, EF]), sb("ehT", [P, 2, EF // P, P])
    x.y, x.picked_y = sb("y", [P, 2, C]), sb("picked_y", [P, PICKS, C])
    if x.shared:
        x.shared_y = sb("shared_y", [P, TILES, C])


def _chunked(np, w, b=None):
    a = np.zeros((CH + 1, 2, w.shape[1]), np.float32)
    a[0:CH] = w.reshape(2, CH, -1).transpose(1, 0, 2)
    if b is not None:
        a[CH, 1] = b
    return a


def _swapped(w):
    return w.reshape(w.shape[0], -1, 2)[:, :, ::-1].reshape(w.shape)


def _columns(v):
    return v.reshape(2, CH).T


def _padded_keys(np, a):
    out = np.zeros(a.shape[:-1] + (6, 2, 4, HD), np.float32)
    out[..., 1, :] = a.reshape(a.shape[:-1] + (6, 2, HD))
    return out.reshape(a.shape[:-1] + (6 * P,))


def _one_hot_rows(np, positions):
    hot = np.zeros((2, 64, len(positions)), np.float32)
    for j, (r, c) in enumerate(positions):
        hot[:, r, j] = 1
        hot[:, 32 + c, j] = 1
    return hot.reshape(P, -1)


def _shrink(np, n_in, n_out):
    inv = np.float32(n_in) / np.float32(n_out)
    at = (np.arange(n_out, dtype=np.float32) + np.float32(0.5)) * inv - np.float32(0.5)
    x = np.abs(at[None, :] - np.arange(n_in, dtype=np.float32)[:, None]) / max(inv, np.float32(1))
    w = np.maximum(0, 1 - x)
    return (w / w.sum(0, keepdims=True)).astype(np.float32)


def _constants(np):
    c = {}
    c["ident"] = np.eye(P, dtype=np.float32)
    c["mask"] = np.triu(np.full((P, P), -1e30, np.float32), 1)
    c["iota"] = np.tile(np.arange(SLOT_TILES + 1, dtype=np.float32), (P, 1))
    qslot = np.zeros((6, HD, 2, HD), np.float32)
    for h in range(6):
        qslot[h, :, h % 2, :] = QSCALE * np.eye(HD)
    c["qslot"] = qslot.reshape(CH, 2, HD)
    odd = np.zeros((6, HD, 2), np.float32)
    for h in range(6):
        odd[h, :, h % 2] = 1
    c["odd"] = odd.reshape(CH, 2)
    c["gavg"] = np.kron(np.eye(16), np.full((6, 6), 1 / 6)).astype(np.float32)
    window = [(r, k) for r in range(WS) for k in range(WS)]
    c["L0_hot"] = _one_hot_rows(np, window * WINDOWS)
    c["L1_hot"] = _one_hot_rows(np, [(r, k) for r in range(SIDE) for k in range(SIDE)])
    at = np.arange(SIDE)[:, None] - np.arange(SIDE)[None, :] + SIDE - 1
    c["shrink"] = _shrink(np, 63, 2 * SIDE - 1)[:, at.reshape(-1)]
    inv = (1.0 / 10000.0 ** (np.arange(0, HD, 2, dtype=np.float32) / HD)).astype(np.float32)
    ang = np.arange(TOKENS, dtype=np.float32)[:, None] * inv[None, :]
    cos, sin = np.cos(ang), np.sin(ang)
    cos, sin = np.stack([cos, cos], -1).reshape(TOKENS, HD), np.stack([-sin, sin], -1).reshape(TOKENS, HD)
    c["cos"], c["sin"] = (np.tile(a.T, (CH // HD, 1)).astype(np.float32) for a in (cos, sin))
    c["own"] = np.kron(np.eye(CH // HD), np.full((HD, 1), QSCALE)).astype(np.float32)
    return c


def _lay_out(np, i):
    a = _constants(np)
    a["x"] = i["x"].reshape(-1, C)
    for layer, p, names in (("L0", "L0_conv_", ("qkv_w", "qkv_b", "proj_w", "proj_b")),
                            ("L1", "L1_conv_", ("w_qkv", "b_qkv", "w_proj", "b_proj"))):
        w, b, wo, bo = (i[p + n] for n in names)
        a[layer + "_wq"] = _chunked(np, w[:, 0:C], b[0:C])
        a[layer + "_wk"] = _chunked(np, _padded_keys(np, w[:, C:2 * C]), _padded_keys(np, b[C:2 * C]))
        a[layer + "_wv"] = _chunked(np, w[:, 2 * C:], b[2 * C:])
        a[layer + "_wo"] = _chunked(np, wo, bo)
    a["L0_kpad"] = _padded_keys(np, i["L0_conv_qkv_b"][C:2 * C]).reshape(6, P).T
    row = np.arange(SIDE) % WS
    at = row[:, None] - np.arange(WS)[None, :] + WS - 1
    win = np.zeros((6, HD, 2, SIDE, 16), np.float32)
    for n, rel in enumerate((i["L0_conv_rel_pos_h"], i["L0_conv_rel_pos_w"])):
        win[:, :, n, :, 0:WS] = rel[at].transpose(2, 0, 1)[None]
    a["L0_win"] = win.reshape(CH, 2, SIDE, 16)
    a["L1_rel"] = np.stack([np.tile(i["L1_conv_rel_pos_" + n], (1, 6)) for n in "hw"], 1)
    for n in ("ln1_w", "ln1_b", "ln2_w", "ln2_b"):
        a["L0_" + n] = _columns(i["L0_conv_" + n])
    a["L0_w1"] = _chunked(np, i["L0_conv_fc1_w"], i["L0_conv_fc1_b"])
    a["L0_w2"] = i["L0_conv_fc2_w"].reshape(FF // P, P, C).transpose(1, 0, 2)
    a["L0_b2"] = i["L0_conv_fc2_b"].reshape(1, C)
    a["L2a_wqk"] = _chunked(np, np.concatenate([i["L2_attn_w" + n].T for n in "qk"], 1),
                            np.concatenate([i["L2_attn_b" + n] for n in "qk"]))
    a["L2a_wv"] = _chunked(np, i["L2_attn_wv"].T, i["L2_attn_bv"])
    a["L2a_wo"] = _chunked(np, i["L2_attn_wo"].T, i["L2_attn_bo"])
    q, k, v = np.split(i["L2_ffn_w_qkv"], [C, C + 3 * HD], 1)
    k = np.repeat(k.reshape(C, 3, HD), HEADS // 3, 1).reshape(C, C)
    a["L2f_wqk"] = _chunked(np, np.concatenate([q, _swapped(q), k, _swapped(k)], 1))
    a["L2f_wv"] = _chunked(np, v)
    a["L2f_wo"] = _chunked(np, i["L2_ffn_w_out"])
    a["L2f_norm1"], a["L2f_norm2"] = _columns(i["L2_ffn_norm1_w"]), _columns(i["L2_ffn_norm2_w"])
    a["L2f_wr"] = _chunked(np, i["L2_ffn_w_router"])
    a["L2f_gu"] = i["L2_ffn_w_gate_up"].reshape(16, 2, CH, 2 * EF).transpose(2, 0, 1, 3)
    a["L2f_dn"] = i["L2_ffn_w_down"].reshape(16, EF // P, P, C).transpose(2, 0, 1, 3)
    q, k, v = (i["L3_attn_w_" + n].T for n in "qkv")
    a["L3a_wqk"] = _chunked(np, np.concatenate([q, _swapped(q), k, _swapped(k)], 1))
    a["L3a_wv"] = _chunked(np, v)
    a["L3a_wo"] = _chunked(np, i["L3_attn_w_o"].T)
    a["L3a_norm1"], a["L3a_norm2"] = _columns(i["L3_attn_w_ln1"]), _columns(i["L3_attn_w_ln2"])
    a["L3a_w1"], a["L3a_w3"] = _chunked(np, i["L3_attn_w_ffn_w1"].T), _chunked(np, i["L3_attn_w_ffn_w3"].T)
    a["L3a_w2"] = i["L3_attn_w_ffn_w2"].T.reshape(FF // P, P, C).transpose(1, 0, 2)
    a["L3f_wr"] = _chunked(np, i["L3_ffn_W_router"], i["L3_ffn_expert_bias"])
    gate = np.concatenate([i["L3_ffn_Wg_r"], i["L3_ffn_Wg_s"]], 0)
    up = np.concatenate([i["L3_ffn_Wu_r"], i["L3_ffn_Wu_s"]], 0)
    down = np.concatenate([i["L3_ffn_Wd_r"], i["L3_ffn_Wd_s"]], 0)
    a["L3f_gu"] = np.concatenate([gate, up], 2).reshape(9, 2, CH, 2 * EF).transpose(2, 0, 1, 3)
    a["L3f_dn"] = down.reshape(9, EF // P, P, C).transpose(2, 0, 1, 3)
    return {k: np.ascontiguousarray(v) for k, v in a.items()}


def kernel(**inputs):
    import numpy as np
    import concourse.bacc as bacc
    from concourse.bass_utils import run_bass_kernel_spmd as run

    nc = bacc.Bacc("TRN2", target_bir_lowering=False, num_devices=1)
    arrays = _lay_out(np, {k: np.asarray(v) for k, v in inputs.items()})
    dram = {k: nc.dram_tensor("in_" + k, v.shape, F32, kind="ExternalInput").ap() for k, v in arrays.items()}
    dram["x"] = dram["x"].rearrange("(t p) c -> p t c", p=P)
    out = nc.dram_tensor("out", (IMAGES * TOKENS, C), F32, kind="ExternalOutput").ap()
    build(nc, dram, out.rearrange("(t p) c -> p t c", p=P))
    r = run(nc, [{"in_" + k: v for k, v in arrays.items()}], core_ids=[0])
    return r.results[0]["out"].reshape(IMAGES, SIDE, SIDE, C)
```

```python
from contextlib import ExitStack, contextmanager

import concourse.bass as bass
from concourse import mybir

F32 = mybir.dt.float32
BF16 = mybir.dt.bfloat16
I32 = mybir.dt.int32
U32 = mybir.dt.uint32
ALU = mybir.AluOpType
ACT = mybir.ActivationFunctionType
AX = mybir.AxisListType

IMAGES, SIDE, C = 4, 16, 192
TOKENS = SIDE * SIDE
P = 128
TILES = IMAGES * TOKENS // P
PAIR = 2
PT = PAIR * TOKENS // P
PN = PAIR * TOKENS
HEADS, HD = 12, 16
CH = C // 2
VW = HD + 1
WS = 14
WN = WS * WS
WINDOWS = 4
QSCALE = HD ** -0.5
FF = 768
EF = 384
BANK = 512
RSQRT_SEED = 0x5F3759DF
PICKS = 2 * TILES
SORTED_TILES = {E: PICKS + E - 1 for E in (16, 8)}
SLOT_TILES = SORTED_TILES[16]
assert SLOT_TILES == SORTED_TILES[8] + TILES
SHARED_FIRST = TILES // 2
WINDOW_BOX = [(0, 14, 0, 14), (0, 14, 14, 2), (14, 2, 0, 14), (14, 2, 14, 2)]
WINDOW_AT = [0, 196, 224, 252]


class Chain:

    def __init__(self, eng, sem):
        self.eng, self.sem, self.n = eng, sem, 0

    def free(self, ins):
        self.n += 1
        ins.then_inc(self.sem, 1)

    def wait(self):
        self.eng.wait_ge(self.sem, self.n)

    def __call__(self, ins):
        self.free(ins)
        self.wait()


def unique(names, name):
    names[name] = names.get(name, 0) + 1
    return name if names[name] == 1 else f"{name}_{names[name]}"


@contextmanager
def stage(nc, names):
    sems = []

    def sem(name):
        sems.append(nc.alloc_semaphore(name=unique(names, name)))
        return sems[-1]

    with nc.Block() as block:
        yield block, sem
    nc.clear_and_free_semaphores(sems)
    nc.all_engine_barrier()


class Scratch:

    def __init__(self, sb):
        self.st = sb("norm_stats", [P, PT, 6])
        self.mv = sb("norm_mean_var", [P, PT, 2])
        self.v = sb("norm_v", [P, PT])
        self.a = sb("norm_a", [P, PT])
        self.w = sb("norm_w", [P, PT])
        self.y, self.y2 = sb("norm_rstd", [P, PT]), sb("norm_rstd_both", [P, PT])


def rsqrt_steps(nc, chain, y, src, v, a, eps):
    chain.free(nc.vector.tensor_scalar(v, src, eps, None, ALU.add))
    yield
    chain.wait()
    chain.free(nc.vector.tensor_scalar(a.bitcast(I32), v.bitcast(I32), 1, None, ALU.logical_shift_right))
    yield
    chain.wait()
    chain.free(nc.vector.tensor_scalar(y.bitcast(I32), a.bitcast(I32), -1, RSQRT_SEED, ALU.mult, ALU.add))
    yield
    for _ in range(3):
        chain.wait()
        chain.free(nc.vector.scalar_tensor_tensor(a, y, -0.5, y, ALU.mult, ALU.mult))
        yield
        chain.wait()
        chain.free(nc.vector.tensor_tensor(a, a, v, ALU.mult))
        yield
        chain.wait()
        chain.free(nc.vector.scalar_tensor_tensor(y, a, 1.5, y, ALU.add, ALU.mult))
        yield


def rsqrt(nc, chain, y, src, v, a, eps):
    for _ in rsqrt_steps(nc, chain, y, src, v, a, eps):
        pass
    chain.wait()


def normalise_steps(nc, chain, s, dst, src, eps, centre, inner=None, tiles=(0, PT)):
    r = slice(*tiles)
    for t in range(*tiles):
        chain.free(nc.vector.bn_stats(s.st[:, t, :], src[:, t, :]))
        yield
    chain.wait()
    for t in range(*tiles):
        chain.free(nc.vector.bn_aggr(s.mv[:, t, :], s.st[:, t, :]))
    yield
    chain.wait()
    if centre:
        yield from rsqrt_steps(nc, chain, s.y[:, r], s.mv[:, r, 1], s.v[:, r], s.a[:, r], eps)
    else:
        chain.free(nc.vector.tensor_tensor(s.a[:, r], s.mv[:, r, 0], s.mv[:, r, 0], ALU.mult))
        yield
        chain.wait()
        chain.free(nc.vector.tensor_tensor(s.w[:, r], s.a[:, r], s.mv[:, r, 1], ALU.add))
        yield
        chain.wait()
        yield from rsqrt_steps(nc, chain, s.y[:, r], s.w[:, r], s.v[:, r], s.a[:, r], eps)
    chain.wait()
    for t in range(*tiles):
        if centre:
            chain.free(nc.vector.tensor_scalar(dst[:, t, :], src[:, t, :], s.mv[:, t, 0:1], s.y[:, t:t + 1],
                                               ALU.subtract, ALU.mult))
        else:
            chain.free(nc.vector.tensor_scalar(dst[:, t, :], src[:, t, :], s.y[:, t:t + 1], None, ALU.mult))
        yield
    if inner is not None:
        chain.free(nc.vector.tensor_tensor(s.a[:, r], s.y[:, r], s.y[:, r], ALU.mult))
        yield
        chain.wait()
        chain.free(nc.vector.tensor_tensor(s.w[:, r], s.mv[:, r, 1], s.a[:, r], ALU.mult))
        yield
        chain.wait()
        yield from rsqrt_steps(nc, chain, s.y2[:, r], s.w[:, r], s.v[:, r], s.a[:, r], inner)


def normalise(nc, chain, s, dst, src, eps, centre, inner=None, tiles=(0, PT)):
    for _ in normalise_steps(nc, chain, s, dst, src, eps, centre, inner, tiles):
        pass
    chain.wait()


def load_function(nc, env, function):
    nc.scalar.activation(env.unused[:, :], env.zeros[:, 0:1], function)


def turn_second_image(nc, pe, banks, src, ident, turned, normed):
    for c in range(2):
        for t in range(2):
            nc.tensor.transpose(banks[0:CH, c, t * P:(t + 1) * P], src[:, t, c * CH:(c + 1) * CH], ident[:, :])
    pe.wait_ge(normed, 1)
    for c in range(2):
        for t in range(2, PT):
            ins = nc.tensor.transpose(banks[0:CH, c, t * P:(t + 1) * P], src[:, t, c * CH:(c + 1) * CH], ident[:, :])
        ins.then_inc(turned, 1)


def turn_tiles(nc, banks, src, ident, turned, pe=None, tile_ready=None):
    for c in range(2):
        for t in range(PT):
            if c == 0 and tile_ready is not None:
                pe.wait_ge(tile_ready, t + 1)
            ins = nc.tensor.transpose(banks[0:CH, c, t * P:(t + 1) * P], src[:, t, c * CH:(c + 1) * CH], ident[:, :])
        ins.then_inc(turned, 1)


def dense(nc, out, lhs, rhs, n_rows=(CH, CH), pe=None, chunk_ready=None):
    for k, rows in enumerate(n_rows):
        if chunk_ready is not None:
            pe.wait_ge(chunk_ready, k + 1)
        ins = nc.tensor.matmul(out, lhs(k, rows), rhs(k, rows), start=(k == 0), stop=(k == 1))
    return ins


BIASED = (CH, CH + 1)


def start_loads(sp, w):
    if not w.early:
        for dst, src in w.loads:
            sp.dma_start(dst, src).then_inc(w.loaded, 16)
    for dst, src in w.ffn_loads:
        sp.dma_start(dst, src).then_inc(w.ffn_loaded, 16)
    for dst, src in w.late_loads:
        sp.dma_start(dst, src).then_inc(w.late_loaded, 16)


def relative_setup(nc, env, w, windows):
    with stage(nc, env.names) as (block, sem):
        loaded, win_made, steps, filled = w.loaded, sem("win_made"), sem("steps"), sem("filled")

        @block.sync
        def _(sp):
            start_loads(sp, w)
            for later in w.prefetch:
                for dst, src in later.loads:
                    sp.dma_start(dst, src).then_inc(later.loaded, 16)
            if not windows:
                sp.dma_start(env.slots_in.rearrange("(t p) c -> p t c", p=P),
                             env.zeros[:, None, :].to_broadcast([P, SLOT_TILES, C])).then_inc(env.slots_zeroed, 16)
            sp.wait_ge(loaded, 16 * len(w.loads))

        @block.gpsimd
        def _(pool):
            chain = Chain(pool, filled)
            chain(nc.gpsimd.memset(w.V[:, :, :, HD:VW], 1.0))
            chain(nc.gpsimd.memset(w.xT[CH:CH + 1, 1, :], 1.0))
            chain(nc.gpsimd.memset(w.OT[CH:CH + 1, 1, :], 1.0))
            chain(nc.gpsimd.memset(w.Q[64:P, 0::2, :], 0.0))
            if windows:
                chain(nc.gpsimd.memset(w.xw[0:CH, :, :, :], 0.0))
                chain(nc.gpsimd.memset(w.xw[CH:CH + 1, 1, :, :], 1.0))

        if windows:
            @block.scalar
            def _(act):
                act.wait_ge(loaded, 16 * len(w.loads))
                for g in range(6):
                    nc.scalar.activation(w.K[:, g, 1, :], w.hot[:, :], ACT.Identity, bias=w.kpad[:, g:g + 1])

        if not windows:
            @block.tensor
            def _(pe):
                pe.wait_ge(loaded, 16 * len(w.loads))
                for n in range(2):
                    ins = nc.tensor.matmul(env.banks[0:CH, n, 0:TOKENS], w.rel[:, n, :], w.shrink[:, :],
                                           start=True, stop=True)
                ins.then_inc(win_made, 1)

        @block.vector
        def _(dve):
            chain = Chain(dve, steps)
            if windows:
                normalise(nc, chain, env.ahead_s, env.ahead, env.X[:, 0:PT, :], 1e-5, True)
            chain.free(nc.vector.memset(w.Q[0:64, 1::2, :], 0.0))
            dve.wait_ge(loaded, 16 * len(w.loads))
            if not windows:
                dve.wait_ge(win_made, 1)
                for n in range(2):
                    chain.free(nc.vector.tensor_copy(w.win[:, n, :, :].rearrange("p a b -> p (a b)"),
                                                     env.banks[0:CH, n, 0:TOKENS]))
                chain.wait()
            for s in range(2):
                chain.free(nc.vector.tensor_copy(w.bd[:, 0, :, s, 16:32], w.qslot[:, None, s, :].to_broadcast([CH, SIDE, HD])))
                chain.free(nc.vector.memset(w.bd[:, 1, :, s, 16:32], 0.0))
                for n in range(2):
                    chain.free(nc.vector.tensor_scalar(w.bd[:, n, :, s, 0:16], w.win[:, n, :, :],
                                                       w.odd[:, s:s + 1], None, ALU.mult))
            if windows:
                for g in range(6):
                    chain.free(nc.vector.tensor_scalar(w.K[:, g, 0, :], w.hot[:, :], w.kpad[:, g:g + 1], None,
                                                       ALU.add))
            chain.wait()


def relative_project(nc, env, w, ip, windows):
    R, banks, ident = env.R, env.banks, env.ident
    n_vjobs = 8 if windows else PT
    with stage(nc, env.names) as (block, sem):
        steps = sem("steps")
        turned, xT_ready = sem("turned"), sem("xT_ready")
        stats_ready, group_ready, affine_ready = sem("stats_ready"), sem("group_ready"), sem("affine_ready")
        xw_ready, xw_steps = sem("xw_ready"), sem("xw_steps")
        a_done, a_out, k_done, k_out = sem("a_done"), sem("a_out"), sem("k_done"), sem("k_out")
        odd_out, copied = sem("odd_out"), sem("copied")

        def queries_out(copy, g, half):
            rows = slice(64 * half, 64 * half + 64)
            bank, q = banks[rows, (2 + n_vjobs + g) % 4, :], w.Q[rows, 2 * g + half, :]
            if not windows:
                return copy(q, bank)
            for n, (h0, nh, w0, nw) in enumerate(WINDOW_BOX):
                src = bank.rearrange("p (m a b) -> p m a b", m=PAIR, b=SIDE)[:, :, h0:h0 + nh, w0:w0 + nw]
                dst = q.rearrange("p (m t) -> p m t", m=PAIR)[:, :, WINDOW_AT[n]:WINDOW_AT[n] + nh * nw]
                ins = copy(dst.rearrange("p m (a b) -> p m a b", b=nw), src)
            return ins

        @block.vector
        def _(dve):
            chain = Chain(dve, steps)
            if not windows:
                nc.vector.tensor_copy(R[:, :, :], env.X[:, bass.ds(ip * PT, PT), :]).then_inc(copied, 1)
                for c in range(2):
                    dve.wait_ge(turned, c + 1)
                    for m in range(PAIR):
                        chain.free(nc.vector.bn_stats(w.gst[:, c * 2 + m, :], banks[0:CH, c, m * TOKENS:(m + 1) * TOKENS]))
                chain.wait()
                for j in range(4):
                    chain.free(nc.vector.bn_aggr(w.gmv[:, j, :], w.gst[:, j, :]))
                chain.wait()
                chain(nc.vector.tensor_tensor(w.ga[:, :], w.gmv[:, :, 0], w.gmv[:, :, 0], ALU.mult))
                chain(nc.vector.tensor_tensor(w.gmv[:, :, 1], w.gmv[:, :, 1], w.ga[:, :], ALU.add))
                dve.sem_inc(stats_ready, 1)
                dve.wait_ge(group_ready, 1)
                chain(nc.vector.tensor_copy(w.gmv[:, :, :].rearrange("p a b -> p (a b)"), banks[0:CH, 2, 0:8]))
                chain(nc.vector.tensor_tensor(w.ga[:, :], w.gmv[:, :, 0], w.gmv[:, :, 0], ALU.mult))
                chain(nc.vector.tensor_tensor(w.gv[:, :], w.gmv[:, :, 1], w.ga[:, :], ALU.subtract))
                rsqrt(nc, chain, w.gscale[:, :], w.gv[:, :], w.gv[:, :], w.ga[:, :], 1e-5)
                chain(nc.vector.scalar_tensor_tensor(w.gbias[:, :], w.gmv[:, :, 0], -1.0, w.gscale[:, :], ALU.mult, ALU.mult))
                dve.sem_inc(affine_ready, 1)
            for g in range(6):
                dve.wait_ge(k_done, g + 1)
                src = banks[:, 4 + g % 4, :]
                if windows:
                    for n, (h0, nh, w0, nw) in enumerate(WINDOW_BOX):
                        real = src.rearrange("p (m a b) -> p m a b", m=PAIR, b=SIDE)[:, :, h0:h0 + nh, w0:w0 + nw]
                        dst = w.K[:, g, :, n * WN:(n + 1) * WN].rearrange("p m (a b) -> p m a b", b=WS)[:, :, 0:nh, 0:nw]
                        hot = w.hot[:, n * WN:(n + 1) * WN].rearrange("p (a b) -> p a b", b=WS)[:, None, 0:nh, 0:nw]
                        ins = nc.vector.tensor_tensor(dst, real, hot.to_broadcast([P, PAIR, nh, nw]), ALU.add)
                else:
                    for m in range(PAIR):
                        ins = nc.vector.tensor_tensor(w.K[:, g, m, :], src[:, m * TOKENS:(m + 1) * TOKENS],
                                                      w.hot[:, :], ALU.add)
                ins.then_inc(k_out, 1)
            for g in range(6):
                dve.wait_ge(a_done, 2 + n_vjobs + g + 1)
                queries_out(nc.vector.tensor_copy, g, 1).then_inc(odd_out, 1)
            dve.wait_ge(odd_out, 6)
            dve.wait_ge(k_out, 6)

        @block.scalar
        def _(act):
            load_function(nc, env, ACT.Identity)
            for c in range(2):
                act.wait_ge(turned, c + 1)
                if windows:
                    nc.scalar.activation(w.xT[0:CH, c, :], banks[0:CH, c, :], ACT.Identity,
                                         bias=w.nb[:, c:c + 1], scale=w.nw[:, c:c + 1]).then_inc(xT_ready, 1)
                else:
                    act.wait_ge(affine_ready, 1)
                    for m in range(PAIR):
                        j = c * 2 + m
                        ins = nc.scalar.activation(w.xT[0:CH, c, m * TOKENS:(m + 1) * TOKENS],
                                                   banks[0:CH, c, m * TOKENS:(m + 1) * TOKENS], ACT.Identity,
                                                   bias=w.gbias[:, j:j + 1], scale=w.gscale[:, j:j + 1])
                    ins.then_inc(xT_ready, 1)
            for a in range(2 + n_vjobs + 6):
                act.wait_ge(a_done, a + 1)
                bank = banks[:, a % 4, :]
                if a < 2:
                    ins = nc.scalar.activation(w.qT[:, a, :], bank[0:CH, :], ACT.Copy)
                elif a < 2 + n_vjobs:
                    j = a - 2
                    if windows:
                        ins = nc.scalar.activation(w.V[0:98, 2 * j:2 * j + 2, :, 0:HD],
                                                   bank[0:98, 0:2 * C].rearrange("p (n h d) -> p n h d", n=2, d=HD), ACT.Copy)
                    else:
                        ins = nc.scalar.activation(w.V[:, j, :, 0:HD], bank[:, 0:C].rearrange("p (h d) -> p h d", d=HD),
                                                   ACT.Copy)
                else:
                    ins = queries_out(nc.scalar.copy, a - 2 - n_vjobs, 0)
                ins.then_inc(a_out, 1)
            act.wait_ge(a_out, 2 + n_vjobs + 6)

        if windows:
            @block.gpsimd
            def _(pool):
                nc.gpsimd.tensor_copy(R[:, :, :], env.X[:, bass.ds(ip * PT, PT), :]).then_inc(copied, 1)
                pool.wait_ge(copied, 1)
                chain = Chain(pool, xw_steps)
                pool.wait_ge(xT_ready, 2)
                for c in range(2):
                    for n, (h0, nh, w0, nw) in enumerate(WINDOW_BOX):
                        for m in range(PAIR):
                            src = w.xT[0:CH, c, m * TOKENS:(m + 1) * TOKENS].rearrange("p (a b) -> p a b", b=SIDE)
                            dst = w.xw[0:CH, c, m, n * WN:(n + 1) * WN].rearrange("p (a b) -> p a b", b=WS)
                            chain(nc.gpsimd.tensor_copy(dst[:, 0:nh, 0:nw], src[:, h0:h0 + nh, w0:w0 + nw]))
                pool.sem_inc(xw_ready, 1)

        @block.tensor
        def _(pe):
            if not windows:
                pe.wait_ge(copied, 1)
            turn_tiles(nc, banks, env.ahead if windows else R, ident, turned)
            if not windows:
                pe.wait_ge(stats_ready, 1)
                nc.tensor.matmul(banks[0:CH, 2, 0:8], w.gavg[:, :], w.gmv[:, :, :].rearrange("p a b -> p (a b)"),
                                 start=True, stop=True).then_inc(group_ready, 1)

            def queries(a):
                pe.wait_ge(xT_ready, a + 1)
                dense(nc, banks[0:CH, a % 4, :], lambda k, r: w.wq[0:r, k, a * CH:(a + 1) * CH],
                      lambda k, r: w.xT[0:r, k, :], BIASED, pe, xT_ready if a == 0 else None).then_inc(a_done, 1)

            def keys(g):
                if g >= 4:
                    pe.wait_ge(k_out, g - 3)
                dense(nc, banks[:, 4 + g % 4, :], lambda k, r: w.wk[0:r, k, g * P:(g + 1) * P],
                      lambda k, r: w.xT[0:r, k, :], BIASED).then_inc(k_done, 1)

            def values(j):
                a = 2 + j
                if a >= 4:
                    pe.wait_ge(a_out, a - 3)
                if not windows:
                    ins = dense(nc, banks[:, a % 4, 0:C], lambda k, r: w.xT[0:r, k, j * P:(j + 1) * P],
                                lambda k, r: w.wv[0:r, k, :], BIASED)
                else:
                    for n in range(2):
                        m, at = divmod((2 * j + n) * 98, WINDOWS * WN)
                        ins = dense(nc, banks[0:98, a % 4, n * C:(n + 1) * C], lambda k, r: w.xw[0:r, k, m, at:at + 98],
                                    lambda k, r: w.wv[0:r, k, :], BIASED)
                ins.then_inc(a_done, 1)

            def relative(g):
                a = 2 + n_vjobs + g
                pe.wait_ge(a_out, a - 3)
                if g >= 4:
                    pe.wait_ge(odd_out, g - 3)
                row, c = 32 * (g % 3), g // 3
                q = w.qT[row:row + 32, c, :].rearrange("p (m a b) -> p m a b", m=PAIR, b=SIDE)
                o = banks[:, a % 4, :].rearrange("p (m a b) -> p m a b", m=PAIR, b=SIDE)
                for r in range(SIDE):
                    for s in range(2):
                        nc.tensor.matmul(o[64 * s:64 * s + 32, :, r, :], w.bd[row:row + 32, 0, r, s, :], q[:, :, r, :],
                                         start=True, stop=True)
                        ins = nc.tensor.matmul(o[64 * s + 32:64 * s + 64, :, :, r], w.bd[row:row + 32, 1, r, s, :],
                                               q[:, :, :, r], start=True, stop=True)
                ins.then_inc(a_done, 1)

            queries(0)
            queries(1)
            for g in range(6):
                keys(g)
            if windows:
                pe.wait_ge(xw_ready, 1)
            for j in range(n_vjobs):
                values(j)
            for g in range(6):
                relative(g)


class Layout:

    def __init__(self, kind, w):
        self.kind, self.w = kind, w
        self.tiles = 3 if kind == "windows" else 2
        self.rows_in = CH if kind == "causal" else P
        self.group = 6 if kind == "causal" else 2

    def rows(self, t):
        return P if self.kind != "windows" else (98, 98, 68)[t]

    def width(self, t):
        return {"windows": WN, "full": TOKENS, "causal": (t + 1) * P}[self.kind]

    def chunk(self):
        return 98 if self.kind == "windows" else P

    def chunks(self, t):
        return self.width(t) // self.chunk()

    def parts(self, t):
        if self.kind != "windows":
            return [(0, P, 0)]
        return [(0, 98, 0)] if t < 2 else [(32 * (n - 1), WINDOW_BOX[n][1] * WINDOW_BOX[n][3], n) for n in (1, 2, 3)]

    def tokens(self, ap, m, t, window):
        if self.kind != "windows":
            return ap[:, m * TOKENS + t * P:m * TOKENS + (t + 1) * P]
        h0, nh, w0, nw = WINDOW_BOX[window]
        if window == 0:
            h0, nh = 7 * t, 7
        a = ap[:, m * TOKENS:(m + 1) * TOKENS].rearrange("p (a b) -> p a b", b=SIDE)
        return a[:, h0:h0 + nh, w0:w0 + nw]

    def q(self, m, t, h, window):
        q = self.w.Q[0:self.rows_in, h, :]
        if self.kind != "windows":
            return self.tokens(q, m, t, window)
        at = m * TOKENS + (98 * t if window == 0 else WINDOW_AT[window])
        return q[:, at:at + (98 if window == 0 else WINDOW_BOX[window][1] * WINDOW_BOX[window][3])]

    def k(self, m, t, h, window):
        g = h // self.group
        if self.kind == "causal":
            return self.w.K[:, g, m * TOKENS:m * TOKENS + self.width(t)]
        if self.kind == "full":
            return self.w.K[:, g, m, :]
        return self.w.K[:, g, m, window * WN:(window + 1) * WN]

    def v(self, m, h, c, window):
        if self.kind == "windows":
            return self.w.V[0:98, m * 8 + window * 2 + c, h, :]
        return self.w.V[:, m * 2 + c, h * self.w.kv_heads // HEADS, :]


def attend(nc, env, w, kind, ip, inner, into_x, behind_eps=None, behind_centre=False):
    R, banks, ident = env.R, env.banks, env.ident
    lay = Layout(kind, w)
    HP = HEADS // 2
    units = [(m, t, hp) for m in range(PAIR) for t in range(lay.tiles) for hp in range(HP)]
    U = len(units)
    ck = lay.chunk()
    with stage(nc, env.names) as (block, sem):
        scores_ready, max_ready, exp_ready = sem("scores_ready"), sem("max_ready"), sem("exp_ready")
        turned, copied, pv_done = sem("turned"), sem("copied"), sem("pv_done")
        normed, o_turned, OT_ready = sem("normed"), sem("o_turned"), sem("OT_ready")
        O_out, om_turned = sem("O_out"), sem("om_turned")
        projected, added, steps = sem("projected"), sem("added"), sem("steps")

        def ends_tile(u):
            return u // HP if 0 <= u < U and u % HP == HP - 1 else None

        def ends_image(u):
            return u // (HP * lay.tiles) if 0 <= u < U and (u + 1) % (HP * lay.tiles) == 0 else None

        def S(u):
            return banks[:, u % 3, :].rearrange("p (h k) -> p h k", h=2)

        def PTb(u):
            return banks[:, 3 + u % 2, :].rearrange("p (s q) -> p s q", q=P)

        def O(tile):
            return banks[:, 5 + tile % 2, 0:3 * P].rearrange("p (g q) -> p g q", q=P)

        OM = banks[:, 7, 0:3 * P].rearrange("p (h d) -> p h d", d=32)

        @block.tensor
        def _(pe):
            for s in range(U + 10):
                if s < U:
                    m, t, hp = units[s]
                    if s >= 3:
                        pe.wait_ge(exp_ready, s - 2)
                    for hh in range(2):
                        h = 2 * hp + hh
                        for r0, rn, win in lay.parts(t):
                            ins = nc.tensor.matmul(S(s)[r0:r0 + rn, hh, 0:lay.width(t)], lay.q(m, t, h, win),
                                                   lay.k(m, t, h, win), start=(hh == 0 or kind != "causal"),
                                                   stop=(kind != "causal"),
                                                   skip_group_check=(kind == "causal"))
                    if kind != "causal":
                        ins.then_inc(scores_ready, 1)
                u = s - 4
                if 0 <= u < U and u % 2 == 1:
                    m, t, hp = units[u]
                    tile = u // HP
                    pe.wait_ge(copied, u + 1)
                    if hp == 1 and tile >= 2:
                        pe.wait_ge(O_out, tile - 1)
                    for r0, rn, win in lay.parts(t):
                        for c in range(lay.chunks(t)):
                            for j in range(4):
                                h = 2 * hp - 2 + j
                                ins = nc.tensor.matmul(O(tile)[32 * j:32 * j + VW, h // 4, r0:r0 + rn],
                                                       lay.v(m, h, c, win),
                                                       w.PT[0:ck, (u - 1 + j // 2) % 4, j % 2 * lay.chunks(t) + c, r0:r0 + rn],
                                                       start=(c == 0), stop=(c == lay.chunks(t) - 1))
                    ins.then_inc(pv_done, 1)
                if s < U and kind == "causal":
                    t = units[s][1]
                    nc.tensor.matmul(S(s)[:, :, t * P:(t + 1) * P], env.ident16[:, :], env.mask16[:, :, :],
                                     start=False, stop=True, skip_group_check=True).then_inc(scores_ready, 1)
                u = s - 2
                if 0 <= u < U:
                    m, t, hp = units[u]
                    rows = lay.rows(t)
                    pe.wait_ge(exp_ready, u + 1)
                    if u >= 2:
                        pe.wait_ge(copied, u - 1)
                    for hh in range(2):
                        for c in range(lay.chunks(t)):
                            ins = nc.tensor.transpose(PTb(u)[0:ck, hh * lay.chunks(t) + c, 0:rows],
                                                      w.Pr[0:rows, u % 3, hh, c * ck:(c + 1) * ck], ident[0:rows, 0:rows])
                    ins.then_inc(turned, 1)
                tile = ends_tile(s - 6)
                if tile is not None:
                    m, t, _ = units[s - 6]
                    rows = lay.rows(t)
                    pe.wait_ge(O_out, tile + 1)
                    if tile >= 1:
                        pe.wait_ge(OT_ready, tile)
                    if m >= 1:
                        pe.wait_ge(added, m)
                    for g in range(3):
                        ins = nc.tensor.transpose(banks[0:rows, 7, g * P:(g + 1) * P], w.Os[:, tile % 2, g, 0:rows],
                                                  ident[:, :])
                    ins.then_inc(om_turned, 1)
                tile = ends_tile(s - 8)
                if tile is not None:
                    m, t, _ = units[s - 8]
                    rows = lay.rows(t)
                    pe.wait_ge(normed, tile + 1)
                    for c in range(2):
                        ins = nc.tensor.transpose(banks[0:CH, 7, c * P:c * P + rows],
                                                  w.On[0:rows, tile % 2, c * CH:(c + 1) * CH], ident[0:rows, 0:rows])
                    ins.then_inc(o_turned, 1)
                m = ends_image(s - 9)
                if m is not None:
                    pe.wait_ge(OT_ready, lay.tiles * (m + 1))
                    for t in range(2):
                        cols = slice(m * TOKENS + t * P, m * TOKENS + (t + 1) * P)
                        ins = dense(nc, banks[:, 7, t * C:(t + 1) * C], lambda k, r: w.OT[0:r, k, cols],
                                    lambda k, r: w.wo[0:r, k, :], w.out_rows)
                    ins.then_inc(projected, 1)

        @block.scalar
        def _(act):
            load_function(nc, env, ACT.Exp)
            for s in range(U + 10):
                if s < U:
                    _, t, _ = units[s]
                    rows = lay.rows(t)
                    act.wait_ge(max_ready, s + 1)
                    if s >= 3:
                        act.wait_ge(turned, s - 2)
                    for hh in range(2):
                        ins = nc.scalar.activation(w.Pr[0:rows, s % 3, hh, 0:lay.width(t)],
                                                   S(s)[0:rows, hh, 0:lay.width(t)], ACT.Exp,
                                                   bias=w.nmax[0:rows, s % 4, hh:hh + 1])
                    ins.then_inc(exp_ready, 1)
                tile = ends_tile(s - 5)
                if tile is not None:
                    _, t, _ = units[s - 5]
                    rows = lay.rows(t)
                    act.wait_ge(pv_done, (s - 5 + 1) // 2)
                    if tile >= 2:
                        act.wait_ge(om_turned, tile - 1)
                    nc.scalar.activation(w.Os[:, tile % 2, :, 0:rows], O(tile)[:, :, 0:rows], ACT.Copy).then_inc(O_out, 1)
                tile = ends_tile(s - 8)
                if tile is not None:
                    m, t, _ = units[s - 8]
                    act.wait_ge(o_turned, tile + 1)
                    for r0, rn, win in lay.parts(t):
                        for c in range(2):
                            src = banks[0:CH, 7, c * P + r0:c * P + r0 + rn]
                            dst = lay.tokens(w.OT[0:CH, c, :], m, t, win)
                            if kind == "windows":
                                src = src.rearrange("p (a b) -> p a b", b=WINDOW_BOX[win][3])
                            ins = nc.scalar.activation(dst, src, ACT.Copy)
                    ins.then_inc(OT_ready, 1)

        @block.vector
        def _(dve):
            chain = Chain(dve, steps)
            other = env.X[:, bass.ds(ip * -PT + PT, PT), :]
            ahead = normalise_steps(nc, chain, env.ahead_s, env.ahead, other, 1e-5, True, inner)
            behind = None
            both = kind == "causal" and behind_eps is not None
            for s in range(U + 10):
                if s < U:
                    _, t, _ = units[s]
                    rows = lay.rows(t)
                    dve.wait_ge(scores_ready, s + 1)
                    if s >= 4:
                        dve.wait_ge(exp_ready, s - 3)
                    nc.vector.tensor_reduce(w.nmax[0:rows, s % 4, :], S(s)[0:rows, :, 0:lay.width(t)], AX.X, ALU.max,
                                            negate=True).then_inc(max_ready, 1)
                u = s - 2
                if 0 <= u < U:
                    _, t, _ = units[u]
                    rows, n = lay.rows(t), 2 * lay.chunks(t)
                    dve.wait_ge(turned, u + 1)
                    if u >= 4:
                        dve.wait_ge(pv_done, u // 2 - 1)
                    nc.vector.tensor_copy(w.PT[0:ck, u % 4, 0:n, 0:rows], PTb(u)[0:ck, 0:n, 0:rows]).then_inc(copied, 1)
                tile = ends_tile(s - 7)
                if tile is not None:
                    _, t, _ = units[s - 7]
                    rows = lay.rows(t)
                    dve.wait_ge(om_turned, tile + 1)
                    if tile >= 2:
                        dve.wait_ge(o_turned, tile - 1)
                    chain(nc.vector.reciprocal(w.rsum[0:rows, tile % 2, :], OM[0:rows, :, HD]))
                    nc.vector.tensor_tensor(w.On[0:rows, tile % 2, :].rearrange("p (h d) -> p h d", d=HD),
                                            OM[0:rows, :, 0:HD],
                                            w.rsum[0:rows, tile % 2, :, None].to_broadcast([rows, HEADS, HD]),
                                            ALU.mult).then_inc(normed, 1)
                for _ in range(0 if s < 2 else 2 if s >= U or (both and s % 2) else 1):
                    if next(ahead, "done") == "done" and behind is not None:
                        next(behind, None)
                m = ends_image(s - 10)
                if m is not None:
                    dve.wait_ge(projected, m + 1)
                    r = env.X[:, bass.ds(ip * PT + 2 * m, 2), :] if into_x else R[:, 2 * m:2 * m + 2, :]
                    nc.vector.tensor_tensor(r, r, banks[:, 7, 0:2 * C].rearrange("p (t c) -> p t c", c=C),
                                            ALU.add).then_inc(added, 1)
                    if m == 0 and behind_eps is not None:
                        dve.wait_ge(added, 1)
                        behind = normalise_steps(nc, chain, env.s, env.xn, R, behind_eps, behind_centre, tiles=(0, 2))
            for _ in ahead:
                pass
            if behind is not None:
                for _ in behind:
                    pass
            chain.wait()
            dve.wait_ge(added, PAIR)


def store_residual(nc, chain, env, ip, add):
    x = env.X[:, bass.ds(ip * PT, PT), :]
    if add:
        chain(nc.vector.tensor_tensor(x, x, env.R[:, :, :], ALU.add))
    else:
        chain(nc.vector.tensor_copy(x, env.R[:, :, :]))


def causal_project(nc, env, w, ip, base_ln, rope):
    R, xn, banks, ident = env.R, env.xn, env.banks, env.ident
    NKV = w.kv_heads
    products = [(n, c, sw) for n in range(2) for c in range(2) for sw in range(2 if rope else 1)]
    per = 2 if rope else 1
    act_heads = [(c, j) for c in range(2) for j in range(6) if (j >= 2 if rope else c == 0)]
    dve_heads = [(c, j) for c in range(2) for j in range(6) if (c, j) not in act_heads]
    with stage(nc, env.names) as (block, sem):
        steps = sem("steps")
        normed, turned, xT_ready = sem("normed"), sem("turned"), sem("xT_ready")
        product_done, v_done, v_out = sem("product_done"), sem("v_done"), sem("v_out")
        copied = sem("copied")
        rotated, Q_out, bank_read = sem("rotated"), sem("Q_out"), sem("bank_read")

        def bank(i):
            return banks[0:CH, 2 + i % 6, :]

        @block.vector
        def _(dve):
            chain = Chain(dve, steps)
            if base_ln:
                for t in range(PT):
                    nc.vector.tensor_scalar(xn[:, t, :], env.ahead[:, t, :], env.ahead_s.y2[:, t:t + 1], None,
                                            ALU.mult).then_inc(normed, 1)

            def heads_out(c, src):
                for _, j in [head for head in dve_heads if head[0] == c]:
                    chain.free(nc.vector.tensor_scalar(w.Q[:, 6 * c + j, :], src, w.own[:, j:j + 1], None, ALU.mult))

            if rope:
                halves = lambda ap: ap.rearrange("p (m q) -> p m q", m=PAIR)
                for i in range(0, len(products), 2):
                    n, c, _ = products[i]
                    dve.wait_ge(product_done, i + 2)
                    cos = w.cos[:, None, :].to_broadcast([CH, PAIR, TOKENS])
                    sin = w.sin[:, None, :].to_broadcast([CH, PAIR, TOKENS])
                    dst = w.qT[:, c, :] if n == 0 else w.K[:, c, :]
                    chain.free(nc.vector.tensor_tensor(halves(dst), halves(bank(i)), cos, ALU.mult))
                    chain.free(nc.vector.tensor_tensor(halves(w.rb[:, :]), halves(bank(i + 1)), sin, ALU.mult))
                    chain.wait()
                    dve.sem_inc(bank_read, 2)
                    chain(nc.vector.tensor_tensor(dst, dst, w.rb[:, :], ALU.add))
                    dve.sem_inc(rotated, 1)
                    if n == 0:
                        heads_out(c, w.qT[:, c, :])
            else:
                for c in range(2):
                    dve.wait_ge(product_done, c + 1)
                    heads_out(c, bank(c))
            chain.wait()

        if base_ln:
            @block.gpsimd
            def _(pool):
                nc.gpsimd.tensor_copy(R[:, :, :], env.ahead[:, :, :]).then_inc(copied, 1)
                pool.wait_ge(copied, 1)

        @block.scalar
        def _(act):
            for c in range(2):
                act.wait_ge(turned, c + 1)
                nc.scalar.activation(w.xT[0:CH, c, :], banks[0:CH, c, :], ACT.Copy if w.nw is None else ACT.Identity,
                                     scale=1.0 if w.nw is None else w.nw[:, c:c + 1]).then_inc(xT_ready, 1)
            for c, j in act_heads:
                act.wait_ge(rotated if rope else product_done, c + 1)
                src = w.qT[:, c, :] if rope else bank(c)
                nc.scalar.activation(w.Q[:, 6 * c + j, :], src, ACT.Identity,
                                     scale=w.own[:, j:j + 1]).then_inc(Q_out, 1)
            if not rope:
                for c in range(2):
                    act.wait_ge(product_done, 2 + c + 1)
                    nc.scalar.activation(w.K[:, c, :], bank(2 + c), ACT.Copy).then_inc(Q_out, 1)
            for b in range(2):
                act.wait_ge(v_done, b + 1)
                nc.scalar.activation(w.V[:, 2 * b:2 * b + 2, :, 0:HD].rearrange("p t h d -> p (t h) d"),
                                     banks[:, b, 0:2 * NKV * HD].rearrange("p (t h d) -> p (t h) d", t=2, d=HD),
                                     ACT.Copy).then_inc(v_out, 1)
            act.wait_ge(v_out, 2)
            act.wait_ge(Q_out, 8)

        @block.tensor
        def _(pe):
            if base_ln:
                turn_tiles(nc, banks, xn, ident, turned, pe, normed)
            else:
                turn_tiles(nc, banks, env.ahead, ident, turned)

            def values():
                for t in range(PT):
                    ins = dense(nc, banks[:, t // 2, t % 2 * NKV * HD:(t % 2 + 1) * NKV * HD],
                                lambda k, r: w.xT[0:r, k, t * P:(t + 1) * P], lambda k, r: w.wv[0:r, k, 0:NKV * HD], w.in_rows)
                    if t % 2 == 1:
                        ins.then_inc(v_done, 1)

            for i, (n, c, sw) in enumerate(products):
                if i == 2 * per:
                    values()
                if i >= 6:
                    pe.wait_ge(bank_read, i - 5)
                at = ((n * per + sw) * 2 + c) * CH
                dense(nc, bank(i), lambda k, r: w.wqk[0:r, k, at:at + CH], lambda k, r: w.xT[0:r, k, :],
                      w.in_rows, pe, xT_ready if i == 0 else None).then_inc(product_done, 1)


def causal_setup(nc, env, w, before=None):
    with stage(nc, env.names) as (block, sem):
        filled = sem("filled")
        if before is not None:
            steps, gathered = sem("steps"), [sem(f"gathered_{q}") for q in range(TILES // 2)]

        @block.sync
        def _(sp):
            if before is not None:
                for q in range(TILES // 2):
                    sp.wait_ge(gathered[q], 64)
            start_loads(sp, w)
            sp.wait_ge(w.loaded, 16 * len(w.loads))

        @block.gpsimd
        def _(pool):
            if before is not None:
                gather(nc, env, before, gathered)
            chain = Chain(pool, filled)
            chain(nc.gpsimd.memset(w.V[:, :, :, HD:VW], 1.0))
            chain(nc.gpsimd.memset(w.xT[CH:CH + 1, 1, :], 1.0))
            chain(nc.gpsimd.memset(w.OT[CH:CH + 1, 1, :], 1.0))
            if w.tile_expert is not None:
                chain(nc.gpsimd.memset(w.route_xT[CH:CH + 1, 1, :], 1.0))
                for lo, hi in shared_tiles(8):
                    chain(nc.gpsimd.memset(w.tile_expert[:, lo:hi], 8))

        if before is not None:
            @block.vector
            def _(dve):
                chain = Chain(dve, steps)
                for q in range(TILES // 2):
                    combine(nc, dve, chain, env, before, gathered, q)
                    if 2 * q + 2 == PT:
                        normalise(nc, chain, env.ahead_s, env.ahead, env.X[:, 0:PT, :], 1e-5, True, 1e-5)


def feed_forward(nc, env, w, ip, gated):
    R, xn, banks, ident = env.R, env.xn, env.banks, env.ident
    NF = FF // P
    with stage(nc, env.names) as (block, sem):
        steps = sem("steps")
        normed, turned, xT_ready = sem("normed"), sem("turned"), sem("xT_ready")
        up_done, act_done, h_ready, out_done = sem("up_done"), sem("act_done"), sem("h_ready"), sem("out_done")

        @block.vector
        def _(dve):
            chain = Chain(dve, steps)
            normalise(nc, chain, env.s, xn, R, 1e-5, not gated, tiles=(2, PT))
            dve.sem_inc(normed, 1)
            if gated:
                for f in range(NF):
                    dve.wait_ge(act_done, f + 1)
                    nc.vector.tensor_tensor(w.hT[:, f, :], w.sg[:, f % 2, :], banks[:, 2 + f % 2, :],
                                            ALU.mult).then_inc(h_ready, 1)
            for t in range(PT):
                dve.wait_ge(out_done, t + 1)
                chain.free(nc.vector.tensor_tensor(R[:, t, :], R[:, t, :], banks[:, 4 + t, 0:C], ALU.add))
            chain.wait()
            store_residual(nc, chain, env, ip, gated)

        @block.scalar
        def _(act):
            load_function(nc, env, ACT.Silu if gated else ACT.Gelu)
            act.wait_ge(w.ffn_loaded, 16 * len(w.ffn_loads))
            for c in range(2):
                act.wait_ge(turned, c + 1)
                nc.scalar.activation(w.xT[0:CH, c, :], banks[0:CH, c, :], ACT.Identity, scale=w.fnw[:, c:c + 1],
                                     bias=0.0 if gated else w.fnb[:, c:c + 1]).then_inc(xT_ready, 1)
            for f in range(NF):
                act.wait_ge(up_done, f + 1)
                if gated:
                    if f >= 2:
                        act.wait_ge(h_ready, f - 1)
                    nc.scalar.activation(w.sg[:, f % 2, :], banks[:, f % 2, :], ACT.Silu).then_inc(act_done, 1)
                else:
                    nc.scalar.activation(w.hT[:, f, :], banks[:, f % 4, :], ACT.Gelu).then_inc(h_ready, 1)

        @block.tensor
        def _(pe):
            turn_second_image(nc, pe, banks, xn, ident, turned, normed)
            pe.wait_ge(w.ffn_loaded, 16 * len(w.ffn_loads))
            for f in range(NF):
                first = xT_ready if f == 0 else None
                slots = 2 if gated else 4
                if f >= slots:
                    pe.wait_ge(h_ready, f - slots + 1)
                x = lambda k, r: w.xT[0:r, k, :]
                if gated:
                    dense(nc, banks[:, f % 2, :], lambda k, r: w.w1[0:r, k, f * P:(f + 1) * P], x, (CH, CH), pe, first)
                    ins = dense(nc, banks[:, 2 + f % 2, :], lambda k, r: w.w3[0:r, k, f * P:(f + 1) * P], x)
                else:
                    ins = dense(nc, banks[:, f % 4, :], lambda k, r: w.w1[0:r, k, f * P:(f + 1) * P], x, BIASED,
                                pe, first)
                ins.then_inc(up_done, 1)
            for t in range(PT):
                for f in range(NF):
                    if t == 0:
                        pe.wait_ge(h_ready, f + 1)
                    ins = nc.tensor.matmul(banks[:, 4 + t, 0:C], w.hT[:, f, t * P:(t + 1) * P], w.w2[:, f, :],
                                           start=(f == 0), stop=(gated and f == NF - 1))
                if not gated:
                    ins = nc.tensor.matmul(banks[:, 4 + t, 0:C], env.ones[0:1, :], w.b2[0:1, :], start=False, stop=True)
                ins.then_inc(out_done, 1)


def route(nc, env, w, ip, first):
    R, xn, banks, ident, E = env.R, env.xn, env.banks, env.ident, w.experts
    with stage(nc, env.names) as (block, sem):
        steps = sem("steps")
        normed, turned, xT_ready, kept = sem("normed"), sem("turned"), sem("xT_ready"), sem("kept")
        logits_done, margin_ready, exp_done = sem("logits_done"), sem("margin_ready"), sem("exp_done")

        @block.vector
        def _(dve):
            chain = Chain(dve, steps)
            if first:
                normalise(nc, chain, env.s, xn, R, 1e-6, False, tiles=(2, PT))
            else:
                normalise(nc, chain, env.s, xn, env.X[:, bass.ds(ip * PT, PT), :], 1e-5, True)
            dve.sem_inc(normed, 1)
            if first:
                store_residual(nc, chain, env, ip, True)
            dve.wait_ge(logits_done, 1)
            chain(nc.vector.tensor_copy(w.logits[:, :, :], banks[:, 2, 0:PT * E].rearrange("p (t e) -> p t e", e=E)))
            for t in range(PT):
                chain.free(nc.vector.max(w.top[:, t, :], w.logits[:, t, :]))
            chain.wait()
            for t in range(PT):
                chain.free(nc.vector.max_index(w.topi[:, t, :], w.top[:, t, :], w.logits[:, t, :]))
            chain.free(nc.vector.tensor_tensor(w.margin[:, :], w.top[:, :, 1], w.top[:, :, 0], ALU.subtract))
            chain.wait()
            dve.sem_inc(margin_ready, 1)
            chain.free(nc.vector.tensor_copy(w.expert[:, bass.ds(ip * PT, PT), :], w.topi[:, :, 0:2]))
            dve.wait_ge(exp_done, 1)
            chain(nc.vector.tensor_scalar(w.g1[:, :], w.margin[:, :], 1.0, None, ALU.add))
            chain(nc.vector.reciprocal(w.g0[:, :], w.g1[:, :]))
            chain.free(nc.vector.tensor_copy(w.weight[:, bass.ds(ip * PT, PT), 0], w.g0[:, :]))
            chain(nc.vector.tensor_tensor(w.weight[:, bass.ds(ip * PT, PT), 1], w.margin[:, :], w.g0[:, :], ALU.mult))

        @block.gpsimd
        def _(pool):
            pool.wait_ge(normed, 1)
            nc.gpsimd.tensor_copy(w.M[:, bass.ds(ip * PT, PT), :], xn[:, :, :]).then_inc(kept, 1)
            pool.wait_ge(kept, 1)

        @block.scalar
        def _(act):
            load_function(nc, env, ACT.Exp)
            act.wait_ge(w.router_loaded, 16 * w.router_loads)
            for c in range(2):
                act.wait_ge(turned, c + 1)
                nc.scalar.activation(w.xT[0:CH, c, :], banks[0:CH, c, :],
                                     ACT.Identity if first else ACT.Copy,
                                     scale=w.nw2[:, c:c + 1] if first else 1.0).then_inc(xT_ready, 1)
            act.wait_ge(margin_ready, 1)
            nc.scalar.activation(w.margin[:, :], w.margin[:, :], ACT.Exp).then_inc(exp_done, 1)

        @block.tensor
        def _(pe):
            if first:
                turn_second_image(nc, pe, banks, xn, ident, turned, normed)
            else:
                pe.wait_ge(normed, 1)
                turn_tiles(nc, banks, xn, ident, turned)
            pe.wait_ge(w.router_loaded, 16 * w.router_loads)
            for t in range(PT):
                ins = dense(nc, banks[:, 2, t * E:(t + 1) * E], lambda k, r: w.xT[0:r, k, t * P:(t + 1) * P],
                            lambda k, r: w.wr[0:r, k, :], w.r_rows, pe, xT_ready if t == 0 else None)
            ins.then_inc(logits_done, 1)


def running_sum(nc, chain, bufs, n, at):
    src, dst = bufs
    s = 1
    while s < n:
        chain.free(nc.vector.tensor_tensor(at(dst, s, n), at(src, s, n), at(src, 0, n - s), ALU.add))
        chain.free(nc.vector.tensor_copy(at(dst, 0, s), at(src, 0, s)))
        chain.wait()
        src, dst, s = dst, src, 2 * s
    return src


def sort_tokens(nc, env, w):
    banks, E = env.banks, w.experts
    with stage(nc, env.names) as (block, sem):
        steps, picked, counted = sem("steps"), sem("picked"), sem("counted")
        slots_ready, scattered, shared_in = sem("slots_ready"), sem("scattered"), sem("shared_in")

        @block.vector
        def _(dve):
            chain = Chain(dve, steps)
            expert = w.expert[:, :, :].rearrange("p t k -> p (t k)")
            chain(nc.vector.tensor_tensor(w.hit[:, :, :], env.iota[:, None, 0:E].to_broadcast([P, PICKS, E]),
                                          expert[:, :, None].to_broadcast([P, PICKS, E]), ALU.is_equal))
            chain(nc.vector.tensor_copy(w.hit16[:, :, :], w.hit[:, :, :]))
            dve.sem_inc(picked, 1)
            dve.wait_ge(counted, 1)
            before = banks[:, 0, 0:PICKS * E].rearrange("p (a e) -> p a e", e=E)
            column = banks[:, 1, 0:PICKS * E].rearrange("p (a e) -> p a e", e=E)
            chain(nc.vector.tensor_copy(w.sum_a[:, :, :], column))
            total = running_sum(nc, chain, (w.sum_a, w.sum_b), PICKS, lambda b, lo, hi: b[:, lo:hi, :])
            chain(nc.vector.tensor_scalar(w.count[:, :], total[:, PICKS - 1, :], float(P - 1), None, ALU.add))
            chain(nc.vector.tensor_scalar(w.count[:, :], w.count[:, :], P.bit_length() - 1, None, ALU.logical_shift_right))
            chain(nc.vector.tensor_copy(w.ends[0][:, :], w.count[:, :]))
            end = running_sum(nc, chain, w.ends, E, lambda b, lo, hi: b[:, lo:hi])
            chain(nc.vector.tensor_tensor(w.passed[:, :, :], env.iota[0:1, 0:SORTED_TILES[E], None].to_broadcast([1, SORTED_TILES[E], E]),
                                          end[0:1, None, :].to_broadcast([1, SORTED_TILES[E], E]), ALU.is_ge))
            chain(nc.vector.tensor_reduce(w.owner[:, :], w.passed[:, :, :], AX.X, ALU.add))
            at = SHARED_FIRST if w.shared else 0
            chain(nc.vector.tensor_scalar(w.tile_expert[:, at:at + SORTED_TILES[E]], w.owner[:, :], float(E - 1), None, ALU.min))
            chain(nc.vector.tensor_tensor(w.slots[:, :, :], total[:, :, :], column, ALU.subtract))
            chain(nc.vector.tensor_tensor(w.slots[:, :, :], w.slots[:, :, :], before, ALU.add))
            chain(nc.vector.tensor_copy(w.first[:, :], w.count[:, :]))
            chain(nc.vector.tensor_tensor(w.first[:, :], end[:, :], w.first[:, :], ALU.subtract))
            if w.shared:
                chain(nc.vector.tensor_scalar(w.first[:, :], w.first[:, :], float(SHARED_FIRST), None, ALU.add))
            chain(nc.vector.scalar_tensor_tensor(w.slots[:, :, :], w.first[:, None, :].to_broadcast([P, PICKS, E]), float(P),
                                                 w.slots[:, :, :], ALU.mult, ALU.add))
            chain(nc.vector.tensor_tensor(w.slots[:, :, :], w.slots[:, :, :], w.hit[:, :, :], ALU.mult))
            chain(nc.vector.tensor_reduce(w.slot[:, :], w.slots[:, :, :], AX.X, ALU.add))
            chain(nc.vector.tensor_copy(w.slot_index[:, :], w.slot[:, :]))
            dve.sem_inc(slots_ready, 1)

        @block.tensor
        def _(pe):
            pe.wait_ge(picked, 1)
            hit = w.hit16[:, :, :].rearrange("p a e -> p (a e)")
            nc.tensor.matmul(banks[:, 0, 0:PICKS * E], env.above16[:, :], hit, start=True, stop=True)
            nc.tensor.matmul(banks[:, 1, 0:PICKS * E], env.ones16[:, :], hit, start=True, stop=True).then_inc(counted, 1)

        if not w.shared:
            @block.gpsimd
            def _(pool):
                pool.wait_ge(env.slots_zeroed, 16)
                pool.wait_ge(slots_ready, 1)
                scatter(nc, env, w, scattered)
                pool.wait_ge(scattered, 16 * PICKS)

        @block.sync
        def _(sp):
            for dst, src in w.last_loads:
                sp.dma_start(dst, src).then_inc(w.experts_loaded, 16)
            for dst, src in w.next_loads:
                sp.dma_start(dst, src).then_inc(w.next_loaded, 16)
            if w.shared:
                sp.wait_ge(env.slots_zeroed, 16)
                for (lo, hi), t in zip(shared_tiles(E), (0, SHARED_FIRST)):
                    dst = env.slots_in[lo * P:hi * P, :].rearrange("(t p) c -> p t c", p=P)
                    sp.dma_start(dst, w.M[:, t:t + hi - lo, :]).then_inc(shared_in, 16)
                sp.wait_ge(shared_in, 32)


def shared_tiles(E):
    return (0, SHARED_FIRST), (SHARED_FIRST + SORTED_TILES[E], SLOT_TILES)


def scatter(nc, env, w, scattered):
    for a in range(PICKS):
        nc.gpsimd.indirect_dma_start(
            env.slots_in[:, :], bass.IndirectOffsetOnAxis(ap=w.slot_index[:, a:a + 1], axis=0),
            w.M[:, a // 2, :], None).then_inc(scattered, 16)


def gather(nc, env, w, gathered):
    for a in range(PICKS):
        nc.gpsimd.indirect_dma_start(
            w.picked_y[:, a, :], None, env.slots_out[:, :],
            bass.IndirectOffsetOnAxis(ap=w.slot_index[:, a:a + 1], axis=0)).then_inc(gathered[a // 4], 16)


def combine(nc, dve, chain, env, w, gathered, q):
    dve.wait_ge(gathered[q], 64)
    for k in range(2):
        for t in (2 * q, 2 * q + 1):
            chain.free(nc.vector.scalar_tensor_tensor(
                env.X[:, t, :], w.picked_y[:, 2 * t + k, :], w.weight[:, t, k:k + 1], env.X[:, t, :],
                ALU.mult, ALU.add))
        chain.wait()


def pipeline(eng, n, jobs):
    last = max(lag for _, lag in jobs)
    head = last + 2 + (n - last) % 2

    def step(s, j=None):
        for job, lag in jobs:
            if j is not None or 0 <= s - lag < n:
                i, half = s - lag, (s - lag) // 2
                job(i if j is None else j * 2 + i, i % 2, half if j is None else j + half)

    for s in range(head):
        step(s)
    with eng.Fori(0, (n - head) // 2) as j:
        for r in range(2):
            step(head + r, j)
    for s in range(n, n + last):
        step(s)


def experts(nc, env, w):
    banks, ident, E = env.banks, env.ident, w.experts
    NF = EF // P
    with stage(nc, env.names) as (block, sem):
        x_loaded = [sem("x_loaded_even"), sem("x_loaded_odd")]
        y_stored = [sem("y_stored_even"), sem("y_stored_odd")]
        x_turned, xT_out, gu_done, silu_done = sem("x_turned"), sem("xT_out"), sem("gu_done"), sem("silu_done")
        h_done, h_turned, hT_out, down_done, y_out = (sem("h_done"), sem("h_turned"), sem("hT_out"), sem("down_done"),
                                                      sem("y_out"))
        gathered = [sem(f"gathered_{q}") for q in range(TILES // 2)]
        shared_out, summed, scattered = sem("shared_out"), sem("summed"), sem("scattered")

        @block.sync
        def _(sp):
            def rows(dram, i):
                r = slice(i * P, (i + 1) * P) if isinstance(i, int) else bass.ds(i * P, P)
                return dram[r, :]

            def load(i, par, half):
                if w.shared and isinstance(i, int) and i == SHARED_FIRST:
                    sp.wait_ge(scattered, 16 * PICKS)
                sp.wait_ge(x_turned, i + 1)
                sp.dma_start(w.xin[:, par, :], rows(env.slots_in, i)).then_inc(x_loaded[par], 16)

            def store(i, par, half):
                sp.wait_ge(y_out, i + 2)
                sp.dma_start(rows(env.slots_out, i), w.y[:, par, :]).then_inc(y_stored[par], 16)

            pipeline(sp, SLOT_TILES, ((load, 0), (store, 5)))
            sp.wait_ge(y_stored[0], 16 * ((SLOT_TILES + 1) // 2))
            sp.wait_ge(y_stored[1], 16 * (SLOT_TILES // 2))
            if w.shared:
                for (lo, hi), t in zip(shared_tiles(E), (0, SHARED_FIRST)):
                    src = env.slots_out[lo * P:hi * P, :].rearrange("(t p) c -> p t c", p=P)
                    sp.dma_start(w.shared_y[:, t:t + hi - lo, :], src).then_inc(shared_out, 16)

        @block.tensor
        def _(pe):
            def expert_of(i):
                at = slice(i, i + 1) if isinstance(i, int) else bass.ds(i, 1)
                return pe.value_load(w.tile_expert[0:1, at], min_val=0, max_val=w.stored - 1)

            def turn(i, par, half):
                pe.wait_ge(x_loaded[par], half * 16 + 16)
                pe.wait_ge(xT_out, i + 1)
                for c in range(2):
                    ins = nc.tensor.transpose(banks[0:CH, par, c * P:(c + 1) * P], w.xin[:, par, c * CH:(c + 1) * CH],
                                              ident[:, :])
                ins.then_inc(x_turned, 1)

            def up(i, par, half):
                e = expert_of(i)
                pe.wait_ge(xT_out, i + 3)
                pe.wait_ge(h_done, i + 1)
                for k in range(2):
                    for n in range(2):
                        ins = nc.tensor.matmul(banks[:, 2 + 2 * par + n, 0:EF], w.sxT[:, par, k, :],
                                               w.gu[:, bass.ds(e, 1), k, n * EF:(n + 1) * EF].rearrange("p o f -> p (o f)"),
                                               start=(k == 0), stop=(k == 1))
                ins.then_inc(gu_done, 1)

            def turn_hidden(i, par, half):
                pe.wait_ge(h_done, i + 3)
                pe.wait_ge(hT_out, i + 1)
                for f in range(NF):
                    ins = nc.tensor.transpose(banks[:, 6, f * P:(f + 1) * P], w.h[:, par, f * P:(f + 1) * P], ident[:, :])
                ins.then_inc(h_turned, 1)

            def down(i, par, half):
                e = expert_of(i)
                pe.wait_ge(hT_out, i + 2)
                pe.wait_ge(y_out, i + 1)
                for f in range(NF):
                    ins = nc.tensor.matmul(banks[:, 7, 0:C], w.ehT[:, par, f, :],
                                           w.dn[:, bass.ds(e, 1), f, :].rearrange("p o c -> p (o c)"),
                                           start=(f == 0), stop=(f == NF - 1))
                ins.then_inc(down_done, 1)

            pe.sem_inc(x_turned, 2)
            pe.sem_inc(gu_done, 2)
            pe.sem_inc(h_turned, 2)
            pe.sem_inc(down_done, 2)
            pe.wait_ge(w.experts_loaded, 16 * (len(w.expert_loads) + len(w.last_loads)))
            pipeline(pe, SLOT_TILES, ((turn, 0), (up, 1), (turn_hidden, 2), (down, 3)))

        @block.scalar
        def _(act):
            def x_evacuate(i, par, half):
                act.wait_ge(x_turned, i + 3)
                act.wait_ge(gu_done, i + 1)
                for c in range(2):
                    ins = nc.scalar.activation(w.sxT[:, par, c, :], banks[0:CH, par, c * P:(c + 1) * P],
                                               ACT.Identity if w.nw2 is not None else ACT.Copy,
                                               scale=1.0 if w.nw2 is None else w.nw2[:, c:c + 1])
                ins.then_inc(xT_out, 1)

            def gate(i, par, half):
                act.wait_ge(gu_done, i + 3)
                act.wait_ge(h_done, i + 1)
                nc.scalar.activation(w.sg[:, par, :], banks[:, 2 + 2 * par, 0:EF], ACT.Silu).then_inc(silu_done, 1)

            def y_evacuate(i, par, half):
                act.wait_ge(down_done, i + 3)
                if not (isinstance(half, int) and half == 0):
                    act.wait_ge(y_stored[par], half * 16)
                nc.scalar.activation(w.y[:, par, :], banks[:, 7, 0:C], ACT.Copy).then_inc(y_out, 1)

            load_function(nc, env, ACT.Silu)
            act.sem_inc(xT_out, 2)
            act.sem_inc(y_out, 1)
            pipeline(act, SLOT_TILES, ((x_evacuate, 0), (gate, 1), (y_evacuate, 3)))

        @block.vector
        def _(dve):
            def hidden(i, par, half):
                dve.wait_ge(silu_done, i + 1)
                dve.wait_ge(h_turned, i + 1)
                nc.vector.tensor_tensor(w.h[:, par, :], w.sg[:, par, :], banks[:, 3 + 2 * par, 0:EF],
                                        ALU.mult).then_inc(h_done, 1)

            def h_evacuate(i, par, half):
                dve.wait_ge(h_turned, i + 3)
                dve.wait_ge(down_done, i + 1)
                nc.vector.tensor_copy(w.ehT[:, par, :, :].rearrange("p f t -> p (f t)"),
                                      banks[:, 6, 0:NF * P]).then_inc(hT_out, 1)

            dve.sem_inc(h_done, 2)
            dve.sem_inc(hT_out, 1)
            pipeline(dve, SLOT_TILES, ((hidden, 1), (h_evacuate, 2)))

            chain = Chain(dve, summed)
            if w.shared:
                for q in range(TILES // 2):
                    combine(nc, dve, chain, env, w, gathered, q)
                dve.wait_ge(shared_out, 32)
                chain(nc.vector.tensor_tensor(env.X[:, :, :], env.X[:, :, :], w.shared_y[:, :, :], ALU.add))

        @block.gpsimd
        def _(pool):
            if w.shared:
                scatter(nc, env, w, scattered)
                done = SHARED_FIRST + SORTED_TILES[E]
                pool.wait_ge(y_stored[0], 16 * ((done + 1) // 2))
                pool.wait_ge(y_stored[1], 16 * (done // 2))
                gather(nc, env, w, gathered)


class Env:
    pass


def build(nc, d, out):
    ctx = ExitStack()
    env = Env()
    env.names = {}

    def allocator(stack):
        def sb(name, shape, dt=F32):
            return stack.enter_context(nc.sbuf_tensor(unique(env.names, name), shape, dt))
        return sb

    with ctx:
        sb = allocator(ctx)
        env.banks = ctx.enter_context(nc.psum_tensor("banks", [P, 8, BANK], F32))
        env.X, env.R, env.xn = sb("X", [P, TILES, C]), sb("R", [P, PT, C]), sb("xn", [P, PT, C])
        env.ident, env.mask = sb("ident", [P, P]), sb("mask", [P, P])
        env.ident16, env.mask16 = sb("ident16", [P, P], BF16), sb("mask16", [P, 2, P], BF16)
        env.ones, env.iota = sb("ones", [1, P]), sb("iota", [P, SLOT_TILES + 1])
        env.above16, env.ones16 = sb("above16", [P, P], BF16), sb("ones16", [P, P], BF16)
        env.zeros, env.unused = sb("zeros", [P, C]), sb("unused", [P, 1])
        env.slots_in = nc.dram_tensor("slots_in", (SLOT_TILES * P, C), F32, kind="Internal").ap()
        env.slots_out = nc.dram_tensor("slots_out", (SLOT_TILES * P, C), F32, kind="Internal").ap()
        env.slots_zeroed = nc.alloc_semaphore(name="slots_zeroed")
        env.s, env.ahead_s, env.ahead = Scratch(sb), Scratch(sb), sb("ahead", [P, PT, C])

        with stage(nc, env.names) as (block, sem):
            loaded, cast, cleared = sem("loaded"), sem("cast"), sem("cleared")

            @block.sync
            def _(sp):
                for dst, src in ((env.X[:], d["x"]), (env.ident[:], d["ident"]), (env.mask[:], d["mask"]),
                                 (env.iota[:], d["iota"])):
                    sp.dma_start(dst, src).then_inc(loaded, 16)
                sp.wait_ge(loaded, 64)

            @block.vector
            def _(dve):
                nc.vector.memset(env.banks[:, :, :].rearrange("p a b -> p (a b)"), 0.0).then_inc(cleared, 1)
                nc.vector.memset(env.ones[:, :], 1.0).then_inc(cleared, 1)
                nc.vector.memset(env.zeros[:, :], 0.0).then_inc(cleared, 1)
                nc.vector.memset(env.ones16[:, :], 1.0).then_inc(cleared, 1)
                dve.wait_ge(loaded, 64)
                nc.vector.tensor_copy(env.ident16[:, :], env.ident[:, :]).then_inc(cast, 1)
                nc.vector.tensor_copy(env.mask16[:, :, :], env.mask[:, None, :].to_broadcast([P, 2, P])).then_inc(cast, 1)
                nc.vector.tensor_scalar(env.above16[:, :], env.mask[:, :], 0.0, None, ALU.is_lt).then_inc(cast, 1)
                dve.wait_ge(cast, 3)
                dve.wait_ge(cleared, 4)

        def attention_buffers(w, sb):
            w.work = sb("work", [P, 6 * TOKENS + 16 * P])
            w.Pr = w.work[:, 0:6 * TOKENS].rearrange("p (u h k) -> p u h k", u=3, h=2)
            w.PT = w.work[:, 6 * TOKENS:].rearrange("p (u s q) -> p u s q", u=4, q=P)
            w.hT = w.work[:, 0:FF // P * PN].rearrange("p (f n) -> p f n", n=PN)
            w.nmax, w.rsum = sb("nmax", [P, 4, 2]), sb("rsum", [P, 2, HEADS])
            w.Os = sb("Os", [P, 2, 3, P])
            w.On, w.OT, w.xT = sb("On", [P, 2, C]), sb("OT", [CH + 1, 2, PN]), sb("xT", [CH + 1, 2, PN])

        def loader(w, sb, layer):
            w.loads, w.ffn_loads, w.late_loads, w.prefetch, w.early = [], [], [], [], False
            w.tile_expert = None
            w.loaded = nc.alloc_semaphore(name=layer + "_loaded")
            w.ffn_loaded = nc.alloc_semaphore(name=layer + "_ffn_loaded")

            def load(name, shape, key, ffn=False):
                t = sb(name, shape)
                (w.ffn_loads if ffn else w.loads).append((t[:], d[key]))
                return t
            return load

        def side_by_side(weights, widths):
            ends = [sum(widths[0:n + 1]) for n in range(len(widths))]
            return [weights[:, :, end - width:end] for end, width in zip(ends, widths)]

        def relative_weights(w, load, layer, windows):
            weights = load("weights", [CH + 1, 2, 3 * C + 6 * P], layer + "_weights")
            w.wq, w.wk, w.wv, w.wo = side_by_side(weights, (C, 6 * P, C, C))
            w.hot = load("hot", [P, WINDOWS * WN if windows else TOKENS], layer + "_hot")
            w.qslot, w.odd = env.qslot, env.odd
            if windows:
                w.loads += [(env.qslot[:], d["qslot"]), (env.odd[:], d["odd"])]
            if not windows:
                w.rel, w.shrink = load("rel", [63, 2, CH], "L1_rel"), load("shrink", [63, TOKENS], "shrink")
                w.gavg = load("gavg", [CH, CH], "gavg")

        def causal_weights(w, sb, load, layer):
            w.kv_heads = 3 if layer == "L2f" else HEADS
            products = 2 * C if layer == "L2a" else 4 * C
            w.weights = load("weights", [CH + 1, 2, products + 2 * C], layer + "_weights")
            w.wqk, w.wv, w.wo = side_by_side(w.weights, (products, C, C))
            w.own = env.own
            if layer == "L2a":
                w.loads.append((env.own[:], d["own"]))
            w.nw = None
            if layer != "L2a":
                w.nw = load("nw", [CH, 2], layer + "_norm1")
                w.cos, w.sin = load("cos", [CH, TOKENS], "cos"), load("sin", [CH, TOKENS], "sin")

        env.qslot, env.odd, env.own = sb("qslot", [CH, 2, HD]), sb("odd", [CH, 2]), sb("own", [CH, 6])
        env.weight, env.slot_index = sb("weight", [P, TILES, 2]), sb("slot_index", [P, PICKS], U32)
        early, early_stack = {}, {}
        for layer in ("L2f", "L2a", "L1"):
            w, early_stack[layer] = Env(), ExitStack()
            early_sb = allocator(early_stack[layer])
            load = loader(w, early_sb, layer)
            w.early = True
            if layer == "L1":
                relative_weights(w, load, layer, False)
            else:
                causal_weights(w, early_sb, load, layer)
            early[layer] = w

        for layer, windows in (("L0", True), ("L1", False)):
            with ExitStack() as stack:
                sb = allocator(stack)
                if windows:
                    w = Env()
                    load = loader(w, sb, layer)
                    relative_weights(w, load, layer, windows)
                    w.prefetch = [early[later] for later in ("L1", "L2a", "L2f")]
                else:
                    w = early[layer]
                attention_buffers(w, sb)
                w.bd, w.qT = sb("bd", [CH, 2, SIDE, 2, 32]), sb("qT", [CH, 2, PN])
                w.Q = sb("Q", [P, HEADS, PN])
                w.in_rows = w.out_rows = BIASED
                w.kv_heads = HEADS
                if windows:
                    w.win = load("win", [CH, 2, SIDE, 16], layer + "_win")
                    w.kpad = load("kpad", [P, 6], layer + "_kpad")
                    w.nw, w.nb = load("nw", [CH, 2], "L0_ln1_w"), load("nb", [CH, 2], "L0_ln1_b")
                    w.fnw, w.fnb = load("fnw", [CH, 2], "L0_ln2_w", True), load("fnb", [CH, 2], "L0_ln2_b", True)
                    w.w1 = load("w1", [CH + 1, 2, FF], "L0_w1", True)
                    w.w2, w.b2 = load("w2", [P, FF // P, C], "L0_w2", True), load("b2", [1, C], "L0_b2", True)
                    w.K, w.V = sb("K", [P, 6, PAIR, WINDOWS * WN]), sb("V", [98, 8 * PAIR, HEADS, VW])
                    w.xw = sb("xw", [CH + 1, 2, PAIR, WINDOWS * WN])
                else:
                    w.win = sb("win", [CH, 2, SIDE, 16])
                    w.K, w.V = sb("K", [P, 6, PAIR, TOKENS]), sb("V", [P, PT, HEADS, VW])
                    w.gst, w.gmv = sb("gst", [CH, 4, 6]), sb("gmv", [CH, 4, 2])
                    w.ga, w.gv, w.gscale, w.gbias = (sb(n, [CH, 4]) for n in ("ga", "gv", "gscale", "gbias"))
                relative_setup(nc, env, w, windows)
                with nc.Fori(0, IMAGES // PAIR) as ip:
                    relative_project(nc, env, w, ip, windows)
                    attend(nc, env, w, "windows" if windows else "full", ip, None, not windows,
                           1e-5 if windows else None, windows)
                    if windows:
                        feed_forward(nc, env, w, ip, False)
        early_stack["L1"].close()

        x = None
        for layer in ("L2a", "L2f", "L3a"):
            experts_stack = ExitStack()
            before = x
            if layer != "L2a":
                x = expert_buffers(env, allocator(experts_stack), nc, d, layer)
            with ExitStack() as stack:
                sb = allocator(stack)
                if layer == "L3a":
                    load = loader(later, sb, layer)
                    later.loads, later.loaded, later.early = before.next_loads, before.next_loaded, True
                    w = later
                else:
                    w = early[layer]
                attention_buffers(w, sb)
                w.in_rows = w.out_rows = BIASED if layer == "L2a" else (CH, CH)
                if layer == "L2f":
                    w.Q = x.gu[:, x.experts - 4:, :, :].rearrange("p e k f -> p (e k f)").rearrange("p (h n) -> p h n", h=HEADS)
                else:
                    w.Q = sb("Q", [CH, HEADS, PN])
                w.K = sb("K", [CH, 2, PN])
                w.V = sb("V", [P, PT, w.kv_heads, VW])
                if layer != "L2a":
                    w.qT, w.rb = sb("qT", [CH, 2, PN]), sb("rb", [CH, PN])
                if layer == "L3a":
                    w.fnw = load("fnw", [CH, 2], "L3a_norm2", True)
                    w.w1, w.w3 = load("w1", [CH + 1, 2, FF], "L3a_w1", True), load("w3", [CH + 1, 2, FF], "L3a_w3", True)
                    w.w2 = load("w2", [P, FF // P, C], "L3a_w2", True)
                    w.sg = sb("sg", [P, 2, PN])
                if layer != "L2a":
                    w.ffn_loads += x.loads
                    x.router_loaded, x.router_loads = w.ffn_loaded, len(w.ffn_loads)
                    w.late_loads, w.late_loaded = x.expert_loads, x.experts_loaded
                if layer == "L2f":
                    x.xT = w.xT
                    later = Env()
                    later.kv_heads = HEADS
                    later.wqk, later.wv, later.wo, later.own, later.nw = w.wqk, w.wv, w.wo, w.own, w.nw
                    later.cos, later.sin = w.cos, w.sin
                    x.next_loads = [(buf[:], d["L3a_" + key]) for buf, key in
                                    ((w.weights, "weights"), (w.nw, "norm1"))]
                    x.next_loaded = nc.alloc_semaphore(name="L3a_early")
                if layer == "L3a":
                    w.tile_expert, w.route_xT = x.tile_expert, x.xT
                    before.picked_y = w.work[:, 0:PICKS * C].rearrange("p (a c) -> p a c", c=C)
                    causal_setup(nc, env, w, before)
                else:
                    causal_setup(nc, env, w)
                with nc.Fori(0, IMAGES // PAIR) as ip:
                    causal_project(nc, env, w, ip, layer != "L2a", layer != "L2a")
                    attend(nc, env, w, "causal", ip, 1e-5 if layer == "L3a" else 1e-6, layer == "L2a",
                           {"L2a": None, "L2f": 1e-6, "L3a": 1e-5}[layer], False)
                    if layer == "L2f":
                        route(nc, env, x, ip, True)
                    elif layer == "L3a":
                        feed_forward(nc, env, w, ip, True)
            if layer == "L3a":
                with nc.Fori(0, IMAGES // PAIR) as ip:
                    route(nc, env, x, ip, False)
            if layer != "L2a":
                with ExitStack() as stack:
                    sort_buffers(x, allocator(stack))
                    sort_tokens(nc, env, x)
                with ExitStack() as stack:
                    slot_buffers(x, allocator(stack))
                    experts(nc, env, x)
                nc.clear_and_free_semaphores([x.experts_loaded])
                nc.all_engine_barrier()
            experts_stack.close()
            if layer == "L2a":
                early_stack["L2a"].close()

        early_stack["L2f"].close()
        with stage(nc, env.names) as (block, sem):
            written = sem("written")

            @block.sync
            def _(sp):
                sp.dma_start(out, env.X[:]).then_inc(written, 16)
                sp.wait_ge(written, 16)


def expert_buffers(env, sb, nc, d, layer):
    x = Env()
    x.experts, name = (16, "L2f") if layer == "L2f" else (8, "L3f")
    n = x.experts
    x.shared = name == "L3f"
    x.stored = n + x.shared
    x.r_rows = BIASED if x.shared else (CH, CH)
    x.wr = sb("wr", [CH + 1, 2, n])
    x.loads = [(x.wr[:], d[name + "_wr"])]
    x.nw2 = None
    if not x.shared:
        x.nw2 = sb("nw2", [CH, 2])
        x.loads.append((x.nw2[:], d["L2f_norm2"]))
    x.gu, x.dn = sb("gu", [CH, x.stored, 2, 2 * EF]), sb("dn", [P, x.stored, EF // P, C])
    x.expert_loads, x.last_loads, x.next_loads = [], [], []
    early = x.stored if x.shared else n - 4
    x.expert_loads += [(x.gu[:, 0:early], d[name + "_gu"][:, 0:early]), (x.dn[:], d[name + "_dn"])]
    if early < x.stored:
        x.last_loads.append((x.gu[:, early:], d[name + "_gu"][:, early:]))
    x.experts_loaded = nc.alloc_semaphore(name=name + "_experts_loaded")
    x.M = sb("M", [P, TILES, C])
    x.expert, x.weight = sb("expert", [P, TILES, 2]), env.weight
    if x.shared:
        x.xT = sb("route_xT", [CH + 1, 2, PN])
    x.logits, x.margin, x.g0, x.g1 = sb("logits", [P, PT, n]), sb("margin", [P, PT]), sb("g0", [P, PT]), sb("g1", [P, PT])
    x.top, x.topi = sb("top", [P, PT, 8]), sb("topi", [P, PT, 8], U32)
    x.slot_index, x.tile_expert = env.slot_index, sb("tile_expert", [1, SLOT_TILES], I32)
    return x


def sort_buffers(x, sb):
    n = x.experts
    x.hit, x.hit16 = sb("hit", [P, PICKS, n]), sb("hit16", [P, PICKS, n], BF16)
    x.sum_a, x.sum_b, x.slots = (sb(name, [P, PICKS, n]) for name in ("sum_a", "sum_b", "slots"))
    x.count, x.ends = sb("count", [P, n], I32), (sb("end_a", [P, n]), sb("end_b", [P, n]))
    x.first, x.slot = sb("first", [P, n]), sb("slot", [P, PICKS])
    x.passed, x.owner = sb("passed", [1, SORTED_TILES[n], n]), sb("owner", [1, SORTED_TILES[n]])


def slot_buffers(x, sb):
    x.xin, x.sxT = sb("xin", [P, 2, C]), sb("sxT", [CH, 2, 2, P])
    x.sg, x.h, x.ehT = sb("sg", [P, 2, EF]), sb("h", [P, 2, EF]), sb("ehT", [P, 2, EF // P, P])
    x.y = sb("y", [P, 2, C])
    if x.shared:
        x.picked_y = sb("picked_y", [P, PICKS, C])
        x.shared_y = sb("shared_y", [P, TILES, C])


def _chunked(np, w, b=None):
    a = np.zeros((CH + 1, 2, w.shape[1]), np.float32)
    a[0:CH] = w.reshape(2, CH, -1).transpose(1, 0, 2)
    if b is not None:
        a[CH, 1] = b
    return a


def _swapped(w):
    return w.reshape(w.shape[0], -1, 2)[:, :, ::-1].reshape(w.shape)


def _columns(v):
    return v.reshape(2, CH).T


def _padded_keys(np, a):
    out = np.zeros(a.shape[:-1] + (6, 2, 4, HD), np.float32)
    out[..., 1, :] = a.reshape(a.shape[:-1] + (6, 2, HD))
    return out.reshape(a.shape[:-1] + (6 * P,))


def _one_hot_rows(np, positions):
    hot = np.zeros((2, 64, len(positions)), np.float32)
    for j, (r, c) in enumerate(positions):
        hot[:, r, j] = 1
        hot[:, 32 + c, j] = 1
    return hot.reshape(P, -1)


def _shrink(np, n_in, n_out):
    inv = np.float32(n_in) / np.float32(n_out)
    at = (np.arange(n_out, dtype=np.float32) + np.float32(0.5)) * inv - np.float32(0.5)
    x = np.abs(at[None, :] - np.arange(n_in, dtype=np.float32)[:, None]) / max(inv, np.float32(1))
    w = np.maximum(0, 1 - x)
    return (w / w.sum(0, keepdims=True)).astype(np.float32)


def _constants(np):
    c = {}
    c["ident"] = np.eye(P, dtype=np.float32)
    c["mask"] = np.triu(np.full((P, P), -1e30, np.float32), 1)
    c["iota"] = np.tile(np.arange(SLOT_TILES + 1, dtype=np.float32), (P, 1))
    qslot = np.zeros((6, HD, 2, HD), np.float32)
    for h in range(6):
        qslot[h, :, h % 2, :] = QSCALE * np.eye(HD)
    c["qslot"] = qslot.reshape(CH, 2, HD)
    odd = np.zeros((6, HD, 2), np.float32)
    for h in range(6):
        odd[h, :, h % 2] = 1
    c["odd"] = odd.reshape(CH, 2)
    c["gavg"] = np.kron(np.eye(16), np.full((6, 6), 1 / 6)).astype(np.float32)
    window = [(r, k) for r in range(WS) for k in range(WS)]
    c["L0_hot"] = _one_hot_rows(np, window * WINDOWS)
    c["L1_hot"] = _one_hot_rows(np, [(r, k) for r in range(SIDE) for k in range(SIDE)])
    at = np.arange(SIDE)[:, None] - np.arange(SIDE)[None, :] + SIDE - 1
    c["shrink"] = _shrink(np, 63, 2 * SIDE - 1)[:, at.reshape(-1)]
    inv = (1.0 / 10000.0 ** (np.arange(0, HD, 2, dtype=np.float32) / HD)).astype(np.float32)
    ang = np.arange(TOKENS, dtype=np.float32)[:, None] * inv[None, :]
    cos, sin = np.cos(ang), np.sin(ang)
    cos, sin = np.stack([cos, cos], -1).reshape(TOKENS, HD), np.stack([-sin, sin], -1).reshape(TOKENS, HD)
    c["cos"], c["sin"] = (np.tile(a.T, (CH // HD, 1)).astype(np.float32) for a in (cos, sin))
    c["own"] = np.kron(np.eye(CH // HD), np.full((HD, 1), QSCALE)).astype(np.float32)
    return c


def _lay_out(np, i):
    a = _constants(np)
    a["x"] = i["x"].reshape(-1, C)
    for layer, p, names in (("L0", "L0_conv_", ("qkv_w", "qkv_b", "proj_w", "proj_b")),
                            ("L1", "L1_conv_", ("w_qkv", "b_qkv", "w_proj", "b_proj"))):
        w, b, wo, bo = (i[p + n] for n in names)
        a[layer + "_weights"] = _chunked(
            np, np.concatenate([w[:, 0:C], _padded_keys(np, w[:, C:2 * C]), w[:, 2 * C:], wo], 1),
            np.concatenate([b[0:C], _padded_keys(np, b[C:2 * C]), b[2 * C:], bo]))
    a["L0_kpad"] = _padded_keys(np, i["L0_conv_qkv_b"][C:2 * C]).reshape(6, P).T
    row = np.arange(SIDE) % WS
    at = row[:, None] - np.arange(WS)[None, :] + WS - 1
    win = np.zeros((6, HD, 2, SIDE, 16), np.float32)
    for n, rel in enumerate((i["L0_conv_rel_pos_h"], i["L0_conv_rel_pos_w"])):
        win[:, :, n, :, 0:WS] = rel[at].transpose(2, 0, 1)[None]
    a["L0_win"] = win.reshape(CH, 2, SIDE, 16)
    a["L1_rel"] = np.stack([np.tile(i["L1_conv_rel_pos_" + n], (1, 6)) for n in "hw"], 1)
    for n in ("ln1_w", "ln1_b", "ln2_w", "ln2_b"):
        a["L0_" + n] = _columns(i["L0_conv_" + n])
    a["L0_w1"] = _chunked(np, i["L0_conv_fc1_w"], i["L0_conv_fc1_b"])
    a["L0_w2"] = i["L0_conv_fc2_w"].reshape(FF // P, P, C).transpose(1, 0, 2)
    a["L0_b2"] = i["L0_conv_fc2_b"].reshape(1, C)
    a["L2a_weights"] = _chunked(np, np.concatenate([i["L2_attn_w" + n].T for n in "qkvo"], 1),
                                np.concatenate([i["L2_attn_b" + n] for n in "qkvo"]))
    q, k, v = np.split(i["L2_ffn_w_qkv"], [C, C + 3 * HD], 1)
    k = np.repeat(k.reshape(C, 3, HD), HEADS // 3, 1).reshape(C, C)
    v = np.concatenate([v, np.zeros((C, C - v.shape[1]), np.float32)], 1)
    a["L2f_weights"] = _chunked(np, np.concatenate(
        [q, _swapped(q), k, _swapped(k), v, i["L2_ffn_w_out"]], 1))
    a["L2f_norm1"], a["L2f_norm2"] = _columns(i["L2_ffn_norm1_w"]), _columns(i["L2_ffn_norm2_w"])
    a["L2f_wr"] = _chunked(np, i["L2_ffn_w_router"])
    a["L2f_gu"] = i["L2_ffn_w_gate_up"].reshape(16, 2, CH, 2 * EF).transpose(2, 0, 1, 3)
    a["L2f_dn"] = i["L2_ffn_w_down"].reshape(16, EF // P, P, C).transpose(2, 0, 1, 3)
    q, k, v = (i["L3_attn_w_" + n].T for n in "qkv")
    a["L3a_weights"] = _chunked(np, np.concatenate(
        [q, _swapped(q), k, _swapped(k), v, i["L3_attn_w_o"].T], 1))
    a["L3a_norm1"], a["L3a_norm2"] = _columns(i["L3_attn_w_ln1"]), _columns(i["L3_attn_w_ln2"])
    a["L3a_w1"], a["L3a_w3"] = _chunked(np, i["L3_attn_w_ffn_w1"].T), _chunked(np, i["L3_attn_w_ffn_w3"].T)
    a["L3a_w2"] = i["L3_attn_w_ffn_w2"].T.reshape(FF // P, P, C).transpose(1, 0, 2)
    a["L3f_wr"] = _chunked(np, i["L3_ffn_W_router"], i["L3_ffn_expert_bias"])
    gate = np.concatenate([i["L3_ffn_Wg_r"], i["L3_ffn_Wg_s"]], 0)
    up = np.concatenate([i["L3_ffn_Wu_r"], i["L3_ffn_Wu_s"]], 0)
    down = np.concatenate([i["L3_ffn_Wd_r"], i["L3_ffn_Wd_s"]], 0)
    a["L3f_gu"] = np.concatenate([gate, up], 2).reshape(9, 2, CH, 2 * EF).transpose(2, 0, 1, 3)
    a["L3f_dn"] = down.reshape(9, EF // P, P, C).transpose(2, 0, 1, 3)
    return {k: np.ascontiguousarray(v) for k, v in a.items()}


def kernel(**inputs):
    import numpy as np
    import concourse.bacc as bacc
    from concourse.bass_utils import run_bass_kernel_spmd as run

    nc = bacc.Bacc("TRN2", target_bir_lowering=False, num_devices=1)
    arrays = _lay_out(np, {k: np.asarray(v) for k, v in inputs.items()})
    dram = {k: nc.dram_tensor("in_" + k, v.shape, F32, kind="ExternalInput").ap() for k, v in arrays.items()}
    dram["x"] = dram["x"].rearrange("(t p) c -> p t c", p=P)
    out = nc.dram_tensor("out", (IMAGES * TOKENS, C), F32, kind="ExternalOutput").ap()
    build(nc, dram, out.rearrange("(t p) c -> p t c", p=P))
    r = run(nc, [{"in_" + k: v for k, v in arrays.items()}], core_ids=[0])
    return r.results[0]["out"].reshape(IMAGES, SIDE, SIDE, C)
```
